# Optimizing a Trainium2 kernel written in Bass

```python
import numpy as np
import jax
import jax.numpy as jnp

def _softmax(x, axis=-1):
    return jax.nn.softmax(x, axis=axis)

def _gelu(x):
    return jax.nn.gelu(x, approximate=True)

def _silu(x):
    return jax.nn.silu(x)

def _sigmoid(x):
    return jax.nn.sigmoid(x)

def _layernorm(x, axis=-1, eps=1e-05):
    m = jnp.mean(x, axis=axis, keepdims=True)
    v = jnp.var(x, axis=axis, keepdims=True)
    return (x - m) / jnp.sqrt(v + eps)

def _scatter_add(tgt, idx, src, axis=0):
    return tgt.at[idx].add(src)

def _segment_sum(src, seg, n):
    return jax.ops.segment_sum(src, seg, n)
kernel_name = 'mk_early_fusion_d1_tok_img256_r4_7df195'

def setup_inputs(seed: int=0):
    np.random.seed(seed)
    _w = jnp.asarray

    def _rec_inputs():
        import jax
        import jax.numpy as jnp
        _rk = jax.random.key(seed)
        x = -0.000928989 + 1.00043 * jax.random.normal(jax.random.fold_in(_rk, 1), (32, 64, 64, 1), jnp.float32)
        txt = -0.0645857 + 1.41221 * jax.random.normal(jax.random.fold_in(_rk, 2), (32, 128, 64), jnp.float32)
        return (x, txt)
    x, txt = _rec_inputs()

    def _L0_tok_setup():
        import jax, jax.numpy as jnp
        import numpy as np
        L = 4
        M1 = 12
        M2 = 12
        BN_EPS = 1e-05

        def _fourier_layer(v, W1, W2):
            B, C, Sx, Sy = v.shape
            x_ft = jnp.fft.rfft2(v)
            out1 = jnp.einsum('bixy,ioxy->boxy', x_ft[:, :, :M1, :M2], W1)
            out2 = jnp.einsum('bixy,ioxy->boxy', x_ft[:, :, -M1:, :M2], W2)
            out_ft = jnp.zeros((B, C, Sx, Sy // 2 + 1), jnp.complex64)
            out_ft = out_ft.at[:, :, :M1, :M2].set(out1)
            out_ft = out_ft.at[:, :, Sx - M1:, :M2].set(out2)
            return jnp.fft.irfft2(out_ft, s=(Sx, Sy))
        key = jax.random.key(seed)
        ks = jax.random.split(key, 10)
        B, S, d_a, d_v, d_u = (16, 64, 3, 32, 1)
        return {'x': jax.random.normal(ks[0], (B, S, S, 1), jnp.float32), 'p_w': jax.random.normal(ks[1], (d_a, d_v), jnp.float32) * 0.3, 'p_b': jax.random.normal(ks[2], (d_v,), jnp.float32) * 0.1, 'fw1': jax.random.normal(ks[3], (L, d_v, d_v, M1, M2, 2), jnp.float32) * (1.0 / d_v), 'fw2': jax.random.normal(ks[4], (L, d_v, d_v, M1, M2, 2), jnp.float32) * (1.0 / d_v), 'w_w': jax.random.normal(ks[5], (L, d_v, d_v), jnp.float32) * (1.0 / np.sqrt(d_v)), 'w_b': jax.random.normal(ks[6], (L, d_v), jnp.float32) * 0.1, 'bn_g': jnp.ones((L, d_v), jnp.float32), 'bn_b': jnp.zeros((L, d_v), jnp.float32), 'q_w': jax.random.normal(ks[7], (d_v, d_u), jnp.float32) * 0.3, 'q_b': jax.random.normal(ks[8], (d_u,), jnp.float32) * 0.1}
    _L0_tok_all = _L0_tok_setup()
    _L0_tok_in = {k: v for k, v in _L0_tok_all.items() if k in ('p_w', 'p_b', 'fw1', 'fw2', 'w_w', 'w_b', 'bn_g', 'bn_b', 'q_w', 'q_b')}
    del _L0_tok_all

    def _L0_attn_setup():
        import jax, jax.numpy as jnp
        import numpy as np
        U_DECAY = 0.97
        X_DECAY = 0.97
        LN_EPS = 1e-05
        L1_EPS = 1e-12

        def _ln(x):
            m = jnp.mean(x, axis=-1, keepdims=True)
            v = jnp.mean((x - m) ** 2, axis=-1, keepdims=True)
            return (x - m) * jax.lax.rsqrt(v + LN_EPS)
        key = jax.random.key(seed)
        k0, k1, k2, k3 = jax.random.split(key, 4)
        B, T, d, n = (8, 64, 64, 256)
        embeddings = jax.random.normal(k0, (B, T, d), dtype=jnp.float32)
        E = jax.random.normal(k1, (d, n), dtype=jnp.float32) / n ** 0.5
        Dx = jax.random.normal(k2, (n, d), dtype=jnp.float32) / d ** 0.5
        Dy = jax.random.normal(k3, (n, d), dtype=jnp.float32) / d ** 0.5
        return {'embeddings': embeddings, 'E': E, 'Dx': Dx, 'Dy': Dy}
    _L0_attn_all = _L0_attn_setup()
    _L0_attn_in = {k: v for k, v in _L0_attn_all.items() if k in ('E', 'Dx', 'Dy')}
    del _L0_attn_all

    def _L0_ffn_setup():
        import jax, jax.numpy as jnp
        import numpy as np
        B, S, D, F, E, K = (8, 512, 64, 256, 8, 2)
        key = jax.random.key(seed)
        ks = jax.random.split(key, 10)
        s = 0.02
        return {'x': jax.random.normal(ks[0], (B, S, D), dtype=jnp.float32), 'Wr': jax.random.normal(ks[1], (D, E), dtype=jnp.float32) * s, 'W1s': jax.random.normal(ks[2], (D, F), dtype=jnp.float32) * s, 'b1s': jnp.zeros((F,), dtype=jnp.float32), 'W2s': jax.random.normal(ks[3], (F, D), dtype=jnp.float32) * s, 'b2s': jnp.zeros((D,), dtype=jnp.float32), 'W1p': jax.random.normal(ks[4], (E, D, F), dtype=jnp.float32) * s, 'b1p': jnp.zeros((E, F), dtype=jnp.float32), 'W2p': jax.random.normal(ks[5], (E, F, D), dtype=jnp.float32) * s, 'b2p': jnp.zeros((E, D), dtype=jnp.float32)}
    _L0_ffn_all = _L0_ffn_setup()
    _L0_ffn_in = {k: v for k, v in _L0_ffn_all.items() if k in ('Wr', 'W1s', 'b1s', 'W2s', 'b2s', 'W1p', 'b1p', 'W2p', 'b2p')}
    del _L0_ffn_all
    return {'x': x, 'txt': txt, 'L0_tok_p_w': _L0_tok_in['p_w'], 'L0_tok_p_b': _L0_tok_in['p_b'], 'L0_tok_fw1': _L0_tok_in['fw1'], 'L0_tok_fw2': _L0_tok_in['fw2'], 'L0_tok_w_w': _L0_tok_in['w_w'], 'L0_tok_w_b': _L0_tok_in['w_b'], 'L0_tok_bn_g': _L0_tok_in['bn_g'], 'L0_tok_bn_b': _L0_tok_in['bn_b'], 'L0_tok_q_w': _L0_tok_in['q_w'], 'L0_tok_q_b': _L0_tok_in['q_b'], 'L0_attn_E': _L0_attn_in['E'], 'L0_attn_Dx': _L0_attn_in['Dx'], 'L0_attn_Dy': _L0_attn_in['Dy'], 'L0_ffn_Wr': _L0_ffn_in['Wr'], 'L0_ffn_W1s': _L0_ffn_in['W1s'], 'L0_ffn_b1s': _L0_ffn_in['b1s'], 'L0_ffn_W2s': _L0_ffn_in['W2s'], 'L0_ffn_b2s': _L0_ffn_in['b2s'], 'L0_ffn_W1p': _L0_ffn_in['W1p'], 'L0_ffn_b1p': _L0_ffn_in['b1p'], 'L0_ffn_W2p': _L0_ffn_in['W2p'], 'L0_ffn_b2p': _L0_ffn_in['b2p']}

def reference(x, txt, L0_tok_p_w, L0_tok_p_b, L0_tok_fw1, L0_tok_fw2, L0_tok_w_w, L0_tok_w_b, L0_tok_bn_g, L0_tok_bn_b, L0_tok_q_w, L0_tok_q_b, L0_attn_E, L0_attn_Dx, L0_attn_Dy, L0_ffn_Wr, L0_ffn_W1s, L0_ffn_b1s, L0_ffn_W2s, L0_ffn_b2s, L0_ffn_W1p, L0_ffn_b1p, L0_ffn_W2p, L0_ffn_b2p):
    import jax
    import jax.numpy as jnp

    def _L0_tok_ref(x, p_w, p_b, fw1, fw2, w_w, w_b, bn_g, bn_b, q_w, q_b):
        import jax, jax.numpy as jnp
        import numpy as np
        L = 4
        M1 = 12
        M2 = 12
        BN_EPS = 1e-05

        def _fourier_layer(v, W1, W2):
            B, C, Sx, Sy = v.shape
            x_ft = jnp.fft.rfft2(v)
            out1 = jnp.einsum('bixy,ioxy->boxy', x_ft[:, :, :M1, :M2], W1)
            out2 = jnp.einsum('bixy,ioxy->boxy', x_ft[:, :, -M1:, :M2], W2)
            out_ft = jnp.zeros((B, C, Sx, Sy // 2 + 1), jnp.complex64)
            out_ft = out_ft.at[:, :, :M1, :M2].set(out1)
            out_ft = out_ft.at[:, :, Sx - M1:, :M2].set(out2)
            return jnp.fft.irfft2(out_ft, s=(Sx, Sy))
        B, Sx, Sy, _ = x.shape
        gx = jnp.broadcast_to(jnp.linspace(0.0, 1.0, Sx, dtype=jnp.float32)[None, :, None, None], (B, Sx, Sy, 1))
        gy = jnp.broadcast_to(jnp.linspace(0.0, 1.0, Sy, dtype=jnp.float32)[None, None, :, None], (B, Sx, Sy, 1))
        h = jnp.concatenate([x, gx, gy], axis=-1)
        v = h @ p_w + p_b
        v = jnp.transpose(v, (0, 3, 1, 2))
        for i in range(L):
            W1 = fw1[i, ..., 0] + 1j * fw1[i, ..., 1]
            W2 = fw2[i, ..., 0] + 1j * fw2[i, ..., 1]
            x1 = _fourier_layer(v, W1, W2)
            x2 = jnp.einsum('bcxy,cd->bdxy', v, w_w[i]) + w_b[i][None, :, None, None]
            v = x1 + x2
            mean = jnp.mean(v, axis=(0, 2, 3), keepdims=True)
            var = jnp.var(v, axis=(0, 2, 3), keepdims=True)
            v = (v - mean) * jax.lax.rsqrt(var + BN_EPS)
            v = v * bn_g[i][None, :, None, None] + bn_b[i][None, :, None, None]
            if i < L - 1:
                v = jax.nn.relu(v)
        out = jnp.einsum('bcxy,cu->bxyu', v, q_w) + q_b
        return jnp.squeeze(out)

    def _L0_attn_ref(embeddings, E, Dx, Dy):
        import jax, jax.numpy as jnp
        import numpy as np
        U_DECAY = 0.97
        X_DECAY = 0.97
        LN_EPS = 1e-05
        L1_EPS = 1e-12

        def _ln(x):
            m = jnp.mean(x, axis=-1, keepdims=True)
            v = jnp.mean((x - m) ** 2, axis=-1, keepdims=True)
            return (x - m) * jax.lax.rsqrt(v + LN_EPS)
        B, T, d = embeddings.shape
        n = E.shape[1]

        def step(carry, v_prev):
            x_state, rho = carry
            x_update = jax.nn.relu(v_prev @ Dx.T)
            x_t = X_DECAY * x_state + x_update
            x_t = x_t / jnp.maximum(jnp.sum(jnp.abs(x_t), axis=-1, keepdims=True), L1_EPS)
            a_star = jnp.einsum('bdn,bn->bd', rho, x_t)
            y_core = _ln(a_star) @ Dy.T
            y_t = jax.nn.relu(y_core) * jax.nn.relu(x_t)
            v_star = _ln(y_t @ E.T)
            rho_t = U_DECAY * rho + _ln(v_prev)[:, :, None] * x_t[:, None, :]
            return ((x_t, rho_t), v_star)
        x0 = jnp.zeros((B, n), dtype=embeddings.dtype)
        rho0 = jnp.zeros((B, d, n), dtype=embeddings.dtype)
        _, vs = jax.lax.scan(step, (x0, rho0), jnp.swapaxes(embeddings, 0, 1))
        return jnp.swapaxes(vs, 0, 1)

    def _L0_ffn_ref(x, Wr, W1s, b1s, W2s, b2s, W1p, b1p, W2p, b2p):
        import jax, jax.numpy as jnp
        import numpy as np
        B, S, D, F, E, K = (8, 512, 64, 256, 8, 2)
        gelu = lambda t: jax.nn.gelu(t, approximate=False)
        shared = gelu(x @ W1s + b1s) @ W2s + b2s
        rw = jax.nn.softmax(x @ Wr, axis=-1)
        topw, topi = jax.lax.top_k(rw, K)
        topw = topw / jnp.sum(topw, axis=-1, keepdims=True)
        mask = jnp.sum(jax.nn.one_hot(topi, E, dtype=topw.dtype) * topw[..., None], axis=-2)
        h = gelu(jnp.einsum('bsd,edf->bsef', x, W1p) + b1p)
        priv = jnp.einsum('bsef,efd->bsed', h, W2p) + b2p
        routed = jnp.einsum('bsed,bse->bsd', priv, mask)
        return shared + routed
    h = _L0_tok_ref(x, L0_tok_p_w, L0_tok_p_b, L0_tok_fw1, L0_tok_fw2, L0_tok_w_w, L0_tok_w_b, L0_tok_bn_g, L0_tok_bn_b, L0_tok_q_w, L0_tok_q_b)
    h = jnp.concatenate([h, txt], axis=1)
    h = h + _L0_attn_ref(_layernorm(h, axis=-1), L0_attn_E, L0_attn_Dx, L0_attn_Dy)
    h = h + _L0_ffn_ref(_layernorm(h, axis=-1), L0_ffn_Wr, L0_ffn_W1s, L0_ffn_b1s, L0_ffn_W2s, L0_ffn_b2s, L0_ffn_W1p, L0_ffn_b1p, L0_ffn_W2p, L0_ffn_b2p)
    return h

_drawn_inputs = setup_inputs


def setup_inputs(seed=0):
    import zlib

    import numpy as np

    out = dict(_drawn_inputs(seed))
    spreads = {'L0_tok_bn_g': (1.0, 0.2),
     'L0_tok_bn_b': (0.0, 0.1),
     'L0_ffn_b1s': (0.0, 0.8),
     'L0_ffn_b2s': (0.0, 0.1),
     'L0_ffn_b1p': (0.0, 0.8),
     'L0_ffn_b2p': (0.0, 0.1)}
    factors = {'L0_tok_p_b': 8.0,
     'L0_tok_w_b': 8.0,
     'L0_ffn_W1s': 3.554,
     'L0_ffn_W2s': 2.926,
     'L0_ffn_W1p': 5.064,
     'L0_ffn_W2p': 4.298}
    for name, (base, spread) in spreads.items():
        noise = np.random.default_rng([zlib.crc32(name.encode()), seed]).standard_normal(out[name].shape)
        drawn = base * np.exp(spread * noise) if base else spread * noise
        out[name] = jnp.asarray(drawn.astype(out[name].dtype))
    for name, factor in factors.items():
        out[name] = (out[name] * factor).astype(out[name].dtype)
    return out
```

```python
from contextlib import ExitStack

import concourse.bass as bass
from concourse import mybir

ACT = mybir.ActivationFunctionType
ALU = mybir.AluOpType
AX = mybir.AxisListType
F32 = mybir.dt.float32

B, SX, SY = 32, 64, 64
C, L, M = 32, 4, 12
Q = 4
G = B // Q
NPOS = SX * SY
KR = 2 * M
TXT, D = 128, 64
T = SX + TXT
N = 256
NJ = B // 2
EPS = 1e-5
DECAY, TINY = 0.97, 1e-12
E, F = 8, 256
NT = 3 * NJ
NW = B * T
CH = 4


def spectral_tables():
    import numpy as np

    y, ky = np.arange(SY), np.arange(M)
    kx = np.concatenate([np.arange(M), np.arange(SX - M, SX)])
    x = np.arange(SX)
    ay = 2 * np.pi * np.outer(y, ky) / SY
    ax = 2 * np.pi * np.outer(x, kx) / SX
    fy = np.zeros((2, SY, 2, M, 2))
    for i in range(2):
        fy[i, :, i, :, 0] = np.cos(ay)
        fy[i, :, i, :, 1] = -np.sin(ay)
    fx = np.zeros((2, SX, 2, 2, M))
    c, s = np.cos(ax).reshape(SX, 2, M), np.sin(ax).reshape(SX, 2, M)
    fx[0, :, :, 0], fx[0, :, :, 1] = c, -s
    fx[1, :, :, 0], fx[1, :, :, 1] = s, c
    ix = np.zeros((2, 2, 32, 2, SX))
    c, s = np.cos(ax).T.reshape(2, M, SX), np.sin(ax).T.reshape(2, M, SX)
    ix[:, :, 0:KR:2, 0], ix[:, :, 0:KR:2, 1] = c, s
    ix[:, :, 1:KR:2, 0], ix[:, :, 1:KR:2, 1] = -s, c
    w = np.where(ky == 0, 1.0, 2.0)[:, None] / (SX * SY)
    iy = np.zeros((4, 32, 4, SY))
    for i in range(4):
        iy[i, 0:KR:2, i] = w * np.cos(ay).T
        iy[i, 1:KR:2, i] = -w * np.sin(ay).T
    f = lambda a, n: a.reshape(128, n).astype(np.float32)
    return f(fy, 48), f(fx, 48), f(ix, 128), f(iy, 256)


def attention_tables():
    import numpy as np

    s, t = np.arange(T)[:, None], np.arange(T)[None, :]
    decay = np.where(s < t, DECAY ** np.maximum(t - 1 - s, 0), 0.0).astype(np.float32)
    rank = np.broadcast_to(np.arange(E, 0, -1, dtype=np.float32), (128, E))
    return np.concatenate([np.concatenate([decay[:SX], decay[:SX]]), decay[SX:, SX:], rank], axis=1)


def build(nc, x, grid, pin, txt, tables, fw, lp, qblk, qb, att, dxy, et, w1, w2, wr, b1, b2, rdram, out):
    ctx = ExitStack()
    with ctx:
        def sb(name, shape):
            return ctx.enter_context(nc.sbuf_tensor(name, shape, F32))

        def sem(name):
            return ctx.enter_context(nc.semaphore(name))

        v = sb("v", [128, G * NPOS])
        phase = sb("phase", [128, 6656])
        R = phase[:, 0:4096]
        F1o = phase[:, 4096:5632].rearrange("p (k x) -> p k x", x=SX)
        T2s = phase[:, 5632:6656].rearrange("p (s n) -> p s n", s=2)
        H = phase[:, 0:6144].rearrange("p (k o b) -> p k o b", k=6, o=C)
        S = sb("S", [128, 2, 512])
        Xr = sb("Xr", [128, B * 144])
        X = Xr[:, :].rearrange("p (b k m) -> p b k m", b=B, k=M)
        I1o = Xr[:, 0:4096].rearrange("p (s x k) -> p s x k", s=2, x=SX)
        hbuf = Xr[:, 0:3 * NJ * D].rearrange("p (j t d) -> p j t d", j=NJ, t=3)
        Yr = sb("Yr", [128, 2048])
        F2o = Yr[:, 0:1152].rearrange("p (s h k m) -> p s h k m", s=2, h=4, k=M)
        Ys = Yr[:, :].rearrange("p (s o k) -> p s o k", s=2, o=C)
        Hg = Yr[:, 0:1536].rearrange("p (s k n) -> p s k n", s=2, k=6)
        XB = sb("XB", [128, 2, M, 64])
        W = sb("W", [128, 4, M, 64])
        fy, fx, ix, iy = sb("fy", [128, 48]), sb("fx", [128, 48]), sb("ix", [128, 128]), sb("iy", [128, 256])
        ident, avg = sb("ident", [128, 128]), sb("avg", [128, 128])
        lps = sb("lps", [128, 131])
        st = sb("st", [128, G * 8 * 6])
        sm = sb("sm", [128, 24])
        qs = sb("qs", [128, 8])
        agg, mv, dif, sq, var, sd, r0, r2, t1, rs, mw, ms, scale, shift, qbias = (
            sm[:, 0:2], sm[:, 2:4], sm[:, 4:5], sm[:, 5:6], sm[:, 6:7], sm[:, 7:8], sm[:, 8:9], sm[:, 9:10],
            sm[:, 10:11], sm[:, 11:12], sm[:, 12:13], sm[:, 13:14], sm[:, 14:15], sm[:, 15:16], sm[:, 16:17])
        ones = sm[:, 18:19]
        wblk, wb, gamma, beta = lps[:, 0:128], lps[:, 128:129], lps[:, 129:130], lps[:, 130:131]

        u_row = v[0:1, 0:NW]
        e2T = v[0:D, 0:NW]
        xa = v[:, NW:3 * NW].rearrange("p (h n) -> p h n", h=2)
        rB, cB = v[:, 3 * NW:4 * NW], v[:, 4 * NW:5 * NW]
        spare = v[:, 5 * NW:]
        es = spare[:, 0:384].rearrange("p (s n) -> p s n", s=2)
        eTs = spare[0:D, 384:1152].rearrange("p (s n) -> p s n", s=2)
        Vs = spare[:, 1152:1536].rearrange("p (s n) -> p s n", s=2)
        Ai = spare[:, 1536:1920].rearrange("p (s n) -> p s n", s=2)
        At = S[:, 0, :].rearrange("p (s n) -> p s n", s=2)
        xs = Xr[:, 3072:4608].rearrange("p (s h n) -> p s h n", s=2, h=2)
        ys = cB[:, 0:1536].rearrange("p (s h n) -> p s h n", s=2, h=2)
        tok = lambda a: a.rearrange("p (k d) -> p k d", d=D)
        h_all = tok(Xr[:, 0:3072])
        eb, vb, tmp, tmp2 = tok(phase[:, 0:3072]), tok(phase[:, 3072:6144]), tok(W[:, :, :, :].rearrange("p a b c -> p (a b c)")), tok(rB[:, 0:3072])
        dx, dy = S[0:D, 1, 0:N], S[0:D, 1, N:2 * N]
        XBr = XB[:, :, :, :].rearrange("p a b c -> p (a b c)")
        W2 = XBr[:, 0:1152].rearrange("p (f e d) -> p f e d", f=2, e=E + 1)
        ET = XBr[:, 1152:1280].rearrange("p (h d) -> p h d", h=2)
        Wr = XBr[0:D, 1280:1288]
        B1 = XBr[:, 1288:1306]
        B2 = Yr[:, 0:576]
        Di, Dt, rank = Yr[:, 576:768], Yr[:, 768:896], XBr[:, 1306:1314]
        U, k1, k2, z, rsum, csum = (Yr[0:B, 896 + i * T:896 + (i + 1) * T] for i in range(6))
        W1 = W[0:D, :, :, :].rearrange("p a b c -> p (a b c)")[:, 0:2304].rearrange("p (e n) -> p e n", e=E + 1)
        lns = Xr[:, 3840:4272]
        lg, lz, ex, rw, eq, cd, oh1, rw2, oh2, mask = (
            cB[:, 2048 + 384 * i:2432 + 384 * i].rearrange("p (k e) -> p k e", e=E) for i in range(10))
        rr = rB[:, 4608:5184].rearrange("p (i k) -> p i k", k=NT)
        e2s = rB[:, 3072:3584].rearrange("p (s n) -> p s n", s=2)
        e2Ts = rB[0:D, 3584:4608].rearrange("p (s n) -> p s n", s=2)
        hT = rB[:, 0:3072].rearrange("p (s n) -> p s n", s=6)
        tb = rB[:, 3648:5696].rearrange("p (t e d) -> p t e d", t=CH, e=E)
        rt = Xr[:, 3072:3328].rearrange("p (t d) -> p t d", d=D)
        s1 = Xr[:, 3328:3584].rearrange("p (t d) -> p t d", d=D)
        s2 = Xr[:, 3584:3840].rearrange("p (t d) -> p t d", d=D)

        ps = ctx.enter_context(nc.psum_tensor("ps", [128, 8, 512], F32))
        TP, FP, T2P, F2P = (0, 1), (2, 3), (4, 5), (6, 7)
        IP, ZP, OP = (0, 1), (2, 3), (4, 5, 6, 7)

        consts, primed, zeroed, carried = (sem(n) for n in ("consts", "primed", "zeroed", "carried"))
        v0_in, v0_mm, v0_done = sem("v0_in"), sem("v0_mm"), sem("v0_done")
        relu_done, t1_done, s_done, f1_done, f1e_done = (sem(n) for n in (
            "relu_done", "t1_done", "s_done", "f1_done", "f1e_done"))
        t2_done, t2e_done, f2_done, f2e_done = (sem(n) for n in ("t2_done", "t2e_done", "f2_done", "f2e_done"))
        v_stored = [sem(f"v_stored{r}") for r in range(4)]
        x_stored = [sem(f"x_stored{s}") for s in range(2)]
        w_loaded = [sem(f"w_loaded{s}") for s in range(4)]
        w_neg, xb0_done, xb1_done, mix_done, y_done, yt_done = (sem(n) for n in (
            "w_neg", "xb0_done", "xb1_done", "mix_done", "y_done", "yt_done"))
        hg_done, i1_done, i1e_done, t4_done, ze_done = (sem(n) for n in (
            "hg_done", "i1_done", "i1e_done", "t4_done", "ze_done"))
        fin_done, oe_done, bs_done = sem("fin_done"), sem("oe_done"), sem("bs_done")
        lp_loaded, dch, sm_done, sq_done = sem("lp_loaded"), sem("dch"), sem("sm_done"), sem("sq_done")
        qs_done, qt_done, qb_done, h_mm, h_done = (sem(n) for n in ("qs_done", "qt_done", "qb_done", "h_mm", "h_done"))
        h_stored = [sem(f"h_stored{s}") for s in range(2)]
        txt_in, out_st = sem("txt_in"), sem("out_st")
        h_in, out_st2 = sem("h_in"), sem("out_st2")
        es_done, tr_done, eT_done, u_done, wv_done, us_done, ur_done = (sem(n) for n in (
            "es_done", "tr_done", "eT_done", "u_done", "wv_done", "us_done", "ur_done"))
        xs_done, vs_done, sc_done, am_done, a_done, at_done = (sem(n) for n in (
            "xs_done", "vs_done", "sc_done", "am_done", "a_done", "at_done"))
        as_done, tr2_done, aT_done, yc_done, ym_done, vo_done, ve_done = (sem(n) for n in (
            "as_done", "tr2_done", "aT_done", "yc_done", "ym_done", "vo_done", "ve_done"))
        e2s_done, tr3_done, e2T_done, rt_done, lg_done, e2c_done = (sem(n) for n in (
            "e2s_done", "tr3_done", "e2T_done", "rt_done", "lg_done", "e2c_done"))
        hm_done, gelu_done, w2_done, p_done, m_done, r_done, sh_done, f_done = (sem(n) for n in (
            "hm_done", "gelu_done", "w2_done", "p_done", "m_done", "r_done", "sh_done", "f_done"))
        ones_done, s2_done = sem("ones_done"), sem("s2_done")
        late, w1_in, twoin = sem("late"), sem("w1_in"), sem("twoin")
        tok_ready, steps, sqrt_done, exp_done = sem("tok_ready"), sem("steps"), sem("sqrt_done"), sem("exp_done")
        u_moved, rc_out, r_in, c_in = sem("u_moved"), sem("rc_out"), sem("r_in"), sem("c_in")
        STEPS = 13
        STEP_E = 12
        STEP_RC = STEP_E + 10
        STEP_V = STEP_RC + 12
        STEP_X = STEP_V + 4
        STEP_A = STEP_X + 12
        STEP_VS = STEP_A + 12
        STEP_H = STEP_VS + 1 + 12
        STEP_L = STEP_H + 2
        STEP_M = STEP_L + 19
        NCONST = 10

        block = ctx.enter_context(nc.Block())

        def groups(eng, body):
            settle(eng)
            with eng.Fori(0, G // 2) as i:
                for s in range(2):
                    body(2 * i + s, s, i)

        def settle(eng):
            eng.sem_inc(carried, 1)

        def layers(eng, first, step):
            first()
            settle(eng)
            with eng.Fori(0, L - 1) as l:
                step(l, False)
            step(L - 1, True)

        @block.sync
        def _(sp):
            sp.dma_start(fy[:, :], tables[0]).then_inc(consts, 16)
            sp.dma_start(fx[:, :], tables[1]).then_inc(consts, 16)
            sp.dma_start(ix[:, :], tables[2]).then_inc(consts, 16)
            sp.dma_start(iy[:, :], tables[3]).then_inc(consts, 16)
            sp.dma_start(ident[:, :], tables[4]).then_inc(consts, 16)
            sp.dma_start(avg[:, :], tables[5]).then_inc(consts, 16)
            sp.dma_start(qs[:, 0:4], qblk).then_inc(consts, 16)
            sp.dma_start(qbias[0:4, :], qb).then_inc(consts, 16)
            sp.dma_start(v[0:Q, :].rearrange("q (g n) -> q g n", g=G), x.rearrange("(g q) n -> q g n", q=Q)).then_inc(v0_in, 16)
            sp.dma_start(v[Q:Q + 3, :].rearrange("q (g n) -> q g n", g=G), grid).then_inc(v0_in, 16)
            sp.dma_start(lps[0:Q + 3, 0:128], pin).then_inc(consts, 16)
            sp.wait_ge(primed, 4)

            def weights(l, kys):
                for ky in kys:
                    sp.wait_ge(mix_done, (l * 6 + ky // 2) * 2 + 2)
                    sp.dma_start(W[:, ky % 4], fw[ky, :, bass.ds(l, 1)].rearrange("p l m n -> p (l m) n")).then_inc(w_loaded[ky % 4], 16)

            def phase_a(a):
                weights(a, range(4))

                def group(g, s, i):
                    for r in range(4):
                        sp.wait_ge(relu_done, (a * G + g) * 4 + r + 1)
                        sp.dma_start(v[:, bass.ds(g * NPOS + r * 1024, 1024)],
                                     R[:, r * 1024:(r + 1) * 1024]).then_inc(v_stored[r], 16)
                    sp.wait_ge(f2e_done, 2 + (a * G + g) * 2 + 2)
                    for q in range(Q):
                        for h in range(4):
                            sp.dma_start(X[32 * h:32 * h + 32, bass.ds(g * Q + q, 1)].rearrange("p b k m -> p (b k m)"),
                                         F2o[32 * q:32 * q + 32, s, h].rearrange("p k m -> p (k m)")).then_inc(x_stored[s], 16)
                groups(sp, group)
                weights(a, range(4, M))

            def params(l):
                sp.dma_start(lps[:, :], lp[bass.ds(l, 1)].rearrange("l p n -> (l p) n")).then_inc(lp_loaded, 16)

            def step(l, last):
                if not last:
                    sp.wait_ge(dch, (l + 1) * STEPS)
                    params(l + 1)
                    phase_a(l + 1)
            sp.wait_ge(v0_mm, 64 + 2)
            params(0)
            layers(sp, lambda: phase_a(0), step)

            def tokens(g, s, i):
                for hf in range(2):
                    sp.wait_ge(h_done, 4 + g * 8 + hf * 4 + 4)
                    for q in range(Q):
                        p0 = (q % 2) * 64 + 32 * hf
                        sp.dma_start(hbuf[p0:p0 + 32, bass.ds(2 * g + q // 2, 1), 0].rearrange("p j d -> p (j d)"),
                                     phase[q:q + 1, hf * 2048:(hf + 1) * 2048].rearrange("p (x y) -> p x y", y=D)
                                     ).then_inc(h_stored[hf], 16)
            sp.wait_ge(fin_done, 4 + L * 64)
            for two in range(2):
                sp.dma_start(hbuf[:, :, 1 + two], txt.rearrange("(j b) t d -> b t j d", b=2)[two]).then_inc(txt_in, 16)
            groups(sp, tokens)
            for dst, src in ((dx, dxy[:, 0:N]), (dy, dxy[:, N:2 * N]), (Di, att[:, 0:T]), (Dt, att[:, T:T + TXT]),
                             (rank, att[:, T + TXT:]), (ET, et), (Wr, wr), (B1, b1), (W2, w2), (B2, b2)):
                sp.dma_start(dst, src).then_inc(late, 16)
            sp.wait_ge(ur_done, 2 + NJ)
            sp.dma_start(U, u_row).then_inc(u_moved, 16)
            sp.wait_ge(steps, STEP_RC)
            sp.dma_start(rdram[0].rearrange("(b t) -> b t", b=B), rsum).then_inc(rc_out, 16)
            sp.dma_start(rdram[1].rearrange("(b t) -> b t", b=B), csum).then_inc(rc_out, 16)
            sp.wait_ge(rc_out, 32)
            sp.dma_start(cB, rdram[1:2, :].partition_broadcast(128)).then_inc(c_in, 16)
            sp.dma_start(rB, rdram[0:1, :].partition_broadcast(128)).then_inc(r_in, 16)
            sp.wait_ge(steps, STEP_V)
            sp.dma_start(W1, w1).then_inc(w1_in, 16)
            sp.wait_ge(f_done, NT // CH)
            o = out.rearrange("(j b) t d -> b t j d", b=2)
            for two in range(2):
                sp.dma_start(o[two, 0:SX], hbuf[64 * two:64 * two + 64, :, 0]).then_inc(out_st, 16)
                sp.dma_start(o[two, SX:T], hbuf[:, :, 1 + two]).then_inc(out_st, 16)
            sp.wait_ge(out_st, 64)

        @block.gpsimd
        def _(pool):
            pool.memset(XB[:, :, :, :], 0.0).then_inc(zeroed, 1)
            pool.memset(Yr[:, :], 0.0).then_inc(zeroed, 1)
            for s in range(2):
                pool.sem_inc(x_stored[s], 256)
                pool.sem_inc(h_stored[s], 16)
            for r in range(4):
                pool.sem_inc(v_stored[r], 16)
            pool.sem_inc(primed, 1)
            pool.wait_ge(primed, 4)

            def mix(l):
                for s in range(2):
                    pool.wait_ge(x_stored[s], 256 * (l * 4 + 4) + 256)
                for ky in range(M):
                    pool.wait_ge(w_loaded[ky % 4], (l * 3 + ky // 4 + 1) * 16)
                    settle(pool)
                    for h in range(2):
                        settle(pool)
                        wi = W[64 * h + 32:64 * h + 64, ky % 4, :, 0:32]
                        pool.tensor_scalar(wi, wi, -1.0, None, ALU.mult).then_inc(w_neg, 1)
                        pool.wait_ge(w_neg, (l * M + ky) * 2 + h + 1)
                    pool.wait_ge(mix_done, (l * 6 + ky // 2) * 2 + 4)
                    settle(pool)
                    pool.tensor_copy(XB[0:64, ky % 2, :, 0:32], X[0:64, :, ky].rearrange("p b m -> p m b")).then_inc(xb0_done, 1)
                    pool.wait_ge(xb0_done, l * M + ky + 1)

            def phase_b(l):
                pool.wait_ge(yt_done, 2 + (l + 1) * 6)

                def group(g, s, i):
                    pool.wait_ge(i1_done, (l * G + g) * 4 + 4)
                    settle(pool)
                    pool.tensor_copy(Hg[:, s].rearrange("p k (q o) -> p k q o", q=Q),
                                     H[:, :, :, bass.ds(g * Q, Q)].rearrange("p k o q -> p k q o")).then_inc(hg_done, 1)
                    pool.wait_ge(hg_done, l * G + g + 1)
                groups(pool, group)

            def step(l, last):
                mix(l)
                phase_b(l)
            pool.wait_ge(zeroed, 2)
            layers(pool, lambda: None, step)
            pool.wait_ge(steps, STEP_V)
            with pool.Fori(0, NJ // 2) as i:
                for s in range(2):
                    j = 2 * i + s
                    pool.wait_ge(a_done, j + 1)
                    settle(pool)
                    pool.tensor_copy(Vs[:, s], phase[:, bass.ds(3072 + j * 192, 192)]).then_inc(vs_done, 1)
                    pool.wait_ge(vs_done, j + 1)

        @block.tensor
        def _(pe):
            pe.sem_inc(t1_done, 8)
            pe.sem_inc(f1_done, 2)
            pe.sem_inc(t2_done, 3)
            pe.sem_inc(f2_done, 2)
            pe.sem_inc(mix_done, 4)
            pe.sem_inc(i1_done, 8)
            pe.sem_inc(t4_done, 8)
            pe.sem_inc(fin_done, 4)
            pe.sem_inc(v0_mm, 2)
            for sm_, n in ((tr_done, 2), (u_done, 4), (sc_done, 2), (a_done, 2), (tr2_done, 2), (yc_done, 4),
                           (vo_done, 2), (tr3_done, 2), (rt_done, 2), (w2_done, 3)):
                pe.sem_inc(sm_, n)
            pe.sem_inc(primed, 1)
            pe.wait_ge(primed, 4)
            pe.wait_ge(consts, 16 * (NCONST - 1))
            pe.wait_ge(v0_in, 32)
            with pe.Fori(0, G * 4) as i:
                for s in range(2):
                    pe.wait_ge(v0_done, 2 * i + s + 1)
                    pe.matmul(ps[:, s, :], lps[0:Q + 3, 0:128], v[0:Q + 3, bass.ds((2 * i + s) * 512, 512)],
                              start=True, stop=True).then_inc(v0_mm, 1)

            def phase_a(a):
                def group(g, s, i):
                    ga = a * G + g

                    def turn(c):
                        if c % 2 == 0:
                            pe.wait_ge(relu_done, ga * 4 + c // 2 + 1)
                        pe.wait_ge(s_done, ga * 8 + c + 1)
                        for j in range(4):
                            mm = pe.transpose(ps[:, TP[c % 2], 128 * j:128 * j + 128],
                                              R[:, 512 * c + 128 * j:512 * c + 128 * j + 128], ident[:, :])
                        mm.then_inc(t1_done, 1)

                    def ydft(c):
                        pe.wait_ge(s_done, ga * 8 + c + 3)
                        if c % 2 == 0:
                            pe.wait_ge(f1e_done, ga * 4 + c // 2 + 1)
                        for j in range(4):
                            o = (c % 2) * 192 + 48 * j
                            mm = pe.matmul(ps[:, FP[(c // 2) % 2], o:o + 48], S[:, c % 2, 128 * j:128 * j + 128],
                                           fy[:, :], start=True, stop=True)
                        mm.then_inc(f1_done, 1)
                    turn(0)
                    for c in range(1, 8):
                        turn(c)
                        ydft(c - 1)
                    ydft(7)

                    def turn2(k):
                        if k == 0:
                            pe.wait_ge(f1e_done, 2 + ga * 4 + 4)
                        pe.wait_ge(t2e_done, ga * 3 + k + 1)
                        for j in range(4):
                            ky = 4 * k + j
                            mm = pe.transpose(ps[:, T2P[(s * 3 + k) % 2], 128 * j:128 * j + 128],
                                              F1o[:, 2 * ky:2 * ky + 2].rearrange("p k x -> p (k x)"), ident[:, :])
                        mm.then_inc(t2_done, 1)

                    def xdft(k):
                        pe.wait_ge(t2e_done, 2 + ga * 3 + k + 1)
                        for j in range(4):
                            ky = 4 * k + j
                            if ky % 6 == 0:
                                pe.wait_ge(f2e_done, ga * 2 + ky // 6 + 1)
                            mm = pe.matmul(ps[:, F2P[ky // 6], 48 * (ky % 6):48 * (ky % 6) + 48],
                                           T2s[:, (s * 3 + k) % 2, 128 * j:128 * j + 128], fx[:, :], start=True, stop=True)
                        mm.then_inc(f2_done, 1)
                    turn2(0)
                    turn2(1)
                    xdft(0)
                    turn2(2)
                    xdft(1)
                    xdft(2)
                groups(pe, group)

            def mix(l):
                for p in range(6):
                    pg = l * 6 + p
                    pe.wait_ge(w_neg, (l * M + 2 * p + 2) * 2)
                    pe.wait_ge(xb0_done, l * M + 2 * p + 2)
                    pe.wait_ge(xb1_done, l * M + 2 * p + 2)
                    for h in range(2):
                        pe.wait_ge(y_done, pg * 2 + h + 1)
                        for m in range(6):
                            kx = 6 * h + m
                            for par in range(2):
                                mm = pe.matmul(ps[64 * par:64 * par + 64, (p % 2) * 2 + h, 64 * m:64 * m + 64],
                                               XB[:, par, kx], W[:, (2 * p + par) % 4, kx],
                                               start=True, stop=True)
                        mm.then_inc(mix_done, 1)

            def phase_b(l):
                for r in range(4):
                    pe.wait_ge(v_stored[r], 16 * G * (l + 1) + 16)
                pe.wait_ge(lp_loaded, 16 * (l + 1))

                def group(g, s, i):
                    gb = l * G + g
                    pe.wait_ge(hg_done, gb + 1)
                    for u in range(4):
                        par = u % 2
                        pe.wait_ge(i1e_done, gb * 4 + u + 1)
                        for j in range(3):
                            kh = 3 * (u // 2) + j
                            mm = pe.matmul(ps[:, IP[par], 128 * j:128 * j + 128],
                                           Hg[64 * par:64 * par + 64, s, kh], ix[64 * par:64 * par + 64, :],
                                           start=True, stop=True)
                        mm.then_inc(i1_done, 1)

                    def turn(z):
                        if z == 0:
                            pe.wait_ge(i1e_done, 2 + gb * 4 + 4)
                        pe.wait_ge(ze_done, gb * 4 + z + 1)
                        for j in range(4):
                            x0 = 16 * z + 4 * j
                            mm = pe.transpose(ps[:, ZP[z % 2], 128 * j:128 * j + 128],
                                              I1o[:, s, x0:x0 + 4].rearrange("p x k -> p (x k)"), ident[:, :])
                        mm.then_inc(t4_done, 1)

                    def add(c):
                        cf = gb * 8 + c
                        pe.wait_ge(ze_done, 2 + gb * 4 + c // 2 + 1)
                        pe.wait_ge(oe_done, cf + 1)
                        pe.matmul(ps[:, OP[c % 4], :], wblk, v[:, bass.ds(g * NPOS + c * 512, 512)],
                                  start=True, stop=False, skip_group_check=True)
                        for j in range(2):
                            z0 = (c % 2) * 256 + 128 * j
                            mm = pe.matmul(ps[:, OP[c % 4], 256 * j:256 * j + 256], S[:, (c // 2) % 2, z0:z0 + 128],
                                           iy[:, :], start=False, stop=True, skip_group_check=True)
                        mm.then_inc(fin_done, 1)
                    turn(0)
                    turn(1)
                    add(0)
                    add(1)
                    turn(2)
                    add(2)
                    add(3)
                    turn(3)
                    for c in range(4, 8):
                        add(c)
                groups(pe, group)
                pe.wait_ge(dch, l * STEPS + 1)
                pe.matmul(ps[:, 0, 0:2], avg[:, :], agg, start=True, stop=True).then_inc(sm_done, 1)
                pe.wait_ge(dch, l * STEPS + 4)
                pe.matmul(ps[:, 1, 0:1], avg[:, :], sq, start=True, stop=True).then_inc(sm_done, 1)

            def step(l, last):
                mix(l)
                phase_b(l)
                if not last:
                    phase_a(l + 1)
            layers(pe, lambda: phase_a(0), step)
            pe.wait_ge(dch, L * STEPS)
            pe.matmul(ps[0:4, 0, 0:1], qs[:, 0:4], shift, start=True, stop=True).then_inc(qt_done, 1)
            pe.wait_ge(qs_done, 1)

            def tokens(g, s, i):
                for c in range(8):
                    pe.wait_ge(h_done, g * 8 + c + 1)
                    pe.matmul(ps[0:4, OP[c % 4], :], qs[:, 4:8], v[:, bass.ds(g * NPOS + c * 512, 512)],
                              start=True, stop=True).then_inc(h_mm, 1)
            groups(pe, tokens)

            def pairs(*stages):
                with pe.Fori(0, NJ // 2) as i:
                    for stage in stages:
                        for s in range(2):
                            stage(2 * i + s, s)

            def turn3(dst, src):
                settle(pe)
                for t in range(3):
                    mm = pe.transpose(dst[0:D, 128 * t:128 * t + 128], src[:, 64 * t:64 * t + 64], ident[:, :])
                return mm

            pe.wait_ge(ones_done, 1)
            pe.wait_ge(late, 160)

            def turn_e(j, s):
                pe.wait_ge(es_done, j + 1)
                pe.wait_ge(eT_done, 2 * j + 2)
                turn3(ps[:, s, :], es[:, s]).then_inc(tr_done, 1)

            def u_mm(j, s):
                pe.wait_ge(eT_done, 4 + 2 * j + 2)
                pe.wait_ge(wv_done, 2 * j + 2)
                for nh in range(2):
                    pe.matmul(ps[:, 2 + 2 * s + nh, 0:384], dx[:, 128 * nh:128 * nh + 128], eTs[:, s],
                              start=True, stop=True).then_inc(u_done, 1)

            def u_sum(j, s):
                pe.wait_ge(wv_done, 4 + 2 * j + 2)
                pe.wait_ge(ur_done, j + 1)
                for nh in range(2):
                    mm = pe.matmul(ps[0:1, 6 + s, 0:384], ones, xa[:, nh, bass.ds(j * 384, 384)],
                                   start=nh == 0, stop=nh == 1)
                mm.then_inc(us_done, 1)
            pairs(turn_e, u_mm, u_sum)

            def scores(j, s):
                pe.wait_ge(xs_done, j + 1)
                pe.wait_ge(am_done, 2 * j + 2)
                for two in range(2):
                    o = two * T
                    for nh in range(2):
                        pe.matmul(ps[64 * two:64 * two + 64, s, 0:T], xs[:, s, nh, o:o + SX], xs[:, s, nh, o:o + T],
                                  start=nh == 0, stop=nh == 1)
                    for nh in range(2):
                        mm = pe.matmul(ps[:, 2 + s, 128 * two:128 * two + 128], xs[:, s, nh, o + SX:o + T],
                                       xs[:, s, nh, o + SX:o + T], start=nh == 0, stop=nh == 1)
                mm.then_inc(sc_done, 1)

            def values(j, s):
                pe.wait_ge(am_done, 4 + 2 * j + 2)
                pe.wait_ge(vs_done, j + 1)
                pe.wait_ge(at_done, 3 * j + 3)
                settle(pe)
                for two in range(2):
                    bank, h = 4 + 2 * s + two, slice(64 * two, 64 * two + 64)
                    pe.matmul(ps[h, bank, 0:64], Ai[h, s, 0:SX], Vs[h, s, 0:D], start=True, stop=True)
                    pe.matmul(ps[:, bank, 64:128], Ai[h, s, SX:T], Vs[h, s, 0:D], start=True, stop=False)
                    mm = pe.matmul(ps[:, bank, 64:128], At[:, s, 128 * two:128 * two + 128],
                                   Vs[:, s, D * (1 + two):D * (2 + two)], start=False, stop=True)
                mm.then_inc(a_done, 1)
            pairs(scores, values)

            def turn_a(j, s):
                pe.wait_ge(as_done, j + 1)
                pe.wait_ge(aT_done, 2 * j + 2)
                turn3(ps[:, s, :], es[:, s]).then_inc(tr2_done, 1)

            def y_mm(j, s):
                pe.wait_ge(aT_done, 4 + 2 * j + 2)
                pe.wait_ge(ym_done, 2 * j + 2)
                for nh in range(2):
                    pe.matmul(ps[:, 2 + 2 * s + nh, 0:384], dy[:, 128 * nh:128 * nh + 128], eTs[:, s],
                              start=True, stop=True).then_inc(yc_done, 1)

            def e_mm(j, s):
                pe.wait_ge(ym_done, 4 + 2 * j + 2)
                pe.wait_ge(ve_done, j + 1)
                for two in range(2):
                    h, o = slice(64 * two, 64 * two + 64), two * T
                    for nh in range(2):
                        pe.matmul(ps[h, 6 + s, 0:D], ys[:, s, nh, o:o + SX], ET[:, nh], start=nh == 0, stop=nh == 1)
                for two in range(2):
                    o = two * T
                    for nh in range(2):
                        mm = pe.matmul(ps[:, 6 + s, D * (1 + two):D * (2 + two)], ys[:, s, nh, o + SX:o + T], ET[:, nh],
                                       start=nh == 0, stop=nh == 1)
                mm.then_inc(vo_done, 1)
            pairs(turn_a, y_mm, e_mm)

            def chunks(*stages):
                with pe.Fori(0, NT // CH // 2) as i:
                    for stage in stages:
                        for s in range(2):
                            stage(2 * i + s, s)

            def turn_h(k, s):
                pe.wait_ge(e2s_done, k + 1)
                pe.wait_ge(e2T_done, k + 1)
                settle(pe)
                for t in range(CH):
                    mm = pe.transpose(ps[0:D, s, 128 * t:128 * t + 128], e2s[:, s, D * t:D * t + D], ident[:, :])
                mm.then_inc(tr3_done, 1)

            def route(k, s):
                pe.wait_ge(e2T_done, 2 + k + 1)
                pe.wait_ge(lg_done, k + 1)
                for t in range(CH):
                    mm = pe.matmul(ps[:, 2 + s, E * t:E * t + E], e2Ts[:, s, 128 * t:128 * t + 128], Wr,
                                   start=True, stop=True)
                mm.then_inc(rt_done, 1)
            chunks(turn_h, route)

            pe.wait_ge(w1_in, 16)
            pe.wait_ge(e2c_done, 2 + NT // CH)
            pe.wait_ge(lg_done, 2 + NT // CH)

            def experts(k, s):
                def up(e):
                    for fh in range(2):
                        n = 2 * e + fh
                        pe.wait_ge(gelu_done, k * 18 + n + 1)
                        settle(pe)
                        pe.matmul(ps[:, n % 3, :], W1[:, e, 128 * fh:128 * fh + 128], e2T[:, bass.ds(k * 512, 512)],
                                  start=True, stop=True).then_inc(hm_done, 1)
                up(0)
                for e in range(E + 1):
                    if e < E:
                        up(e + 1)
                    else:
                        pe.wait_ge(sh_done, k + 1)
                    pe.wait_ge(gelu_done, 3 + k * 18 + 2 * e + 2)
                    for t in range(CH):
                        if e == 0:
                            pe.wait_ge(p_done, 4 * k + t + 1)
                        for fh in range(2):
                            o = ps[:, 4 + t, D * e:D * e + D] if e < E else ps[:, 3, D * t:D * t + D]
                            mm = pe.matmul(o, hT[:, 2 * (e % 3) + fh, 128 * t:128 * t + 128], W2[:, fh, e],
                                           start=fh == 0, stop=fh == 1)
                    mm.then_inc(w2_done, 1)
            chunks(experts)

        @block.scalar
        def _(act):
            act.sem_inc(v0_done, 2)
            act.sem_inc(t2e_done, 2)
            act.sem_inc(f2e_done, 2)
            act.sem_inc(y_done, 4)
            act.sem_inc(ze_done, 2)
            act.sem_inc(oe_done, 4)
            act.sem_inc(h_done, 4)
            for sm_, n in ((wv_done, 4), (at_done, 6), (ve_done, 2), (e2c_done, 2), (gelu_done, 3)):
                act.sem_inc(sm_, n)
            act.sem_inc(primed, 1)
            act.wait_ge(primed, 4)
            with act.Fori(0, G * 4) as i:
                for s in range(2):
                    act.wait_ge(v0_mm, 2 + 2 * i + s + 1)
                    act.activation(v[:, bass.ds((2 * i + s) * 512, 512)], ps[:, s, :], ACT.Copy).then_inc(v0_done, 1)

            def phase_a(a, func):
                def group(g, s, i):
                    ga = a * G + g
                    for r in range(4):
                        act.wait_ge(t1_done, ga * 8 + 2 * r + 2)
                        act.wait_ge(v_stored[r], 16 * ga + 16)
                        src = v[:, bass.ds(g * NPOS + r * 1024, 1024)]
                        dst = R[:, r * 1024:(r + 1) * 1024]
                        if func is ACT.Copy:
                            act.activation(dst, src, func).then_inc(relu_done, 1)
                        else:
                            act.activation(dst, src, func, bias=shift, scale=scale).then_inc(relu_done, 1)
                    for k in range(3):
                        k3 = ga * 3 + k
                        act.wait_ge(t2_done, 3 + k3 + 1)
                        act.wait_ge(f2_done, k3 + 1)
                        act.activation(T2s[:, (s * 3 + k) % 2], ps[:, T2P[(s * 3 + k) % 2], :], ACT.Copy).then_inc(t2e_done, 1)
                    for m in range(2):
                        act.wait_ge(f2_done, 2 + ga * 3 + 2 + m)
                        act.wait_ge(x_stored[s], 256 * (a * 4 + i) + 256)
                        act.activation(F2o[:, s, :, 6 * m:6 * m + 6].rearrange("p h k m -> p k h m"),
                                       ps[:, F2P[m], 0:288].rearrange("p (k h m) -> p k h m", k=6, h=4),
                                       ACT.Copy).then_inc(f2e_done, 1)
                groups(act, group)

            def mix(l):
                for p in range(6):
                    for h in range(2):
                        hh = (l * 6 + p) * 2 + h
                        act.wait_ge(mix_done, 4 + hh + 1)
                        act.wait_ge(yt_done, l * 6 + p + 1)
                        act.activation(Ys[:, p % 2, :, 12 * h:12 * h + 12].rearrange("p o k -> p k o"),
                                       ps[:, (p % 2) * 2 + h, 0:384].rearrange("p (k o) -> p k o", o=C),
                                       ACT.Copy).then_inc(y_done, 1)

            def phase_b(l):
                act.wait_ge(lp_loaded, 16 * (l + 1))

                def group(g, s, i):
                    gb = l * G + g

                    def zcopy(z):
                        act.wait_ge(t4_done, 8 + gb * 4 + z + 1)
                        act.wait_ge(fin_done, (gb * 4 + z) * 2 + 2)
                        act.activation(S[:, z % 2], ps[:, ZP[z % 2], :], ACT.Copy).then_inc(ze_done, 1)

                    def keep(c):
                        act.wait_ge(fin_done, 4 + gb * 8 + c + 1)
                        act.activation(v[:, bass.ds(g * NPOS + c * 512, 512)], ps[:, OP[c % 4], :], ACT.Identity,
                                       bias=wb).then_inc(oe_done, 1)
                    zcopy(0)
                    zcopy(1)
                    keep(0)
                    keep(1)
                    zcopy(2)
                    keep(2)
                    keep(3)
                    zcopy(3)
                    for c in range(4, 8):
                        keep(c)
                groups(act, group)
                act.wait_ge(dch, l * STEPS + 5)
                act.activation(sd, var, ACT.Sqrt).then_inc(sq_done, 1)
                act.wait_ge(dch, (l + 1) * STEPS)
                act.wait_ge(oe_done, 4 + (l + 1) * 64)

            def step(l, last):
                mix(l)
                phase_b(l)
                if not last:
                    phase_a(l + 1, ACT.Relu)
            act.wait_ge(v0_done, 2 + G * 8)
            layers(act, lambda: phase_a(0, ACT.Copy), step)
            act.wait_ge(qb_done, 1)

            def tokens(g, s, i):
                for c in range(8):
                    act.wait_ge(h_mm, g * 8 + c + 1)
                    if c % 4 == 0:
                        act.wait_ge(h_stored[c // 4], 64 * g + 16)
                    act.activation(phase[0:4, 512 * c:512 * c + 512], ps[0:4, OP[c % 4], :], ACT.Identity,
                                   bias=sm[0:4, 17:18]).then_inc(h_done, 1)
            groups(act, tokens)

            def pairs(*stages):
                settle(act)
                with act.Fori(0, NJ // 2) as i:
                    for stage in stages:
                        for s in range(2):
                            stage(2 * i + s, s)

            def root(n, after):
                act.wait_ge(steps, after)
                act.activation(lns[:, 192:240], lns[:, 144:192], ACT.Sqrt).then_inc(sqrt_done, 1)

            root(1, STEP_E - 6)
            act.wait_ge(steps, STEP_E)

            def e_copy(j, s):
                act.wait_ge(tr_done, j + 1)
                settle(act)
                act.activation(es[:, s], phase[:, bass.ds(j * 192, 192)], ACT.Copy).then_inc(es_done, 1)

            def u_relu(j, s):
                for nh in range(2):
                    act.wait_ge(u_done, 4 + 2 * j + nh + 1)
                    settle(act)
                    act.activation(xa[:, nh, bass.ds(j * 384, 384)], ps[:, 2 + 2 * s + nh, 0:384],
                                   ACT.Relu).then_inc(wv_done, 1)
            pairs(e_copy, u_relu)
            root(2, STEP_V - 6)
            act.wait_ge(steps, STEP_X)

            def x_copy(j, s):
                act.wait_ge(sc_done, j + 1)
                settle(act)
                act.activation(xs[:, s], xa[:, :, bass.ds(j * 384, 384)], ACT.Copy).then_inc(xs_done, 1)

            def a_copy(j, s):
                act.wait_ge(a_done, 2 + j + 1)
                o = bass.ds(j * 192, 64)
                settle(act)
                act.activation(phase[0:64, o], ps[0:64, 4 + 2 * s, 0:64], ACT.Copy).then_inc(at_done, 1)
                act.activation(phase[64:128, o], ps[64:128, 5 + 2 * s, 0:64], ACT.Copy).then_inc(at_done, 1)
                act.activation(phase[:, bass.ds(j * 192 + 64, 128)].rearrange("p (b d) -> p b d", b=2),
                               ps[:, 4 + 2 * s:6 + 2 * s, 64:128], ACT.Copy).then_inc(at_done, 1)
            pairs(x_copy, a_copy)
            root(3, STEP_A - 6)
            act.wait_ge(steps, STEP_A)

            def an_copy(j, s):
                act.wait_ge(tr2_done, j + 1)
                settle(act)
                act.activation(es[:, s], phase[:, bass.ds(j * 192, 192)], ACT.Copy).then_inc(as_done, 1)

            def v_copy(j, s):
                act.wait_ge(vo_done, 2 + j + 1)
                settle(act)
                act.activation(phase[:, bass.ds(3072 + j * 192, 192)], ps[:, 6 + s, 0:192], ACT.Copy).then_inc(ve_done, 1)
            pairs(an_copy, v_copy)
            root(4, STEP_VS - 6)
            root(5, STEP_H - 6)
            act.wait_ge(steps, STEP_H)

            def chunks(*stages):
                settle(act)
                with act.Fori(0, NT // CH // 2) as i:
                    for stage in stages:
                        for s in range(2):
                            stage(2 * i + s, s)

            def h_copy(k, s):
                act.wait_ge(tr3_done, k + 1)
                settle(act)
                act.activation(e2s[:, s], phase[:, bass.ds(k * 256, 256)], ACT.Copy).then_inc(e2s_done, 1)

            def keep_turned(k, s):
                act.wait_ge(e2T_done, 2 + k + 1)
                settle(act)
                act.activation(e2T[:, bass.ds(k * 512, 512)], e2Ts[:, s], ACT.Copy).then_inc(e2c_done, 1)
            chunks(h_copy, keep_turned)
            act.wait_ge(steps, STEP_L)
            act.activation(ex, lz, ACT.Exp).then_inc(exp_done, 1)

            def gelus(k, s):
                for e in range(E + 1):
                    act.wait_ge(w2_done, k * 9 + e + 1)
                    for fh in range(2):
                        n = 2 * e + fh
                        act.wait_ge(hm_done, k * 18 + n + 1)
                        act.activation(hT[:, 2 * (e % 3) + fh], ps[:, n % 3, :], ACT.Gelu,
                                       bias=B1[:, n:n + 1]).then_inc(gelu_done, 1)
            act.wait_ge(steps, STEP_M)
            chunks(gelus)

        @block.vector
        def _(dve):
            dve.sem_inc(s_done, 2)
            dve.sem_inc(f1e_done, 2)
            dve.sem_inc(yt_done, 2)
            dve.sem_inc(i1e_done, 2)
            dve.sem_inc(bs_done, 4)
            for sm_, n in ((eT_done, 4), (ur_done, 2), (am_done, 4), (aT_done, 4), (ym_done, 4), (e2T_done, 2),
                           (lg_done, 2), (p_done, 4), (m_done, 4), (sh_done, 1)):
                dve.sem_inc(sm_, n)
            dve.memset(ones, 1.0).then_inc(ones_done, 1)
            dve.sem_inc(primed, 1)
            dve.wait_ge(primed, 4)
            dve.wait_ge(consts, 16 * (NCONST - 1))
            dve.wait_ge(zeroed, 2)

            def phase_a(a):
                def group(g, s, i):
                    ga = a * G + g
                    for c in range(8):
                        dve.wait_ge(t1_done, 8 + ga * 8 + c + 1)
                        dve.wait_ge(f1_done, ga * 8 + c + 1)
                        dve.tensor_copy(S[:, c % 2], ps[:, TP[c % 2], :]).then_inc(s_done, 1)
                        if c % 2 == 1:
                            m = c // 2
                            dve.wait_ge(f1_done, 2 + ga * 8 + c + 1)
                            dve.wait_ge(t2_done, ga * 3 + 3)
                            dve.tensor_copy(F1o[:, :, 16 * m:16 * m + 16],
                                            ps[:, FP[m % 2], 0:384].rearrange("p (x k) -> p k x", k=KR)).then_inc(f1e_done, 1)
                groups(dve, group)

            def mix(l):
                for s in range(2):
                    dve.wait_ge(x_stored[s], 256 * (l * 4 + 4) + 256)
                for r in range(4):
                    dve.wait_ge(v_stored[r], 16 * G * (l + 1) + 16)
                for p in range(6):
                    for par in range(2):
                        ky = 2 * p + par
                        dve.wait_ge(mix_done, (l * 6 + p) * 2 + 4)
                        dve.tensor_copy(XB[64:128, par, :, 32:64], X[64:128, :, ky].rearrange("p b m -> p m b")).then_inc(xb1_done, 1)
                    if p >= 1:
                        turn(l, p - 1)
                turn(l, 5)

            def turn(l, p):
                dve.wait_ge(y_done, 4 + (l * 6 + p) * 2 + 2)
                dve.transpose(H[:, p].rearrange("p o b -> p (o b)"), Ys[:, p % 2].rearrange("p o k -> p (o k)")).then_inc(yt_done, 1)

            def phase_b(l):
                def group(g, s, i):
                    gb = l * G + g
                    dve.wait_ge(t4_done, gb * 4 + 4)
                    for u in range(4):
                        par = u % 2
                        k0 = 12 * (u // 2)
                        dve.wait_ge(i1_done, 8 + gb * 4 + u + 1)
                        dst = I1o[:, s, :, k0:k0 + 12].rearrange("p x (k e r) -> p k e r x", e=2, r=2)[:, :, par]
                        dve.tensor_copy(dst, ps[:, IP[par], 0:384].rearrange("p (k r x) -> p k r x", r=2, x=SX)).then_inc(i1e_done, 1)
                    for c in range(8):
                        dve.wait_ge(oe_done, 4 + gb * 8 + c + 1)
                        settle(dve)
                        dve.bn_stats(st[:, bass.ds((g * 8 + c) * 6, 6)],
                                     v[:, bass.ds(g * NPOS + c * 512, 512)]).then_inc(bs_done, 1)
                groups(dve, group)

                def link(n, ins):
                    ins.then_inc(dch, 1)
                    dve.wait_ge(dch, l * STEPS + n)
                dve.wait_ge(bs_done, 4 + (l + 1) * 64)
                settle(dve)
                link(1, dve.bn_aggr(agg, st[:, :]))
                dve.wait_ge(sm_done, 2 * l + 1)
                link(2, dve.tensor_copy(mv, ps[:, 0, 0:2]))
                link(3, dve.tensor_tensor(dif, agg[:, 0:1], mv[:, 0:1], ALU.subtract))
                link(4, dve.tensor_tensor(sq, dif, dif, ALU.mult))
                dve.wait_ge(sm_done, 2 * l + 2)
                link(5, dve.tensor_scalar(var, ps[:, 1, 0:1], mv[:, 1:2], EPS, ALU.add, ALU.add))
                dve.wait_ge(sq_done, l + 1)
                link(6, dve.reciprocal(r0, sd))
                link(7, dve.tensor_tensor(r2, r0, r0, ALU.mult))
                link(8, dve.tensor_scalar(t1, r2, var, -0.5, ALU.mult, ALU.mult))
                link(9, dve.tensor_scalar(rs, t1, 1.5, r0, ALU.add, ALU.mult))
                link(10, dve.tensor_tensor(scale, rs, gamma, ALU.mult))
                link(11, dve.tensor_copy(mw, mv[:, 0:1]))
                link(12, dve.tensor_tensor(ms, mw, scale, ALU.mult))
                link(13, dve.tensor_tensor(shift, beta, ms, ALU.subtract))

            def step(l, last):
                mix(l)
                phase_b(l)
                if not last:
                    phase_a(l + 1)
            layers(dve, lambda: phase_a(0), step)
            dve.tensor_scalar(qs[:, 4:8], qs[:, 0:4], scale, None, ALU.mult).then_inc(qs_done, 1)
            dve.wait_ge(qt_done, 1)
            dve.tensor_tensor(sm[0:4, 17:18], ps[0:4, 0, 0:1], qbias[0:4, :], ALU.add).then_inc(qb_done, 1)


            def pairs(*stages):
                settle(dve)
                with dve.Fori(0, NJ // 2) as i:
                    for stage in stages:
                        for s in range(2):
                            stage(2 * i + s, s)

            done = [0]

            def do(ins):
                done[0] += 1
                ins.then_inc(steps, 1)
                dve.wait_ge(steps, done[0])

            def norm(dst, src, scratch, eps, nth):
                wide = lambda a: a.unsqueeze(2).broadcast_to([128, NT, D])
                tot, mean, vs, ve, sdv, rv, rv2, nt, rst = (lns[:, 48 * i:48 * i + 48] for i in range(9))
                do(dve.tensor_reduce(tot, src, AX.X, ALU.add))
                do(dve.tensor_scalar(mean, tot, 1.0 / D, None, ALU.mult))
                do(dve.tensor_tensor(dst, src, wide(mean), ALU.subtract))
                do(dve.tensor_tensor(scratch, dst, dst, ALU.mult))
                do(dve.tensor_reduce(vs, scratch, AX.X, ALU.add))
                do(dve.tensor_scalar(ve, vs, 1.0 / D, eps, ALU.mult, ALU.add))
                dve.wait_ge(sqrt_done, nth)
                do(dve.reciprocal(rv, sdv))
                do(dve.tensor_tensor(rv2, rv, rv, ALU.mult))
                do(dve.tensor_tensor(nt, rv2, ve, ALU.mult))
                do(dve.tensor_scalar(rst, nt, -0.5, 1.5, ALU.mult, ALU.add))
                do(dve.tensor_tensor(rst, rst, rv, ALU.mult))
                do(dve.tensor_tensor(dst, dst, wide(rst), ALU.mult))

            dve.wait_ge(txt_in, 32)
            for s in range(2):
                dve.wait_ge(h_stored[s], 16 * (1 + 4 * G))
            norm(eb, h_all, tmp, EPS, 1)
            assert done[0] == STEP_E

            def by_batch(k, s, done_sem):
                src, dst = ps[0:D, s, :], eTs[:, s].rearrange("p (b t) -> p b t", b=2)
                dve.tensor_copy(dst[:, :, 0:SX], src[:, 0:128].rearrange("p (b t) -> p b t", b=2)).then_inc(done_sem, 1)
                dve.tensor_copy(dst[:, :, SX:T], src[:, 128:384].rearrange("p (b t) -> p b t", b=2)).then_inc(done_sem, 1)

            def e_turned(j, s):
                dve.wait_ge(tr_done, 2 + j + 1)
                dve.wait_ge(u_done, 2 * j + 2)
                by_batch(j, s, eT_done)

            def u_total(j, s):
                dve.wait_ge(us_done, j + 1)
                dve.tensor_copy(u_row[:, bass.ds(j * 384, 384)], ps[0:1, 6 + s, 0:384]).then_inc(ur_done, 1)
            pairs(e_turned, u_total)

            dve.wait_ge(u_moved, 16)
            big = DECAY / TINY
            do(dve.tensor_scalar(k1, U, TINY, -big, ALU.is_ge, ALU.mult))
            do(dve.tensor_scalar(k2, k1, big, 1.0, ALU.add, ALU.max))
            do(dve.tensor_tensor_scan(z, k2, U, 0.0, ALU.mult, ALU.add))
            do(dve.tensor_scalar(k1[:, 1:T], z[:, 0:T - 1], big, DECAY, ALU.mult, ALU.min))
            do(dve.memset(k1[:, 0:1], 0.0))
            do(dve.tensor_tensor(k2, k1, U, ALU.add))
            do(dve.tensor_scalar(k1, k2, TINY, None, ALU.max))
            do(dve.reciprocal(rsum, k1))
            do(dve.memset(csum[:, 0:1], 0.0))
            do(dve.tensor_scalar(csum[:, 1:T], rsum[:, 0:T - 1], DECAY, None, ALU.mult))
            assert done[0] == STEP_RC
            norm(vb, eb, tmp, EPS, 2)
            assert done[0] == STEP_V
            dve.wait_ge(c_in, 16)
            for nh in range(2):
                do(dve.tensor_tensor_scan(xa[:, nh], cB, xa[:, nh], 0.0, ALU.mult, ALU.add))
            dve.wait_ge(r_in, 16)
            for nh in range(2):
                do(dve.tensor_tensor(xa[:, nh], xa[:, nh], rB, ALU.mult))
            assert done[0] == STEP_X

            def decay(j, s):
                dve.wait_ge(sc_done, 2 + j + 1)
                dve.wait_ge(a_done, j + 1)
                dve.tensor_tensor(Ai[:, s], ps[:, s, 0:T], Di, ALU.mult).then_inc(am_done, 1)
                dve.tensor_tensor(At[:, s].rearrange("p (b t) -> p b t", b=2),
                                  ps[:, 2 + s, 0:256].rearrange("p (b t) -> p b t", b=2),
                                  Dt.unsqueeze(1).broadcast_to([128, 2, TXT]), ALU.mult).then_inc(am_done, 1)
            pairs(decay)
            dve.wait_ge(at_done, 6 + 3 * NJ)
            norm(eb, eb, tmp2, EPS, 3)
            assert done[0] == STEP_A

            def a_turned(j, s):
                dve.wait_ge(tr2_done, 2 + j + 1)
                dve.wait_ge(yc_done, 2 * j + 2)
                by_batch(j, s, aT_done)

            def gate(j, s):
                dve.wait_ge(vo_done, j + 1)
                for nh in range(2):
                    dve.wait_ge(yc_done, 4 + 2 * j + nh + 1)
                    dve.scalar_tensor_tensor(ys[:, s, nh], ps[:, 2 + 2 * s + nh, 0:384], 0.0,
                                             xa[:, nh, bass.ds(j * 384, 384)], ALU.max, ALU.mult).then_inc(ym_done, 1)
            pairs(a_turned, gate)
            dve.wait_ge(ve_done, 2 + NJ)
            norm(vb, vb, tmp2, EPS, 4)
            do(dve.tensor_tensor(h_all, h_all, vb, ALU.add))
            norm(eb, h_all, tmp2, EPS, 5)
            assert done[0] == STEP_H

            def chunks(*stages):
                settle(dve)
                with dve.Fori(0, NT // CH // 2) as i:
                    for stage in stages:
                        for s in range(2):
                            stage(2 * i + s, s)

            def h_turned(k, s):
                dve.wait_ge(tr3_done, 2 + k + 1)
                dve.wait_ge(rt_done, k + 1)
                dve.wait_ge(e2c_done, k + 1)
                dve.tensor_copy(e2Ts[:, s], ps[0:D, s, :]).then_inc(e2T_done, 1)

            def logits(k, s):
                dve.wait_ge(rt_done, 2 + k + 1)
                dve.tensor_copy(cB[:, bass.ds(2048 + k * CH * E, CH * E)], ps[:, 2 + s, 0:CH * E]).then_inc(lg_done, 1)
            chunks(h_turned, logits)
            dve.wait_ge(lg_done, 2 + NT // CH)
            settle(dve)

            wide = lambda a: a.unsqueeze(2).broadcast_to([128, NT, E])
            ranks = rank.unsqueeze(1).broadcast_to([128, NT, E])
            top, tot, inv, m1, c1, m2, c2, den, dinv = (rr[:, i] for i in range(9))
            do(dve.tensor_reduce(top, lg, AX.X, ALU.max))
            do(dve.tensor_tensor(lz, lg, wide(top), ALU.subtract))
            assert done[0] == STEP_L
            dve.wait_ge(exp_done, 1)
            do(dve.tensor_reduce(tot, ex, AX.X, ALU.add))
            do(dve.reciprocal(inv, tot))
            do(dve.tensor_tensor(rw, ex, wide(inv), ALU.mult))
            do(dve.tensor_reduce(m1, rw, AX.X, ALU.max))
            do(dve.tensor_tensor(eq, rw, wide(m1), ALU.is_equal))
            do(dve.tensor_tensor(cd, eq, ranks, ALU.mult))
            do(dve.tensor_reduce(c1, cd, AX.X, ALU.max))
            do(dve.tensor_tensor(oh1, wide(c1), ranks, ALU.is_equal))
            do(dve.scalar_tensor_tensor(rw2, oh1, -4.0, rw, ALU.mult, ALU.add))
            do(dve.tensor_reduce(m2, rw2, AX.X, ALU.max))
            do(dve.tensor_tensor(eq, rw2, wide(m2), ALU.is_equal))
            do(dve.tensor_tensor(cd, eq, ranks, ALU.mult))
            do(dve.tensor_reduce(c2, cd, AX.X, ALU.max))
            do(dve.tensor_tensor(oh2, wide(c2), ranks, ALU.is_equal))
            do(dve.tensor_tensor(den, m1, m2, ALU.add))
            do(dve.reciprocal(dinv, den))
            do(dve.tensor_tensor(oh1, oh1, oh2, ALU.add))
            do(dve.tensor_tensor(oh1, oh1, rw, ALU.mult))
            do(dve.tensor_tensor(mask, oh1, wide(dinv), ALU.mult))
            assert done[0] == STEP_M

            def combine(k, s):
                dve.wait_ge(w2_done, 3 + 9 * k + E)
                for t in range(CH):
                    dve.wait_ge(m_done, 4 * k + t + 1)
                    dve.tensor_tensor(tb[:, t].rearrange("p e d -> p (e d)"), ps[:, 4 + t, :], B2[:, 0:E * D],
                                      ALU.add).then_inc(p_done, 1)
                for t in range(CH):
                    dve.wait_ge(p_done, 4 + 4 * k + t + 1)
                    mk = cB[:, bass.ds(2048 + 9 * 384 + (k * CH + t) * E, E)].unsqueeze(2).broadcast_to([128, E, D])
                    dve.tensor_tensor(tb[:, t], tb[:, t], mk, ALU.mult).then_inc(m_done, 1)
                for t in range(CH):
                    dve.wait_ge(m_done, 4 + 4 * k + t + 1)
                    dve.tensor_reduce(rt[:, t], tb[:, t].rearrange("p e d -> p d e"), AX.X, ALU.add).then_inc(r_done, 1)
                dve.wait_ge(w2_done, 3 + 9 * k + 9)
                dve.tensor_tensor(s1, ps[:, 3, 0:256].rearrange("p (t d) -> p t d", d=D),
                                  B2[:, E * D:].unsqueeze(1).broadcast_to([128, CH, D]), ALU.add).then_inc(sh_done, 1)
                dve.wait_ge(r_done, 4 * k + 4)
                dve.wait_ge(sh_done, 1 + k + 1)
                dve.tensor_tensor(s2, s1, rt, ALU.add).then_inc(s2_done, 1)
                dve.wait_ge(s2_done, k + 1)
                hk = Xr[:, bass.ds(k * 256, 256)].rearrange("p (t d) -> p t d", d=D)
                dve.tensor_tensor(hk, hk, s2, ALU.add).then_inc(f_done, 1)
            chunks(combine)


def kernel(**inputs):
    import numpy as np
    import concourse.bacc as bacc
    from concourse.bass_utils import run_bass_kernel_spmd

    f = {k: np.ascontiguousarray(a) for k, a in inputs.items()}
    arrays = {}
    arrays["x"] = f["x"].reshape(B, NPOS)
    gx = np.linspace(0.0, 1.0, SX, dtype=np.float32)
    grid = np.stack([np.repeat(gx, SY), np.tile(gx, SX), np.ones(NPOS, np.float32)])
    arrays["grid"] = np.ascontiguousarray(np.broadcast_to(grid[:, None], (3, G, NPOS)))
    pin = np.zeros((Q + 3, Q, C), np.float32)
    for q in range(Q):
        pin[q, q] = f["L0_tok_p_w"][0]
        pin[Q, q] = f["L0_tok_p_w"][1]
        pin[Q + 1, q] = f["L0_tok_p_w"][2]
        pin[Q + 2, q] = f["L0_tok_p_b"]
    arrays["pin"] = pin.reshape(Q + 3, 128)
    arrays["txt"] = f["txt"]
    avg = np.kron(np.full((Q, Q), 1.0 / Q), np.eye(C)).astype(np.float32)
    names = []
    for n, a in enumerate([*spectral_tables(), np.eye(128, dtype=np.float32), avg]):
        arrays[f"table{n}"] = a
        names.append(f"table{n}")
    fw = np.stack([f["L0_tok_fw1"], f["L0_tok_fw2"]])
    a = fw.transpose(5, 0, 2, 1, 4, 6, 3)
    a = np.stack([a, a[..., ::-1, :]], axis=2)
    arrays["fw"] = np.ascontiguousarray(a.reshape(M, 128, L, M, 64))
    lp = np.zeros((L, 128, 131), np.float32)
    for q in range(Q):
        s = slice(q * C, (q + 1) * C)
        lp[:, s, s] = f["L0_tok_w_w"]
        lp[:, s, 128], lp[:, s, 129], lp[:, s, 130] = f["L0_tok_w_b"], f["L0_tok_bn_g"], f["L0_tok_bn_b"]
    arrays["lp"] = lp
    qblk = np.zeros((128, 4), np.float32)
    for q in range(Q):
        qblk[q * C:(q + 1) * C, q] = f["L0_tok_q_w"][:, 0]
    arrays["qblk"] = qblk
    arrays["qb"] = np.ascontiguousarray(np.broadcast_to(f["L0_tok_q_b"].reshape(1, 1), (4, 1)))

    arrays["att"] = attention_tables()
    arrays["dxy"] = np.concatenate([f["L0_attn_Dx"].T, f["L0_attn_Dy"].T], axis=1)
    arrays["et"] = f["L0_attn_E"].T.reshape(2, 128, D).transpose(1, 0, 2)
    w1 = np.concatenate([f["L0_ffn_W1p"], f["L0_ffn_W1s"][None]])
    w2 = np.concatenate([f["L0_ffn_W2p"], f["L0_ffn_W2s"][None]])
    b1 = np.concatenate([f["L0_ffn_b1p"], f["L0_ffn_b1s"][None]])
    b2 = np.concatenate([f["L0_ffn_b2p"], f["L0_ffn_b2s"][None]])
    arrays["w1"] = w1.transpose(1, 0, 2)
    arrays["w2"] = w2.reshape(E + 1, 2, 128, D).transpose(2, 1, 0, 3)
    arrays["wr"] = f["L0_ffn_Wr"]
    arrays["b1"] = b1.reshape(2 * (E + 1), 128).T
    arrays["b2"] = np.broadcast_to(b2.reshape(1, -1), (128, (E + 1) * D))

    nc = bacc.Bacc("TRN2", target_bir_lowering=False, num_devices=1)
    arrays = {f"in_{k}": np.ascontiguousarray(a) for k, a in arrays.items()}
    ap = {k: nc.dram_tensor(k, a.shape, mybir.dt.from_np(a.dtype), kind="ExternalInput").ap() for k, a in arrays.items()}
    out = nc.dram_tensor("out_0", (B, T, D), F32, kind="ExternalOutput").ap()
    build(nc, ap["in_x"], ap["in_grid"], ap["in_pin"], ap["in_txt"], [ap[f"in_{n}"] for n in names], ap["in_fw"],
          ap["in_lp"], ap["in_qblk"], ap["in_qb"], ap["in_att"], ap["in_dxy"], ap["in_et"], ap["in_w1"], ap["in_w2"],
          ap["in_wr"], ap["in_b1"], ap["in_b2"], nc.dram_tensor("norms", (2, NW), F32, kind="Internal").ap(), out)
    r = run_bass_kernel_spmd(nc, [arrays], core_ids=[0])
    return r.results[0]["out_0"]
```

```python
from contextlib import ExitStack

import concourse.bass as bass
from concourse import mybir

ACT = mybir.ActivationFunctionType
ALU = mybir.AluOpType
AX = mybir.AxisListType
F32, F16 = mybir.dt.float32, mybir.dt.float16

B, SX, SY = 32, 64, 64
C, L, M = 32, 4, 12
Q = 4
G = B // Q
NPOS = SX * SY
KR = 2 * M
TXT, D = 128, 64
T = SX + TXT
N = 256
NJ = B // 2
EPS = 1e-5
DECAY, TINY = 0.97, 1e-12
E, F = 8, 256
NT = 3 * NJ
NW = B * T
CH = 4
NC = NT // CH
WS, RS = 2.0 ** 8, 2.0 ** 10


def spectral_tables():
    import numpy as np

    y, ky = np.arange(SY), np.arange(M)
    kx = np.concatenate([np.arange(M), np.arange(SX - M, SX)])
    x = np.arange(SX)
    ay = 2 * np.pi * np.outer(y, ky) / SY
    ax = 2 * np.pi * np.outer(x, kx) / SX
    fy = np.zeros((2, SY, 2, M, 2))
    for i in range(2):
        fy[i, :, i, :, 0] = np.cos(ay)
        fy[i, :, i, :, 1] = -np.sin(ay)
    fx = np.zeros((2, SX, 2, 2, M))
    c, s = np.cos(ax).reshape(SX, 2, M), np.sin(ax).reshape(SX, 2, M)
    fx[0, :, :, 0], fx[0, :, :, 1] = c, -s
    fx[1, :, :, 0], fx[1, :, :, 1] = s, c
    ix = np.zeros((2, 2, 32, 2, SX))
    c, s = np.cos(ax).T.reshape(2, M, SX), np.sin(ax).T.reshape(2, M, SX)
    ix[:, :, 0:KR:2, 0], ix[:, :, 0:KR:2, 1] = c, s
    ix[:, :, 1:KR:2, 0], ix[:, :, 1:KR:2, 1] = -s, c
    w = np.where(ky == 0, 1.0, 2.0)[:, None] / (SX * SY)
    iy = np.zeros((4, 32, 4, SY))
    for i in range(4):
        iy[i, 0:KR:2, i] = w * np.cos(ay).T
        iy[i, 1:KR:2, i] = -w * np.sin(ay).T
    f = lambda a, n: a.reshape(128, n).astype(np.float32)
    fy1 = fy[0, :, 0].reshape(SY, KR)
    fx2 = np.zeros((2, SX, 2, 2, 2, 2, M))
    for i in range(2):
        fx2[i, :, :, i] = fx.transpose(1, 0, 2, 3, 4)
    gx, one = np.linspace(0, 1, SX), np.ones(SX)
    modes = np.stack([np.exp(-1j * ay).T @ b[:, None] * (a[None] @ np.exp(-1j * ax)) for a, b in ((gx, one), (one, gx), (one, one))])
    modes = modes.reshape(3, M, 2, M).transpose(0, 2, 1, 3)
    gm = np.stack([modes.real, modes.imag], axis=2).reshape(12, M * M).astype(np.float32)
    def halves(a):
        a = a.reshape(128, 48)
        high = a.astype(np.float16)
        return np.concatenate([high, (a - high).astype(np.float16)], axis=1)
    return halves(fy), halves(fx), f(ix, 128), f(iy, 256), fy1.astype(np.float32), f(fx2, 192), gm


def attention_tables():
    import numpy as np

    s, t = np.arange(T)[:, None], np.arange(T)[None, :]
    decay = np.where(s < t, DECAY ** np.maximum(t - 1 - s, 0), 0.0).astype(np.float32)
    rank = np.broadcast_to(np.arange(E, 0, -1, dtype=np.float32), (128, E))
    return np.concatenate([np.concatenate([decay[:SX], decay[:SX]]), decay[SX:, SX:], rank], axis=1)


def build(nc, x, grid, xt, pint, pblk, txt, tables, fw, lp, qblk, qb, att, dxy, et, w1, w2, wr, b1, b2, rdram, out):
    ctx = ExitStack()
    with ctx:
        def sb(name, shape, dt=F32):
            return ctx.enter_context(nc.sbuf_tensor(name, shape, dt))

        def sem(name):
            return ctx.enter_context(nc.semaphore(name))

        v = sb("v", [128, G * NPOS])
        phase = sb("phase", [128, 6656])
        R = phase[:, 0:4096]
        F1o = phase[:, 4096:5632].rearrange("p (k x) -> p k x", x=SX)
        T2h, T2l = (phase[:, a:a + 512].bitcast(F16).rearrange("p (s n) -> p s n", s=2) for a in (5632, 6144))
        H = phase[:, 0:6144].rearrange("p (k o b) -> p k o b", k=6, o=C)
        S = sb("S", [128, 2, 512])
        Sh, Sl = (S[:, i].bitcast(F16).rearrange("p (s n) -> p s n", s=2) for i in range(2))
        Xr = sb("Xr", [128, B * 144])
        X = Xr[:, :].rearrange("p (b k m) -> p b k m", b=B, k=M)
        I1o = Xr[:, 0:4096].rearrange("p (s x k) -> p s x k", s=2, x=SX)
        hbuf = Xr[:, 0:3 * NJ * D].rearrange("p (j t d) -> p j t d", j=NJ, t=3)
        Yr = sb("Yr", [128, 2048])
        F2o = Yr[:, 0:1152].rearrange("p (s h k m) -> p s h k m", s=2, h=4, k=M)
        Ys = Yr[:, :].rearrange("p (s o k) -> p s o k", s=2, o=C)
        Hg = Yr[:, 0:1536].rearrange("p (s k n) -> p s k n", s=2, k=6)
        XB = sb("XB", [128, 2, M, 64])
        W = sb("W", [128, 4, M, 64])
        fy, fx, ix, iy = sb("fy", [128, 96], F16), sb("fx", [128, 96], F16), sb("ix", [128, 128]), sb("iy", [128, 256])
        ident, avg = sb("ident", [128, 128]), sb("avg", [128, 128])
        lps = sb("lps", [128, 131])
        st = sb("st", [128, G * 8 * 6])
        sm = sb("sm", [128, 24])
        qs = sb("qs", [128, 8])
        agg, mv, dif, sq, var, sd, r0, r2, t1, rs, mw, ms, scale, shift, qbias = (
            sm[:, 0:2], sm[:, 2:4], sm[:, 4:5], sm[:, 5:6], sm[:, 6:7], sm[:, 7:8], sm[:, 8:9], sm[:, 9:10],
            sm[:, 10:11], sm[:, 11:12], sm[:, 12:13], sm[:, 13:14], sm[:, 14:15], sm[:, 15:16], sm[:, 16:17])
        ones = sm[:, 18:19]
        wblk, wb, gamma, beta = lps[:, 0:128], lps[:, 128:129], lps[:, 129:130], lps[:, 130:131]

        xts = phase[0:SY, 4608:6656]
        hat = phase[0:16, 0:B * M * M]
        Gy = S[:, 0, 0:384].rearrange("p (r m) -> p r m", r=2)
        Gx = st[0:8 * M, 0:192]
        fx2, pT, pb, fy1 = S[:, 1, 0:192].rearrange("p (r n) -> p r n", r=2), S[:, 1, 192:320], S[0:16, 1, 320:448], S[0:SY, 1, 448:472]

        u_row = v[0:1, 0:NW]
        e2T = v[:, 0:NW // 2].bitcast(F16)
        xa = v[:, NW:3 * NW].rearrange("p (h n) -> p h n", h=2)
        rB, cB = v[:, 3 * NW:4 * NW], v[:, 4 * NW:5 * NW]
        spare = v[:, 5 * NW:]
        es = spare[:, 0:384].rearrange("p (s n) -> p s n", s=2)
        eTs = spare[0:D, 384:1152].rearrange("p (s n) -> p s n", s=2)
        Vs = spare[:, 1152:1536].rearrange("p (s n) -> p s n", s=2)
        Ai = spare[:, 1536:1920].rearrange("p (s n) -> p s n", s=2)
        At = S[:, 0, :].rearrange("p (s n) -> p s n", s=2)
        xs = Xr[:, 3072:4608].rearrange("p (s h n) -> p s h n", s=2, h=2)
        ys = cB[:, 0:1536].rearrange("p (s h n) -> p s h n", s=2, h=2)
        tok = lambda a: a.rearrange("p (k d) -> p k d", d=D)
        h_all = tok(Xr[:, 0:3072])
        eb, vb, tmp, tmp2 = tok(phase[:, 0:3072]), tok(phase[:, 3072:6144]), tok(W[:, :, :, :].rearrange("p a b c -> p (a b c)")), tok(rB[:, 0:3072])
        dx, dy = S[0:D, 1, 0:N], S[0:D, 1, N:2 * N]
        XBr = XB[:, :, :, :].rearrange("p a b c -> p (a b c)")
        W2f = XBr[:, 0:1152]
        ET = XBr[:, 1152:1280].rearrange("p (h d) -> p h d", h=2)
        Wr = XBr[:, 1280:1288]
        B1 = XBr[:, 1288:1306]
        B2 = Yr[:, 0:576]
        Di, Dt, rank = Yr[:, 576:768], Yr[:, 768:896], XBr[:, 1306:1314]
        U, k1, k2, z, rsum, csum = (Yr[0:B, 896 + i * T:896 + (i + 1) * T] for i in range(6))
        Wf = W[:, :, :, :].rearrange("p a b c -> p (a b c)")
        W1 = Wf[:, 0:2304]
        W1h, W1l = (v[:, 3072 + 1152 * i:4224 + 1152 * i].bitcast(F16) for i in range(2))
        W2h, W2l = v[:, 5376:5952].bitcast(F16), Wf[:, 2304:2880].bitcast(F16)
        Wrh, Wrl, ident16 = (Wf[:, a:b].bitcast(F16) for a, b in ((2880, 2884), (2884, 2888), (2888, 2952)))
        W2hv, W2lv = (a.rearrange("p (f e d) -> p f e d", f=2, e=E + 1) for a in (W2h, W2l))
        lns = Xr[:, 3840:4272]
        lg, lz, ex, rw, eq, cd, oh1, rw2, oh2, mask = (
            cB[:, 2048 + 384 * i:2432 + 384 * i].rearrange("p (k e) -> p k e", e=E) for i in range(10))
        rr = rB[:, 4608:5184].rearrange("p (i k) -> p i k", k=NT)
        ehl = rB[:, 0:3072].bitcast(F16).rearrange("p (k h d) -> p k h d", h=2, d=D)
        hid = v[:, NW:NW + 3072].rearrange("p (s n) -> p s n", s=3)
        hh, hl = (v[:, NW + 3072 + 1536 * i:NW + 4608 + 1536 * i].bitcast(F16).rearrange("p (s n) -> p s n", s=3) for i in range(2))
        tb = rB[:, 3648:5696].rearrange("p (t e d) -> p t e d", t=CH, e=E)
        rt = Xr[:, 3072:3328].rearrange("p (t d) -> p t d", d=D)
        s1 = Xr[:, 3328:3584].rearrange("p (t d) -> p t d", d=D)
        s2 = Xr[:, 3584:3840].rearrange("p (t d) -> p t d", d=D)

        ps = ctx.enter_context(nc.psum_tensor("ps", [128, 8, 512], F32))
        TP, FP, T2P, F2P = (0, 1), (2, 3), (4, 5), (6, 7)
        IP, ZP, OP = (0, 1), (2, 3), (4, 5, 6, 7)

        consts, primed, zeroed, carried = (sem(n) for n in ("consts", "primed", "zeroed", "carried"))
        v_in, xt_in, v_zero, xy_done, xye_done, xx_done, xxe_done = (sem(n) for n in (
            "v_in", "xt_in", "v_zero", "xy_done", "xye_done", "xx_done", "xxe_done"))
        hat_in, x0_done, x0e_done, fold_done, folded = (sem(n) for n in (
            "hat_in", "x0_done", "x0e_done", "fold_done", "folded"))
        relu_done, t1_done, sh_split, sl_split, f1_done, f1e_done = (sem(n) for n in (
            "relu_done", "t1_done", "sh_split", "sl_split", "f1_done", "f1e_done"))
        t2_done, t2h_done, t2l_done, f2_done, f2e_done = (sem(n) for n in (
            "t2_done", "t2h_done", "t2l_done", "f2_done", "f2e_done"))
        v_stored = [sem(f"v_stored{r}") for r in range(4)]
        x_stored = [sem(f"x_stored{s}") for s in range(2)]
        w_loaded = [sem(f"w_loaded{s}") for s in range(4)]
        w_neg, xb0_done, xb1_done, mix_done, y_done, yt_done = (sem(n) for n in (
            "w_neg", "xb0_done", "xb1_done", "mix_done", "y_done", "yt_done"))
        hg_done, i1_done, i1e_done, t4_done, ze_done = (sem(n) for n in (
            "hg_done", "i1_done", "i1e_done", "t4_done", "ze_done"))
        fin_done, oe_done, bs_done = sem("fin_done"), sem("oe_done"), sem("bs_done")
        lp_loaded, dch, sm_done, sq_done = sem("lp_loaded"), sem("dch"), sem("sm_done"), sem("sq_done")
        qs_done, qt_done, qb_done, h_mm, h_done = (sem(n) for n in ("qs_done", "qt_done", "qb_done", "h_mm", "h_done"))
        h_stored = [sem(f"h_stored{s}") for s in range(2)]
        txt_in, out_st = sem("txt_in"), sem("out_st")
        h_in, out_st2 = sem("h_in"), sem("out_st2")
        es_done, tr_done, eT_done, u_done, wv_done, us_done, ur_done = (sem(n) for n in (
            "es_done", "tr_done", "eT_done", "u_done", "wv_done", "us_done", "ur_done"))
        xs_done, vs_done, sc_done, am_done, a_done, at_done = (sem(n) for n in (
            "xs_done", "vs_done", "sc_done", "am_done", "a_done", "at_done"))
        as_done, tr2_done, aT_done, yc_done, ym_done, vo_done, ve_done = (sem(n) for n in (
            "as_done", "tr2_done", "aT_done", "yc_done", "ym_done", "vo_done", "ve_done"))
        tr3_done, e2T_done, rt_done, lg_done = (sem(n) for n in ("tr3_done", "e2T_done", "rt_done", "lg_done"))
        split, hh_done, hl_done = sem("split"), sem("hh_done"), sem("hl_done")
        hm_done, gelu_done, w2_done, p_done, m_done, r_done, sh_done, f_done = (sem(n) for n in (
            "hm_done", "gelu_done", "w2_done", "p_done", "m_done", "r_done", "sh_done", "f_done"))
        ones_done, s2_done = sem("ones_done"), sem("s2_done")
        late, w1_in, twoin = sem("late"), sem("w1_in"), sem("twoin")
        tok_ready, steps, sqrt_done, exp_done = sem("tok_ready"), sem("steps"), sem("sqrt_done"), sem("exp_done")
        u_moved, rc_out, r_in, c_in = sem("u_moved"), sem("rc_out"), sem("r_in"), sem("c_in")
        STEPS = 13
        STEP_E = 12
        STEP_RC = STEP_E + 10
        STEP_V = STEP_RC + 12
        STEP_X = STEP_V + 4
        STEP_A = STEP_X + 12
        STEP_VS = STEP_A + 12
        STEP_H = STEP_VS + 1 + 12
        STEP_S = STEP_H + 2
        STEP_L = STEP_S + 2
        STEP_M = STEP_L + 19
        NCONST = 12

        block = ctx.enter_context(nc.Block())

        def groups(eng, body):
            settle(eng)
            with eng.Fori(0, G // 2) as i:
                for s in range(2):
                    body(2 * i + s, s, i)

        def skewed(eng, body):
            body(0, 0, True, False, True)
            settle(eng)
            with eng.Fori(0, G // 2 - 1) as i:
                for s in (1, 0):
                    body(2 * i + 2 - s, s, True, True, True)
            body(G - 1, 1, True, True, False)
            body(G, 0, False, True, False)

        def settle(eng):
            eng.sem_inc(carried, 1)

        def layers(eng, first, step):
            first()
            settle(eng)
            with eng.Fori(0, L - 1) as l:
                step(l, False)
            step(L - 1, True)

        @block.sync
        def _(sp):
            sp.dma_start(xts, xt).then_inc(xt_in, 16)
            for dst, src in ((fy1, tables[4]), (fx2, tables[5].rearrange("p (r n) -> p r n", r=2)), (pT, pint), (pb, pblk),
                             (fy[:, :], tables[0]), (fx[:, :], tables[1]), (ix[:, :], tables[2]), (iy[:, :], tables[3]),
                             (ident[:, :], tables[7]), (avg[:, :], tables[8]), (qs[:, 0:4], qblk), (qbias[0:4, :], qb)):
                sp.dma_start(dst, src).then_inc(consts, 16)
            sp.dma_start(hat[4:16].rearrange("p (b n) -> p b n", b=B),
                         tables[6].unsqueeze(1).broadcast_to([12, B, M * M])).then_inc(hat_in, 16)
            sp.dma_start(lps[:, :], lp[0]).then_inc(lp_loaded, 16)
            sp.wait_ge(v_zero, 2)
            sp.dma_start(v[0:Q, :].rearrange("q (g n) -> q g n", g=G), x.rearrange("(g q) n -> q g n", q=Q)).then_inc(v_in, 16)
            sp.dma_start(v[Q:Q + 3, :].rearrange("q (g n) -> q g n", g=G), grid).then_inc(v_in, 16)
            sp.wait_ge(primed, 4)

            def weights(l, kys):
                for ky in kys:
                    sp.wait_ge(mix_done, (l * 6 + ky // 2) * 2 + 2)
                    sp.dma_start(W[:, ky % 4], fw[ky, :, bass.ds(l, 1)].rearrange("p l m n -> p (l m) n")).then_inc(w_loaded[ky % 4], 16)

            def first():
                weights(0, range(4))
                sp.wait_ge(xxe_done, 1)
                for part in range(4):
                    for two in range(2):
                        for image in range(2):
                            b0 = image * NJ + two * 8
                            o = two * 96 + image * 48 + part * M
                            sp.dma_start(hat[part:part + 1, b0 * M * M:(b0 + 8) * M * M].rearrange("p (n m) -> p n m", m=M),
                                         Gx[:, o:o + M]).then_inc(hat_in, 16)
                weights(0, range(4, M))

            def phase_a(a):
                weights(a + 1, range(4))

                def store(g, r):
                    sp.wait_ge(relu_done, (a * G + g) * 4 + r + 1)
                    sp.dma_start(v[:, bass.ds(g * NPOS + r * 1024, 1024)],
                                 R[:, r * 1024:(r + 1) * 1024]).then_inc(v_stored[r], 16)

                def group(g, s, now, before, after):
                    if now:
                        for r in range(4):
                            store(g, r)
                    if before:
                        sp.wait_ge(f2e_done, 2 + (a * G + g) * 2)
                        for q in range(Q):
                            for h in range(4):
                                sp.dma_start(X[32 * h:32 * h + 32, bass.ds((g - 1) * Q + q, 1)].rearrange("p b k m -> p (b k m)"),
                                             F2o[32 * q:32 * q + 32, 1 - s, h].rearrange("p k m -> p (k m)")
                                             ).then_inc(x_stored[1 - s], 16)
                skewed(sp, group)
                weights(a + 1, range(4, M))

            def params(l):
                sp.dma_start(lps[:, :], lp[bass.ds(l, 1)].rearrange("l p n -> (l p) n")).then_inc(lp_loaded, 16)

            def step(l, last):
                if not last:
                    sp.wait_ge(dch, (l + 1) * STEPS)
                    params(l + 1)
                    phase_a(l)
            layers(sp, first, step)

            def tokens(g, s, i):
                for hf in range(2):
                    sp.wait_ge(h_done, 4 + g * 8 + hf * 4 + 4)
                    for q in range(Q):
                        p0 = (q % 2) * 64 + 32 * hf
                        sp.dma_start(hbuf[p0:p0 + 32, bass.ds(2 * g + q // 2, 1), 0].rearrange("p j d -> p (j d)"),
                                     phase[q:q + 1, hf * 2048:(hf + 1) * 2048].rearrange("p (x y) -> p x y", y=D)
                                     ).then_inc(h_stored[hf], 16)
            sp.wait_ge(fin_done, 4 + L * 64)
            for two in range(2):
                sp.dma_start(hbuf[:, :, 1 + two], txt.rearrange("(j b) t d -> b t j d", b=2)[two]).then_inc(txt_in, 16)
            groups(sp, tokens)
            for dst, src in ((dx, dxy[:, 0:N]), (dy, dxy[:, N:2 * N]), (Di, att[:, 0:T]), (Dt, att[:, T:T + TXT]),
                             (rank, att[:, T + TXT:]), (ET, et), (Wr[0:D], wr), (Wr[D:2 * D], wr), (B1, b1), (W2f.rearrange("p (f e d) -> p f e d", f=2, e=E + 1), w2), (B2, b2)):
                sp.dma_start(dst, src).then_inc(late, 16)
            sp.wait_ge(ur_done, 2 + NJ)
            sp.dma_start(U, u_row).then_inc(u_moved, 16)
            sp.wait_ge(steps, STEP_RC)
            sp.dma_start(rdram[0].rearrange("(b t) -> b t", b=B), rsum).then_inc(rc_out, 16)
            sp.dma_start(rdram[1].rearrange("(b t) -> b t", b=B), csum).then_inc(rc_out, 16)
            sp.wait_ge(rc_out, 32)
            sp.dma_start(cB, rdram[1:2, :].partition_broadcast(128)).then_inc(c_in, 16)
            sp.dma_start(rB, rdram[0:1, :].partition_broadcast(128)).then_inc(r_in, 16)
            sp.wait_ge(steps, STEP_V)
            for two in range(2):
                sp.dma_start(W1[D * two:D * two + D], w1).then_inc(w1_in, 16)
            o = out.rearrange("(j b) t d -> b t j d", b=2)
            for j0, j1 in ((0, NJ // 2), (NJ // 2, NJ)):
                sp.wait_ge(f_done, j1 * 3 // CH)
                for two in range(2):
                    sp.dma_start(o[two, 0:SX, j0:j1], hbuf[64 * two:64 * two + 64, j0:j1, 0]).then_inc(out_st, 16)
                    sp.dma_start(o[two, SX:T, j0:j1], hbuf[:, j0:j1, 1 + two]).then_inc(out_st, 16)
            sp.wait_ge(out_st, 128)

        @block.gpsimd
        def _(pool):
            pool.memset(v[:, 0:G * NPOS // 4], 0.0).then_inc(v_zero, 1)
            pool.memset(XB[:, :, :, :], 0.0).then_inc(zeroed, 1)
            pool.memset(Yr[:, :], 0.0).then_inc(zeroed, 1)
            for s in range(2):
                pool.sem_inc(x_stored[s], 256)
                pool.sem_inc(h_stored[s], 16)
            for r in range(4):
                pool.sem_inc(v_stored[r], 16)
            pool.sem_inc(hl_done, 3)
            pool.sem_inc(primed, 1)
            pool.wait_ge(primed, 4)

            def mix(l):
                for s in range(2):
                    pool.wait_ge(x_stored[s], 256 * l * 4 + 256)
                for ky in range(M):
                    pool.wait_ge(w_loaded[ky % 4], (l * 3 + ky // 4 + 1) * 16)
                    settle(pool)
                    for h in range(2):
                        settle(pool)
                        wi = W[64 * h + 32:64 * h + 64, ky % 4, :, 0:32]
                        pool.tensor_scalar(wi, wi, -1.0, None, ALU.mult).then_inc(w_neg, 1)
                        pool.wait_ge(w_neg, (l * M + ky) * 2 + h + 1)
                    pool.wait_ge(mix_done, (l * 6 + ky // 2) * 2 + 4)
                    settle(pool)
                    pool.tensor_copy(XB[0:64, ky % 2, :, 0:32], X[0:64, :, ky].rearrange("p b m -> p m b")).then_inc(xb0_done, 1)
                    pool.wait_ge(xb0_done, l * M + ky + 1)

            def phase_b(l):
                pool.wait_ge(yt_done, 2 + (l + 1) * 6)

                def group(g, s, i):
                    pool.wait_ge(i1_done, (l * G + g) * 4 + 4)
                    settle(pool)
                    pool.tensor_copy(Hg[:, s].rearrange("p k (q o) -> p k q o", q=Q),
                                     H[:, :, :, bass.ds(g * Q, Q)].rearrange("p k o q -> p k q o")).then_inc(hg_done, 1)
                    pool.wait_ge(hg_done, l * G + g + 1)
                groups(pool, group)

            def step(l, last):
                mix(l)
                phase_b(l)
            pool.wait_ge(zeroed, 2)
            layers(pool, lambda: pool.wait_ge(x0e_done, 9), step)
            pool.wait_ge(steps, STEP_V)
            with pool.Fori(0, NJ // 2) as i:
                for s in range(2):
                    j = 2 * i + s
                    pool.wait_ge(a_done, j + 1)
                    settle(pool)
                    pool.tensor_copy(Vs[:, s], phase[:, bass.ds(3072 + j * 192, 192)]).then_inc(vs_done, 1)
                    pool.wait_ge(vs_done, j + 1)
            pool.wait_ge(w1_in, 32)
            pool.wait_ge(late, 176)
            n_split = [0]

            def part(ins):
                n_split[0] += 1
                ins.then_inc(split, 1)
                pool.wait_ge(split, n_split[0])
            part(pool.tensor_copy(ident16, ident[:, :]))
            for full, high, low, factor, rows in ((Wr, Wrh, Wrl, RS, D), (W1, W1h, W1l, WS, D), (W2f, W2h, W2l, WS, 128)):
                part(pool.tensor_scalar(full, full, factor, None, ALU.mult))
                part(pool.tensor_copy(high, full))
                part(pool.tensor_tensor(low[0:rows], full[0:rows], high[0:rows], ALU.subtract))
                if rows == D:
                    part(pool.memset(low[D:128], 0.0))
            assert n_split[0] == 12

            def chunk(k):
                for e in range(E + 1):
                    pool.wait_ge(w2_done, k * 9 + e + 1)
                    pool.wait_ge(hh_done, 3 + k * 9 + e + 1)
                    settle(pool)
                    pool.tensor_tensor(hl[:, e % 3], hid[:, e % 3], hh[:, e % 3], ALU.subtract).then_inc(hl_done, 1)
                    pool.wait_ge(hl_done, 3 + k * 9 + e + 1)
            settle(pool)
            with pool.Fori(0, NC) as k:
                chunk(k)

        @block.tensor
        def _(pe):
            pe.sem_inc(t1_done, 8)
            pe.sem_inc(f1_done, 2)
            pe.sem_inc(t2_done, 2)
            pe.sem_inc(f2_done, 2)
            pe.sem_inc(mix_done, 4)
            pe.sem_inc(i1_done, 8)
            pe.sem_inc(t4_done, 8)
            pe.sem_inc(fin_done, 4)
            for sm_, n in ((tr_done, 2), (u_done, 4), (sc_done, 2), (a_done, 2), (tr2_done, 2), (yc_done, 4),
                           (vo_done, 2), (tr3_done, 2), (rt_done, 2), (w2_done, 3)):
                pe.sem_inc(sm_, n)
            pe.sem_inc(primed, 1)
            pe.wait_ge(primed, 4)
            pe.wait_ge(consts, 16 * NCONST)
            pe.wait_ge(xt_in, 16)

            def first():
                for p in range(NJ):
                    mm = pe.matmul(ps[:, 0, KR * p:KR * p + KR], xts[:, 128 * p:128 * p + 128], fy1, start=True, stop=True)
                mm.then_inc(xy_done, 1)
                pe.wait_ge(lp_loaded, 16)
                pe.matmul(ps[:, 2, 0:128], pT, wblk, start=True, stop=True).then_inc(fold_done, 1)
                pe.wait_ge(xye_done, 1)
                for two in range(2):
                    for ri in range(2):
                        mm = pe.matmul(ps[0:96, 1, 192 * two:192 * two + 96], Gy[:, ri, 96 * two:96 * two + 96], fx2[:, ri],
                                       start=ri == 0, stop=ri == 1)
                mm.then_inc(xx_done, 1)
                pe.wait_ge(hat_in, 17 * 16)
                for c in range(9):
                    if c >= 5:
                        pe.wait_ge(x0e_done, c - 4)
                    pe.matmul(ps[:, 3 + c % 5, :], pb, hat[:, 512 * c:512 * c + 512], start=True, stop=True).then_inc(x0_done, 1)
                pe.wait_ge(v_in, 32)
                pe.wait_ge(folded, 1)
                pe.wait_ge(x0e_done, 9)

            def phase_a(a):
                def group(g, s, now, before, after):
                    ga = a * G + g

                    def turn(c):
                        if c % 2 == 0:
                            pe.wait_ge(relu_done, ga * 4 + c // 2 + 1)
                        pe.wait_ge(sl_split, ga * 8 + c + 1)
                        for j in range(4):
                            mm = pe.transpose(ps[:, TP[c % 2], 128 * j:128 * j + 128],
                                              R[:, 512 * c + 128 * j:512 * c + 128 * j + 128], ident[:, :])
                        mm.then_inc(t1_done, 1)

                    def ydft(c):
                        pe.wait_ge(sl_split, ga * 8 + c + 3)
                        if c % 2 == 0:
                            pe.wait_ge(f1e_done, ga * 4 + c // 2 + 1)
                        for j in range(4):
                            o, rows = (c % 2) * 192 + 48 * j, slice(128 * j, 128 * j + 128)
                            out1 = ps[:, FP[(c // 2) % 2], o:o + 48]
                            pe.matmul(out1, Sh[:, c % 2, rows], fy[:, 0:48], start=True, stop=False)
                            pe.matmul(out1, Sh[:, c % 2, rows], fy[:, 48:96], start=False, stop=False)
                            mm = pe.matmul(out1, Sl[:, c % 2, rows], fy[:, 0:48], start=False, stop=True)
                        mm.then_inc(f1_done, 1)

                    gb, sb_ = ga - 1, 1 - s

                    def turn2(k):
                        if k == 0:
                            pe.wait_ge(f1e_done, 2 + gb * 4 + 4)
                        pe.wait_ge(t2l_done, gb * 3 + k + 1)
                        for j in range(4):
                            ky = 4 * k + j
                            mm = pe.transpose(ps[:, T2P[(sb_ * 3 + k) % 2], 128 * j:128 * j + 128],
                                              F1o[:, 2 * ky:2 * ky + 2].rearrange("p k x -> p (k x)"), ident[:, :])
                        mm.then_inc(t2_done, 1)

                    def xdft(k):
                        pe.wait_ge(t2l_done, 2 + gb * 3 + k + 1)
                        slot = (sb_ * 3 + k) % 2
                        for j in range(4):
                            ky, rows = 4 * k + j, slice(128 * j, 128 * j + 128)
                            if ky % 6 == 0:
                                pe.wait_ge(f2e_done, gb * 2 + ky // 6 + 1)
                            out2 = ps[:, F2P[ky // 6], 48 * (ky % 6):48 * (ky % 6) + 48]
                            pe.matmul(out2, T2h[:, slot, rows], fx[:, 0:48], start=True, stop=False)
                            pe.matmul(out2, T2h[:, slot, rows], fx[:, 48:96], start=False, stop=False)
                            mm = pe.matmul(out2, T2l[:, slot, rows], fx[:, 0:48], start=False, stop=True)
                        mm.then_inc(f2_done, 1)

                    for c in range(9):
                        if now and c < 8:
                            turn(c)
                        if now and c > 0:
                            ydft(c - 1)
                        if before and 2 <= c < 5:
                            xdft(c - 2)
                        if before and c < 3:
                            turn2(c)
                skewed(pe, group)

            def mix(l):
                for p in range(6):
                    pg = l * 6 + p
                    pe.wait_ge(w_neg, (l * M + 2 * p + 2) * 2)
                    pe.wait_ge(xb0_done, l * M + 2 * p + 2)
                    pe.wait_ge(xb1_done, l * M + 2 * p + 2)
                    for h in range(2):
                        pe.wait_ge(y_done, pg * 2 + h + 1)
                        for m in range(6):
                            kx = 6 * h + m
                            for par in range(2):
                                mm = pe.matmul(ps[64 * par:64 * par + 64, (p % 2) * 2 + h, 64 * m:64 * m + 64],
                                               XB[:, par, kx], W[:, (2 * p + par) % 4, kx],
                                               start=True, stop=True)
                        mm.then_inc(mix_done, 1)

            def phase_b(l):
                for r in range(4):
                    pe.wait_ge(v_stored[r], 16 * G * l + 16)
                pe.wait_ge(lp_loaded, 16 * (l + 1))

                def group(g, s, i):
                    gb = l * G + g
                    pe.wait_ge(hg_done, gb + 1)
                    for u in range(4):
                        par = u % 2
                        pe.wait_ge(i1e_done, gb * 4 + u + 1)
                        for j in range(3):
                            kh = 3 * (u // 2) + j
                            mm = pe.matmul(ps[:, IP[par], 128 * j:128 * j + 128],
                                           Hg[64 * par:64 * par + 64, s, kh], ix[64 * par:64 * par + 64, :],
                                           start=True, stop=True)
                        mm.then_inc(i1_done, 1)

                    def turn(z):
                        if z == 0:
                            pe.wait_ge(i1e_done, 2 + gb * 4 + 4)
                        pe.wait_ge(ze_done, gb * 4 + z + 1)
                        for j in range(4):
                            x0 = 16 * z + 4 * j
                            mm = pe.transpose(ps[:, ZP[z % 2], 128 * j:128 * j + 128],
                                              I1o[:, s, x0:x0 + 4].rearrange("p x k -> p (x k)"), ident[:, :])
                        mm.then_inc(t4_done, 1)

                    def add(c):
                        cf = gb * 8 + c
                        pe.wait_ge(ze_done, 2 + gb * 4 + c // 2 + 1)
                        pe.wait_ge(oe_done, cf + 1)
                        pe.matmul(ps[:, OP[c % 4], :], wblk, v[:, bass.ds(g * NPOS + c * 512, 512)],
                                  start=True, stop=False, skip_group_check=True)
                        for j in range(2):
                            z0 = (c % 2) * 256 + 128 * j
                            mm = pe.matmul(ps[:, OP[c % 4], 256 * j:256 * j + 256], S[:, (c // 2) % 2, z0:z0 + 128],
                                           iy[:, :], start=False, stop=True, skip_group_check=True)
                        mm.then_inc(fin_done, 1)
                    turn(0)
                    turn(1)
                    add(0)
                    add(1)
                    turn(2)
                    add(2)
                    add(3)
                    turn(3)
                    for c in range(4, 8):
                        add(c)
                groups(pe, group)
                pe.wait_ge(dch, l * STEPS + 1)
                pe.matmul(ps[:, 0, 0:2], avg[:, :], agg, start=True, stop=True).then_inc(sm_done, 1)
                pe.wait_ge(dch, l * STEPS + 4)
                pe.matmul(ps[:, 1, 0:1], avg[:, :], sq, start=True, stop=True).then_inc(sm_done, 1)

            def step(l, last):
                mix(l)
                phase_b(l)
                if not last:
                    phase_a(l)
            layers(pe, first, step)
            pe.wait_ge(dch, L * STEPS)
            pe.matmul(ps[0:4, 0, 0:1], qs[:, 0:4], shift, start=True, stop=True).then_inc(qt_done, 1)
            pe.wait_ge(qs_done, 1)

            def tokens(g, s, i):
                for c in range(8):
                    pe.wait_ge(h_done, g * 8 + c + 1)
                    pe.matmul(ps[0:4, OP[c % 4], :], qs[:, 4:8], v[:, bass.ds(g * NPOS + c * 512, 512)],
                              start=True, stop=True).then_inc(h_mm, 1)
            groups(pe, tokens)

            def pairs(*stages):
                with pe.Fori(0, NJ // 2) as i:
                    for stage in stages:
                        for s in range(2):
                            stage(2 * i + s, s)

            def turn3(dst, src):
                settle(pe)
                for t in range(3):
                    mm = pe.transpose(dst[0:D, 128 * t:128 * t + 128], src[:, 64 * t:64 * t + 64], ident[:, :])
                return mm

            pe.wait_ge(ones_done, 1)
            pe.wait_ge(late, 176)

            def turn_e(j, s):
                pe.wait_ge(es_done, j + 1)
                pe.wait_ge(eT_done, 2 * j + 2)
                turn3(ps[:, s, :], es[:, s]).then_inc(tr_done, 1)

            def u_mm(j, s):
                pe.wait_ge(eT_done, 4 + 2 * j + 2)
                pe.wait_ge(wv_done, 2 * j + 2)
                for nh in range(2):
                    pe.matmul(ps[:, 2 + 2 * s + nh, 0:384], dx[:, 128 * nh:128 * nh + 128], eTs[:, s],
                              start=True, stop=True).then_inc(u_done, 1)

            def u_sum(j, s):
                pe.wait_ge(wv_done, 4 + 2 * j + 2)
                pe.wait_ge(ur_done, j + 1)
                for nh in range(2):
                    mm = pe.matmul(ps[0:1, 6 + s, 0:384], ones, xa[:, nh, bass.ds(j * 384, 384)],
                                   start=nh == 0, stop=nh == 1)
                mm.then_inc(us_done, 1)
            pairs(turn_e, u_mm, u_sum)

            def scores(j, s):
                pe.wait_ge(xs_done, j + 1)
                pe.wait_ge(am_done, 2 * j + 2)
                for two in range(2):
                    o = two * T
                    for nh in range(2):
                        pe.matmul(ps[64 * two:64 * two + 64, s, 0:T], xs[:, s, nh, o:o + SX], xs[:, s, nh, o:o + T],
                                  start=nh == 0, stop=nh == 1)
                    for nh in range(2):
                        mm = pe.matmul(ps[:, 2 + s, 128 * two:128 * two + 128], xs[:, s, nh, o + SX:o + T],
                                       xs[:, s, nh, o + SX:o + T], start=nh == 0, stop=nh == 1)
                mm.then_inc(sc_done, 1)

            def values(j, s):
                pe.wait_ge(am_done, 4 + 2 * j + 2)
                pe.wait_ge(vs_done, j + 1)
                pe.wait_ge(at_done, 3 * j + 3)
                settle(pe)
                for two in range(2):
                    bank, h = 4 + 2 * s + two, slice(64 * two, 64 * two + 64)
                    pe.matmul(ps[h, bank, 0:64], Ai[h, s, 0:SX], Vs[h, s, 0:D], start=True, stop=True)
                    pe.matmul(ps[:, bank, 64:128], Ai[h, s, SX:T], Vs[h, s, 0:D], start=True, stop=False)
                    mm = pe.matmul(ps[:, bank, 64:128], At[:, s, 128 * two:128 * two + 128],
                                   Vs[:, s, D * (1 + two):D * (2 + two)], start=False, stop=True)
                mm.then_inc(a_done, 1)
            pairs(scores, values)

            def turn_a(j, s):
                pe.wait_ge(as_done, j + 1)
                pe.wait_ge(aT_done, 2 * j + 2)
                turn3(ps[:, s, :], es[:, s]).then_inc(tr2_done, 1)

            def y_mm(j, s):
                pe.wait_ge(aT_done, 4 + 2 * j + 2)
                pe.wait_ge(ym_done, 2 * j + 2)
                for nh in range(2):
                    pe.matmul(ps[:, 2 + 2 * s + nh, 0:384], dy[:, 128 * nh:128 * nh + 128], eTs[:, s],
                              start=True, stop=True).then_inc(yc_done, 1)

            def e_mm(j, s):
                pe.wait_ge(ym_done, 4 + 2 * j + 2)
                pe.wait_ge(ve_done, j + 1)
                for two in range(2):
                    h, o = slice(64 * two, 64 * two + 64), two * T
                    for nh in range(2):
                        pe.matmul(ps[h, 6 + s, 0:D], ys[:, s, nh, o:o + SX], ET[:, nh], start=nh == 0, stop=nh == 1)
                for two in range(2):
                    o = two * T
                    for nh in range(2):
                        mm = pe.matmul(ps[:, 6 + s, D * (1 + two):D * (2 + two)], ys[:, s, nh, o + SX:o + T], ET[:, nh],
                                       start=nh == 0, stop=nh == 1)
                mm.then_inc(vo_done, 1)
            pairs(turn_a, y_mm, e_mm)

            def chunks(*stages):
                with pe.Fori(0, NT // CH // 2) as i:
                    for stage in stages:
                        for s in range(2):
                            stage(2 * i + s, s)

            def turn_h(k, s):
                pe.wait_ge(e2T_done, k + 1)
                settle(pe)
                o = ps[:, s, 0:256].bitcast(F16)
                for t in range(CH):
                    mm = pe.transpose(o[:, 128 * t:128 * t + 128], rB[:, bass.ds((k * CH + t) * 64, 64)].bitcast(F16), ident16)
                mm.then_inc(tr3_done, 1)

            def route(k, s):
                pe.wait_ge(e2T_done, 2 + k + 1)
                pe.wait_ge(lg_done, k + 1)
                settle(pe)
                for t in range(CH):
                    for w in (Wrh, Wrl):
                        mm = pe.matmul(ps[:, 2 + s, E * t:E * t + E], v[:, bass.ds((k * CH + t) * 64, 64)].bitcast(F16), w,
                                       start=w is Wrh, stop=w is Wrl)
                mm.then_inc(rt_done, 1)
            pe.wait_ge(split, 12)
            pe.wait_ge(steps, STEP_S)
            chunks(turn_h, route)

            pe.wait_ge(lg_done, 2 + NC)

            def up(k, e):
                for fh in range(2):
                    n = 2 * e + fh
                    pe.wait_ge(gelu_done, k * 18 + n + 1)
                    settle(pe)
                    for w in (W1h, W1l):
                        mm = pe.matmul(ps[:, n % 3, :], w[:, 256 * e + 128 * fh:256 * e + 128 * fh + 128],
                                       v[:, bass.ds(k * 256, 256)].bitcast(F16), start=w is W1h, stop=w is W1l)
                    mm.then_inc(hm_done, 1)

            def down(k, e):
                pe.wait_ge(hl_done, 3 + k * 9 + e + 1)
                if e == E:
                    pe.wait_ge(sh_done, k + 1)
                for t in range(CH):
                    if e == 0:
                        pe.wait_ge(p_done, 4 * k + t + 1)
                    o = ps[:, 4 + t, D * e:D * e + D] if e < E else ps[:, 3, D * t:D * t + D]
                    for fh in range(2):
                        a = slice(512 * fh + 128 * t, 512 * fh + 128 * t + 128)
                        pe.matmul(o, hh[:, e % 3, a], W2hv[:, fh, e], start=fh == 0, stop=False)
                        pe.matmul(o, hh[:, e % 3, a], W2lv[:, fh, e], start=False, stop=False)
                        mm = pe.matmul(o, hl[:, e % 3, a], W2hv[:, fh, e], start=False, stop=fh == 1)
                mm.then_inc(w2_done, 1)

            def experts(k, last=False):
                for e in range(E + 1):
                    if e + 2 <= E:
                        up(k, e + 2)
                    elif not last:
                        up(k + 1, e + 2 - (E + 1))
                    down(k, e)
            up(0, 0)
            up(0, 1)
            with pe.Fori(0, NC - 1) as k:
                experts(k)
            experts(NC - 1, True)

        @block.scalar
        def _(act):
            act.sem_inc(f2e_done, 2)
            act.sem_inc(y_done, 4)
            act.sem_inc(ze_done, 2)
            act.sem_inc(oe_done, 4)
            act.sem_inc(h_done, 4)
            for sm_, n in ((wv_done, 4), (at_done, 6), (ve_done, 2), (gelu_done, 3)):
                act.sem_inc(sm_, n)
            act.sem_inc(primed, 1)
            act.wait_ge(primed, 4)

            def first():
                act.wait_ge(xy_done, 1)
                act.activation(Gy, ps[:, 0, 0:384].rearrange("p (m r) -> p r m", r=2), ACT.Copy).then_inc(xye_done, 1)
                act.wait_ge(fold_done, 1)
                act.activation(wblk, ps[:, 2, 0:128], ACT.Copy).then_inc(folded, 1)
                act.wait_ge(xx_done, 1)
                act.activation(Gx.rearrange("p (a n) -> p a n", a=2),
                               ps[0:96, 1, 0:384].rearrange("p (a n) -> p a n", a=2)[:, :, 0:96], ACT.Copy).then_inc(xxe_done, 1)
                for c in range(9):
                    act.wait_ge(x0_done, c + 1)
                    act.activation(Xr[:, 512 * c:512 * c + 512], ps[:, 3 + c % 5, :], ACT.Copy).then_inc(x0e_done, 1)

            def phase_a(a):
                def relu(g, r):
                    ga = a * G + g
                    act.wait_ge(t1_done, ga * 8 + 2 * r + 2)
                    act.wait_ge(v_stored[r], 16 * ga + 16)
                    act.activation(R[:, r * 1024:(r + 1) * 1024], v[:, bass.ds(g * NPOS + r * 1024, 1024)], ACT.Relu,
                                   bias=shift, scale=scale).then_inc(relu_done, 1)

                def group(g, s, now, before, after):
                    ga = a * G + g
                    gb, sb_ = ga - 1, 1 - s

                    def high(c):
                        act.wait_ge(t1_done, 8 + ga * 8 + c + 1)
                        act.wait_ge(f1_done, ga * 8 + c + 1)
                        act.activation(Sh[:, c % 2], ps[:, TP[c % 2], :], ACT.Copy).then_inc(sh_split, 1)

                    def high2(k):
                        act.wait_ge(t2_done, 2 + gb * 3 + k + 1)
                        act.wait_ge(f2_done, gb * 3 + k + 1)
                        act.activation(T2h[:, (sb_ * 3 + k) % 2], ps[:, T2P[(sb_ * 3 + k) % 2], :], ACT.Copy).then_inc(t2h_done, 1)

                    def modes(m):
                        act.wait_ge(f2_done, 2 + gb * 3 + 2 + m)
                        act.wait_ge(x_stored[sb_], 128 * (a * 8 + g - 1 - sb_) + 256)
                        act.activation(F2o[:, sb_, :, 6 * m:6 * m + 6].rearrange("p h k m -> p k h m"),
                                       ps[:, F2P[m], 0:288].rearrange("p (k h m) -> p k h m", k=6, h=4),
                                       ACT.Copy).then_inc(f2e_done, 1)

                    for c in range(8):
                        if now:
                            if c in (0, 2):
                                relu(g, 2 + c // 2)
                            if c in (4, 6) and after:
                                relu(g + 1, c // 2 - 2)
                            high(c)
                        if before:
                            if c < 3:
                                high2(c)
                            if c in (3, 4):
                                modes(c - 3)
                relu(0, 0)
                relu(0, 1)
                skewed(act, group)

            def mix(l):
                for p in range(6):
                    for h in range(2):
                        hh = (l * 6 + p) * 2 + h
                        act.wait_ge(mix_done, 4 + hh + 1)
                        act.wait_ge(yt_done, l * 6 + p + 1)
                        act.activation(Ys[:, p % 2, :, 12 * h:12 * h + 12].rearrange("p o k -> p k o"),
                                       ps[:, (p % 2) * 2 + h, 0:384].rearrange("p (k o) -> p k o", o=C),
                                       ACT.Copy).then_inc(y_done, 1)

            def phase_b(l):
                act.wait_ge(lp_loaded, 16 * (l + 1))

                def group(g, s, i):
                    gb = l * G + g

                    def zcopy(z):
                        act.wait_ge(t4_done, 8 + gb * 4 + z + 1)
                        act.wait_ge(fin_done, (gb * 4 + z) * 2 + 2)
                        act.activation(S[:, z % 2], ps[:, ZP[z % 2], :], ACT.Copy).then_inc(ze_done, 1)

                    def keep(c):
                        act.wait_ge(fin_done, 4 + gb * 8 + c + 1)
                        act.activation(v[:, bass.ds(g * NPOS + c * 512, 512)], ps[:, OP[c % 4], :], ACT.Identity,
                                       bias=wb).then_inc(oe_done, 1)
                    zcopy(0)
                    zcopy(1)
                    keep(0)
                    keep(1)
                    zcopy(2)
                    keep(2)
                    keep(3)
                    zcopy(3)
                    for c in range(4, 8):
                        keep(c)
                groups(act, group)
                act.wait_ge(dch, l * STEPS + 5)
                act.activation(sd, var, ACT.Sqrt).then_inc(sq_done, 1)
                act.wait_ge(dch, (l + 1) * STEPS)
                act.wait_ge(oe_done, 4 + (l + 1) * 64)

            def step(l, last):
                mix(l)
                phase_b(l)
                if not last:
                    phase_a(l)
            layers(act, first, step)
            act.wait_ge(qb_done, 1)

            def tokens(g, s, i):
                for c in range(8):
                    act.wait_ge(h_mm, g * 8 + c + 1)
                    if c % 4 == 0:
                        act.wait_ge(h_stored[c // 4], 64 * g + 16)
                    act.activation(phase[0:4, 512 * c:512 * c + 512], ps[0:4, OP[c % 4], :], ACT.Identity,
                                   bias=sm[0:4, 17:18]).then_inc(h_done, 1)
            groups(act, tokens)

            def pairs(*stages):
                settle(act)
                with act.Fori(0, NJ // 2) as i:
                    for stage in stages:
                        for s in range(2):
                            stage(2 * i + s, s)

            def root(n, after):
                act.wait_ge(steps, after)
                act.activation(lns[:, 192:240], lns[:, 144:192], ACT.Sqrt).then_inc(sqrt_done, 1)

            root(1, STEP_E - 6)
            act.wait_ge(steps, STEP_E)

            def e_copy(j, s):
                act.wait_ge(tr_done, j + 1)
                settle(act)
                act.activation(es[:, s], phase[:, bass.ds(j * 192, 192)], ACT.Copy).then_inc(es_done, 1)

            def u_relu(j, s):
                for nh in range(2):
                    act.wait_ge(u_done, 4 + 2 * j + nh + 1)
                    settle(act)
                    act.activation(xa[:, nh, bass.ds(j * 384, 384)], ps[:, 2 + 2 * s + nh, 0:384],
                                   ACT.Relu).then_inc(wv_done, 1)
            pairs(e_copy, u_relu)
            root(2, STEP_V - 6)
            act.wait_ge(steps, STEP_X)

            def x_copy(j, s):
                act.wait_ge(sc_done, j + 1)
                settle(act)
                act.activation(xs[:, s], xa[:, :, bass.ds(j * 384, 384)], ACT.Copy).then_inc(xs_done, 1)

            def a_copy(j, s):
                act.wait_ge(a_done, 2 + j + 1)
                o = bass.ds(j * 192, 64)
                settle(act)
                act.activation(phase[0:64, o], ps[0:64, 4 + 2 * s, 0:64], ACT.Copy).then_inc(at_done, 1)
                act.activation(phase[64:128, o], ps[64:128, 5 + 2 * s, 0:64], ACT.Copy).then_inc(at_done, 1)
                act.activation(phase[:, bass.ds(j * 192 + 64, 128)].rearrange("p (b d) -> p b d", b=2),
                               ps[:, 4 + 2 * s:6 + 2 * s, 64:128], ACT.Copy).then_inc(at_done, 1)
            pairs(x_copy, a_copy)
            root(3, STEP_A - 6)
            act.wait_ge(steps, STEP_A)

            def an_copy(j, s):
                act.wait_ge(tr2_done, j + 1)
                settle(act)
                act.activation(es[:, s], phase[:, bass.ds(j * 192, 192)], ACT.Copy).then_inc(as_done, 1)

            def v_copy(j, s):
                act.wait_ge(vo_done, 2 + j + 1)
                settle(act)
                act.activation(phase[:, bass.ds(3072 + j * 192, 192)], ps[:, 6 + s, 0:192], ACT.Copy).then_inc(ve_done, 1)
            pairs(an_copy, v_copy)
            root(4, STEP_VS - 6)
            root(5, STEP_H - 6)
            act.wait_ge(steps, STEP_H)

            def chunks(*stages):
                settle(act)
                with act.Fori(0, NT // CH // 2) as i:
                    for stage in stages:
                        for s in range(2):
                            stage(2 * i + s, s)

            act.wait_ge(steps, STEP_L)
            act.activation(ex, lz, ACT.Exp).then_inc(exp_done, 1)

            def gelus(k, s):
                for e in range(E + 1):
                    act.wait_ge(hl_done, k * 9 + e + 1)
                    for fh in range(2):
                        n = 2 * e + fh
                        act.wait_ge(hm_done, k * 18 + n + 1)
                        act.activation(hid[:, e % 3, 512 * fh:512 * fh + 512], ps[:, n % 3, :], ACT.Gelu,
                                       bias=B1[:, n:n + 1], scale=1.0 / WS).then_inc(gelu_done, 1)
            act.wait_ge(steps, STEP_M)
            chunks(gelus)

        @block.vector
        def _(dve):
            dve.sem_inc(sl_split, 2)
            dve.sem_inc(t2l_done, 2)
            dve.sem_inc(f1e_done, 2)
            dve.sem_inc(yt_done, 2)
            dve.sem_inc(i1e_done, 2)
            dve.sem_inc(bs_done, 4)
            for sm_, n in ((eT_done, 4), (ur_done, 2), (am_done, 4), (aT_done, 4), (ym_done, 4), (e2T_done, 2),
                           (lg_done, 2), (p_done, 4), (m_done, 4), (sh_done, 1), (hh_done, 3)):
                dve.sem_inc(sm_, n)
            dve.memset(ones, 1.0).then_inc(ones_done, 1)
            dve.sem_inc(primed, 1)
            dve.wait_ge(primed, 4)
            dve.memset(v[:, G * NPOS // 4:], 0.0).then_inc(v_zero, 1)
            dve.wait_ge(consts, 16 * NCONST)
            dve.wait_ge(zeroed, 2)

            def phase_a(a):
                def group(g, s, now, before, after):
                    ga = a * G + g
                    gb, sb_ = ga - 1, 1 - s

                    def low(c):
                        dve.wait_ge(sh_split, ga * 8 + c + 1)
                        dve.tensor_tensor(Sl[:, c % 2], ps[:, TP[c % 2], :], Sh[:, c % 2], ALU.subtract).then_inc(sl_split, 1)

                    def low2(k):
                        dve.wait_ge(t2h_done, gb * 3 + k + 1)
                        slot = (sb_ * 3 + k) % 2
                        dve.tensor_tensor(T2l[:, slot], ps[:, T2P[slot], :], T2h[:, slot], ALU.subtract).then_inc(t2l_done, 1)

                    def modes(m):
                        dve.wait_ge(f1_done, 2 + ga * 8 + 2 * m + 2)
                        dve.wait_ge(t2_done, 2 + ga * 3)
                        dve.tensor_copy(F1o[:, :, 16 * m:16 * m + 16],
                                        ps[:, FP[m % 2], 0:384].rearrange("p (x k) -> p k x", k=KR)).then_inc(f1e_done, 1)

                    for c in range(9):
                        if now and c in (3, 5, 7):
                            modes((c - 3) // 2)
                        if now and c < 8:
                            low(c)
                        if before and c < 3:
                            low2(c)
                    if now:
                        modes(3)
                skewed(dve, group)

            def mix(l):
                for s in range(2):
                    dve.wait_ge(x_stored[s], 256 * l * 4 + 256)
                for r in range(4):
                    dve.wait_ge(v_stored[r], 16 * G * l + 16)
                for p in range(6):
                    for par in range(2):
                        ky = 2 * p + par
                        dve.wait_ge(mix_done, (l * 6 + p) * 2 + 4)
                        dve.tensor_copy(XB[64:128, par, :, 32:64], X[64:128, :, ky].rearrange("p b m -> p m b")).then_inc(xb1_done, 1)
                    if p >= 1:
                        turn(l, p - 1)
                turn(l, 5)

            def turn(l, p):
                dve.wait_ge(y_done, 4 + (l * 6 + p) * 2 + 2)
                dve.transpose(H[:, p].rearrange("p o b -> p (o b)"), Ys[:, p % 2].rearrange("p o k -> p (o k)")).then_inc(yt_done, 1)

            def phase_b(l):
                def group(g, s, i):
                    gb = l * G + g
                    dve.wait_ge(t4_done, gb * 4 + 4)
                    for u in range(4):
                        par = u % 2
                        k0 = 12 * (u // 2)
                        dve.wait_ge(i1_done, 8 + gb * 4 + u + 1)
                        dst = I1o[:, s, :, k0:k0 + 12].rearrange("p x (k e r) -> p k e r x", e=2, r=2)[:, :, par]
                        dve.tensor_copy(dst, ps[:, IP[par], 0:384].rearrange("p (k r x) -> p k r x", r=2, x=SX)).then_inc(i1e_done, 1)
                    for c in range(8):
                        dve.wait_ge(oe_done, 4 + gb * 8 + c + 1)
                        settle(dve)
                        dve.bn_stats(st[:, bass.ds((g * 8 + c) * 6, 6)],
                                     v[:, bass.ds(g * NPOS + c * 512, 512)]).then_inc(bs_done, 1)
                groups(dve, group)

                def link(n, ins):
                    ins.then_inc(dch, 1)
                    dve.wait_ge(dch, l * STEPS + n)
                dve.wait_ge(bs_done, 4 + (l + 1) * 64)
                settle(dve)
                link(1, dve.bn_aggr(agg, st[:, :]))
                dve.wait_ge(sm_done, 2 * l + 1)
                link(2, dve.tensor_copy(mv, ps[:, 0, 0:2]))
                link(3, dve.tensor_tensor(dif, agg[:, 0:1], mv[:, 0:1], ALU.subtract))
                link(4, dve.tensor_tensor(sq, dif, dif, ALU.mult))
                dve.wait_ge(sm_done, 2 * l + 2)
                link(5, dve.tensor_scalar(var, ps[:, 1, 0:1], mv[:, 1:2], EPS, ALU.add, ALU.add))
                dve.wait_ge(sq_done, l + 1)
                link(6, dve.reciprocal(r0, sd))
                link(7, dve.tensor_tensor(r2, r0, r0, ALU.mult))
                link(8, dve.tensor_scalar(t1, r2, var, -0.5, ALU.mult, ALU.mult))
                link(9, dve.tensor_scalar(rs, t1, 1.5, r0, ALU.add, ALU.mult))
                link(10, dve.tensor_tensor(scale, rs, gamma, ALU.mult))
                link(11, dve.tensor_copy(mw, mv[:, 0:1]))
                link(12, dve.tensor_tensor(ms, mw, scale, ALU.mult))
                link(13, dve.tensor_tensor(shift, beta, ms, ALU.subtract))

            def step(l, last):
                mix(l)
                phase_b(l)
                if not last:
                    phase_a(l)
            layers(dve, lambda: dve.wait_ge(x0e_done, 9), step)
            dve.tensor_scalar(qs[:, 4:8], qs[:, 0:4], scale, None, ALU.mult).then_inc(qs_done, 1)
            dve.wait_ge(qt_done, 1)
            dve.tensor_tensor(sm[0:4, 17:18], ps[0:4, 0, 0:1], qbias[0:4, :], ALU.add).then_inc(qb_done, 1)


            def pairs(*stages):
                settle(dve)
                with dve.Fori(0, NJ // 2) as i:
                    for stage in stages:
                        for s in range(2):
                            stage(2 * i + s, s)

            done = [0]

            def do(ins):
                done[0] += 1
                ins.then_inc(steps, 1)
                dve.wait_ge(steps, done[0])

            def norm(dst, src, scratch, eps, nth):
                wide = lambda a: a.unsqueeze(2).broadcast_to([128, NT, D])
                tot, mean, vs, ve, sdv, rv, rv2, nt, rst = (lns[:, 48 * i:48 * i + 48] for i in range(9))
                do(dve.tensor_reduce(tot, src, AX.X, ALU.add))
                do(dve.tensor_scalar(mean, tot, 1.0 / D, None, ALU.mult))
                do(dve.tensor_tensor(dst, src, wide(mean), ALU.subtract))
                do(dve.tensor_tensor(scratch, dst, dst, ALU.mult))
                do(dve.tensor_reduce(vs, scratch, AX.X, ALU.add))
                do(dve.tensor_scalar(ve, vs, 1.0 / D, eps, ALU.mult, ALU.add))
                dve.wait_ge(sqrt_done, nth)
                do(dve.reciprocal(rv, sdv))
                do(dve.tensor_tensor(rv2, rv, rv, ALU.mult))
                do(dve.tensor_tensor(nt, rv2, ve, ALU.mult))
                do(dve.tensor_scalar(rst, nt, -0.5, 1.5, ALU.mult, ALU.add))
                do(dve.tensor_tensor(rst, rst, rv, ALU.mult))
                do(dve.tensor_tensor(dst, dst, wide(rst), ALU.mult))

            dve.wait_ge(txt_in, 32)
            for s in range(2):
                dve.wait_ge(h_stored[s], 16 * (1 + 4 * G))
            norm(eb, h_all, tmp, EPS, 1)
            assert done[0] == STEP_E

            def by_batch(k, s, done_sem):
                src, dst = ps[0:D, s, :], eTs[:, s].rearrange("p (b t) -> p b t", b=2)
                dve.tensor_copy(dst[:, :, 0:SX], src[:, 0:128].rearrange("p (b t) -> p b t", b=2)).then_inc(done_sem, 1)
                dve.tensor_copy(dst[:, :, SX:T], src[:, 128:384].rearrange("p (b t) -> p b t", b=2)).then_inc(done_sem, 1)

            def e_turned(j, s):
                dve.wait_ge(tr_done, 2 + j + 1)
                dve.wait_ge(u_done, 2 * j + 2)
                by_batch(j, s, eT_done)

            def u_total(j, s):
                dve.wait_ge(us_done, j + 1)
                dve.tensor_copy(u_row[:, bass.ds(j * 384, 384)], ps[0:1, 6 + s, 0:384]).then_inc(ur_done, 1)
            pairs(e_turned, u_total)

            dve.wait_ge(u_moved, 16)
            big = DECAY / TINY
            do(dve.tensor_scalar(k1, U, TINY, -big, ALU.is_ge, ALU.mult))
            do(dve.tensor_scalar(k2, k1, big, 1.0, ALU.add, ALU.max))
            do(dve.tensor_tensor_scan(z, k2, U, 0.0, ALU.mult, ALU.add))
            do(dve.tensor_scalar(k1[:, 1:T], z[:, 0:T - 1], big, DECAY, ALU.mult, ALU.min))
            do(dve.memset(k1[:, 0:1], 0.0))
            do(dve.tensor_tensor(k2, k1, U, ALU.add))
            do(dve.tensor_scalar(k1, k2, TINY, None, ALU.max))
            do(dve.reciprocal(rsum, k1))
            do(dve.memset(csum[:, 0:1], 0.0))
            do(dve.tensor_scalar(csum[:, 1:T], rsum[:, 0:T - 1], DECAY, None, ALU.mult))
            assert done[0] == STEP_RC
            norm(vb, eb, tmp, EPS, 2)
            assert done[0] == STEP_V
            dve.wait_ge(c_in, 16)
            for nh in range(2):
                do(dve.tensor_tensor_scan(xa[:, nh], cB, xa[:, nh], 0.0, ALU.mult, ALU.add))
            dve.wait_ge(r_in, 16)
            for nh in range(2):
                do(dve.tensor_tensor(xa[:, nh], xa[:, nh], rB, ALU.mult))
            assert done[0] == STEP_X

            def decay(j, s):
                dve.wait_ge(sc_done, 2 + j + 1)
                dve.wait_ge(a_done, j + 1)
                dve.tensor_tensor(Ai[:, s], ps[:, s, 0:T], Di, ALU.mult).then_inc(am_done, 1)
                dve.tensor_tensor(At[:, s].rearrange("p (b t) -> p b t", b=2),
                                  ps[:, 2 + s, 0:256].rearrange("p (b t) -> p b t", b=2),
                                  Dt.unsqueeze(1).broadcast_to([128, 2, TXT]), ALU.mult).then_inc(am_done, 1)
            pairs(decay)
            dve.wait_ge(at_done, 6 + 3 * NJ)
            norm(eb, eb, tmp2, EPS, 3)
            assert done[0] == STEP_A

            def a_turned(j, s):
                dve.wait_ge(tr2_done, 2 + j + 1)
                dve.wait_ge(yc_done, 2 * j + 2)
                by_batch(j, s, aT_done)

            def gate(j, s):
                dve.wait_ge(vo_done, j + 1)
                for nh in range(2):
                    dve.wait_ge(yc_done, 4 + 2 * j + nh + 1)
                    dve.scalar_tensor_tensor(ys[:, s, nh], ps[:, 2 + 2 * s + nh, 0:384], 0.0,
                                             xa[:, nh, bass.ds(j * 384, 384)], ALU.max, ALU.mult).then_inc(ym_done, 1)
            pairs(a_turned, gate)
            dve.wait_ge(ve_done, 2 + NJ)
            norm(vb, vb, tmp2, EPS, 4)
            do(dve.tensor_tensor(h_all, h_all, vb, ALU.add))
            norm(eb, h_all, tmp2, EPS, 5)
            assert done[0] == STEP_H

            def chunks(*stages):
                settle(dve)
                with dve.Fori(0, NT // CH // 2) as i:
                    for stage in stages:
                        for s in range(2):
                            stage(2 * i + s, s)

            do(dve.tensor_copy(ehl[:, :, 0], eb))
            do(dve.tensor_tensor(ehl[:, :, 1], eb, ehl[:, :, 0], ALU.subtract))
            assert done[0] == STEP_S

            def h_turned(k, s):
                dve.wait_ge(tr3_done, 2 + k + 1)
                settle(dve)
                dve.tensor_copy(v[:, bass.ds(k * 256, 256)].bitcast(F16), ps[:, s, 0:256].bitcast(F16)).then_inc(e2T_done, 1)

            def logits(k, s):
                dve.wait_ge(rt_done, 2 + k + 1)
                settle(dve)
                dve.tensor_scalar(cB[:, bass.ds(2048 + k * CH * E, CH * E)], ps[:, 2 + s, 0:CH * E], 1.0 / RS, None,
                                  ALU.mult).then_inc(lg_done, 1)
            chunks(h_turned, logits)
            dve.wait_ge(lg_done, 2 + NC)
            settle(dve)

            wide = lambda a: a.unsqueeze(2).broadcast_to([128, NT, E])
            ranks = rank.unsqueeze(1).broadcast_to([128, NT, E])
            top, tot, inv, m1, c1, m2, c2, den, dinv = (rr[:, i] for i in range(9))
            do(dve.tensor_reduce(top, lg, AX.X, ALU.max))
            do(dve.tensor_tensor(lz, lg, wide(top), ALU.subtract))
            assert done[0] == STEP_L
            dve.wait_ge(exp_done, 1)
            do(dve.tensor_reduce(tot, ex, AX.X, ALU.add))
            do(dve.reciprocal(inv, tot))
            do(dve.tensor_tensor(rw, ex, wide(inv), ALU.mult))
            do(dve.tensor_reduce(m1, rw, AX.X, ALU.max))
            do(dve.tensor_tensor(eq, rw, wide(m1), ALU.is_equal))
            do(dve.tensor_tensor(cd, eq, ranks, ALU.mult))
            do(dve.tensor_reduce(c1, cd, AX.X, ALU.max))
            do(dve.tensor_tensor(oh1, wide(c1), ranks, ALU.is_equal))
            do(dve.scalar_tensor_tensor(rw2, oh1, -4.0, rw, ALU.mult, ALU.add))
            do(dve.tensor_reduce(m2, rw2, AX.X, ALU.max))
            do(dve.tensor_tensor(eq, rw2, wide(m2), ALU.is_equal))
            do(dve.tensor_tensor(cd, eq, ranks, ALU.mult))
            do(dve.tensor_reduce(c2, cd, AX.X, ALU.max))
            do(dve.tensor_tensor(oh2, wide(c2), ranks, ALU.is_equal))
            do(dve.tensor_tensor(den, m1, m2, ALU.add))
            do(dve.reciprocal(dinv, den))
            do(dve.tensor_tensor(oh1, oh1, oh2, ALU.add))
            do(dve.tensor_tensor(oh1, oh1, rw, ALU.mult))
            do(dve.tensor_tensor(mask, oh1, wide(dinv), ALU.mult))
            assert done[0] == STEP_M

            def high(k, e):
                dve.wait_ge(gelu_done, 3 + k * 18 + 2 * e + 2)
                dve.wait_ge(w2_done, k * 9 + e + 1)
                settle(dve)
                dve.tensor_copy(hh[:, e % 3], hid[:, e % 3]).then_inc(hh_done, 1)

            def biased(k, t):
                dve.wait_ge(w2_done, 3 + 9 * k + E)
                dve.wait_ge(m_done, 4 * k + t + 1)
                dve.scalar_tensor_tensor(tb[:, t].rearrange("p e d -> p (e d)"), ps[:, 4 + t, :], 1.0 / WS, B2[:, 0:E * D],
                                         ALU.mult, ALU.add).then_inc(p_done, 1)

            def weighted(k, t):
                dve.wait_ge(p_done, 4 + 4 * k + t + 1)
                mk = cB[:, bass.ds(2048 + 9 * 384 + (k * CH + t) * E, E)].unsqueeze(2).broadcast_to([128, E, D])
                dve.tensor_tensor(tb[:, t], tb[:, t], mk, ALU.mult).then_inc(m_done, 1)
                dve.wait_ge(m_done, 4 + 4 * k + t + 1)
                dve.tensor_reduce(rt[:, t], tb[:, t].rearrange("p e d -> p d e"), AX.X, ALU.add).then_inc(r_done, 1)

            def shared(k):
                dve.wait_ge(w2_done, 3 + 9 * k + 9)
                dve.scalar_tensor_tensor(s1, ps[:, 3, 0:256].rearrange("p (t d) -> p t d", d=D), 1.0 / WS,
                                         B2[:, E * D:].unsqueeze(1).broadcast_to([128, CH, D]),
                                         ALU.mult, ALU.add).then_inc(sh_done, 1)

            def total(k):
                dve.wait_ge(r_done, 4 * k + 4)
                dve.wait_ge(sh_done, 1 + k + 1)
                dve.tensor_tensor(s2, s1, rt, ALU.add).then_inc(s2_done, 1)
                dve.wait_ge(s2_done, k + 1)
                hk = Xr[:, bass.ds(k * 256, 256)].rearrange("p (t d) -> p t d", d=D)
                dve.tensor_tensor(hk, hk, s2, ALU.add).then_inc(f_done, 1)

            def combine(k, piece):
                if piece == 0:
                    for t in range(CH):
                        biased(k, t)
                elif piece <= CH:
                    weighted(k, piece - 1)
                elif piece == CH + 1:
                    shared(k)
                elif piece == CH + 2:
                    total(k)

            for e in range(E + 1):
                high(0, e)
            settle(dve)
            with dve.Fori(1, NC) as k:
                for e in range(E + 1):
                    high(k, e)
                    combine(k - 1, e)
            for piece in range(E + 1):
                combine(NC - 1, piece)


def kernel(**inputs):
    import numpy as np
    import concourse.bacc as bacc
    from concourse.bass_utils import run_bass_kernel_spmd

    f = {k: np.ascontiguousarray(a) for k, a in inputs.items()}
    arrays = {}
    arrays["x"] = f["x"].reshape(B, NPOS)
    gx = np.linspace(0.0, 1.0, SX, dtype=np.float32)
    grid = np.stack([np.repeat(gx, SY), np.tile(gx, SX), np.ones(NPOS, np.float32)])
    arrays["grid"] = np.ascontiguousarray(np.broadcast_to(grid[:, None], (3, G, NPOS)))
    pin = np.zeros((Q + 3, Q, C), np.float32)
    for q in range(Q):
        pin[q, q] = f["L0_tok_p_w"][0]
        pin[Q, q] = f["L0_tok_p_w"][1]
        pin[Q + 1, q] = f["L0_tok_p_w"][2]
        pin[Q + 2, q] = f["L0_tok_p_b"]
    pint = np.zeros((128, 128), np.float32)
    pint[:, 0:Q + 3] = pin.reshape(Q + 3, 128).T
    arrays["pint"] = pint
    pblk = np.zeros((4, 4, 4, C), np.float32)
    for part in range(4):
        pblk[:, part, part] = np.concatenate([f["L0_tok_p_w"], f["L0_tok_p_b"][None]])
    arrays["pblk"] = pblk.reshape(16, 128)
    arrays["xt"] = f["x"].reshape(2, NJ, SX, SY).transpose(3, 1, 0, 2).reshape(SY, NJ * 128)
    arrays["txt"] = f["txt"]
    avg = np.kron(np.full((Q, Q), 1.0 / Q), np.eye(C)).astype(np.float32)
    names = []
    for n, a in enumerate([*spectral_tables(), np.eye(128, dtype=np.float32), avg]):
        arrays[f"table{n}"] = a
        names.append(f"table{n}")
    fw = np.stack([f["L0_tok_fw1"], f["L0_tok_fw2"]])
    a = fw.transpose(5, 0, 2, 1, 4, 6, 3)
    a = np.stack([a, a[..., ::-1, :]], axis=2)
    arrays["fw"] = np.ascontiguousarray(a.reshape(M, 128, L, M, 64))
    lp = np.zeros((L, 128, 131), np.float32)
    for q in range(Q):
        s = slice(q * C, (q + 1) * C)
        lp[:, s, s] = f["L0_tok_w_w"]
        lp[:, s, 128], lp[:, s, 129], lp[:, s, 130] = f["L0_tok_w_b"], f["L0_tok_bn_g"], f["L0_tok_bn_b"]
    arrays["lp"] = lp
    qblk = np.zeros((128, 4), np.float32)
    for q in range(Q):
        qblk[q * C:(q + 1) * C, q] = f["L0_tok_q_w"][:, 0]
    arrays["qblk"] = qblk
    arrays["qb"] = np.ascontiguousarray(np.broadcast_to(f["L0_tok_q_b"].reshape(1, 1), (4, 1)))

    arrays["att"] = attention_tables()
    arrays["dxy"] = np.concatenate([f["L0_attn_Dx"].T, f["L0_attn_Dy"].T], axis=1)
    arrays["et"] = f["L0_attn_E"].T.reshape(2, 128, D).transpose(1, 0, 2)
    w1 = np.concatenate([f["L0_ffn_W1p"], f["L0_ffn_W1s"][None]])
    w2 = np.concatenate([f["L0_ffn_W2p"], f["L0_ffn_W2s"][None]])
    b1 = np.concatenate([f["L0_ffn_b1p"], f["L0_ffn_b1s"][None]])
    b2 = np.concatenate([f["L0_ffn_b2p"], f["L0_ffn_b2s"][None]])
    arrays["w1"] = w1.transpose(1, 0, 2)
    arrays["w2"] = w2.reshape(E + 1, 2, 128, D).transpose(2, 1, 0, 3)
    arrays["wr"] = f["L0_ffn_Wr"]
    arrays["b1"] = b1.reshape(2 * (E + 1), 128).T
    arrays["b2"] = np.broadcast_to(b2.reshape(1, -1), (128, (E + 1) * D))

    nc = bacc.Bacc("TRN2", target_bir_lowering=False, num_devices=1)
    arrays = {f"in_{k}": np.ascontiguousarray(a) for k, a in arrays.items()}
    ap = {k: nc.dram_tensor(k, a.shape, mybir.dt.from_np(a.dtype), kind="ExternalInput").ap() for k, a in arrays.items()}
    out = nc.dram_tensor("out_0", (B, T, D), F32, kind="ExternalOutput").ap()
    build(nc, ap["in_x"], ap["in_grid"], ap["in_xt"], ap["in_pint"], ap["in_pblk"], ap["in_txt"], [ap[f"in_{n}"] for n in names], ap["in_fw"],
          ap["in_lp"], ap["in_qblk"], ap["in_qb"], ap["in_att"], ap["in_dxy"], ap["in_et"], ap["in_w1"], ap["in_w2"],
          ap["in_wr"], ap["in_b1"], ap["in_b2"], nc.dram_tensor("norms", (2, NW), F32, kind="Internal").ap(), out)
    r = run_bass_kernel_spmd(nc, [arrays], core_ids=[0])
    return r.results[0]["out_0"]
```

```python
from contextlib import ExitStack

import concourse.bass as bass
from concourse import mybir

ACT = mybir.ActivationFunctionType
ALU = mybir.AluOpType
AX = mybir.AxisListType
F32, F16 = mybir.dt.float32, mybir.dt.float16

B, SX, SY = 32, 64, 64
C, L, M = 32, 4, 12
Q = 4
G = B // Q
NPOS = SX * SY
KR = 2 * M
TXT, D = 128, 64
T = SX + TXT
N = 256
NJ = B // 2
EPS = 1e-5
DECAY, TINY = 0.97, 1e-12
E, F = 8, 256
NT = 3 * NJ
NW = B * T
CH = 4
NC = NT // CH
LP = 832
WS, RS = 2.0 ** 8, 2.0 ** 10
DS, ES = 2.0 ** 6, 2.0 ** 8


def spectral_tables():
    import numpy as np

    y, ky = np.arange(SY), np.arange(M)
    kx = np.concatenate([np.arange(M), np.arange(SX - M, SX)])
    x = np.arange(SX)
    ay = 2 * np.pi * np.outer(y, ky) / SY
    ax = 2 * np.pi * np.outer(x, kx) / SX
    fy = np.zeros((2, SY, 2, M, 2))
    for i in range(2):
        fy[i, :, i, :, 0] = np.cos(ay)
        fy[i, :, i, :, 1] = -np.sin(ay)
    fx = np.zeros((2, SX, 2, 2, M))
    c, s = np.cos(ax).reshape(SX, 2, M), np.sin(ax).reshape(SX, 2, M)
    fx[0, :, :, 0], fx[0, :, :, 1] = c, -s
    fx[1, :, :, 0], fx[1, :, :, 1] = s, c
    ix = np.zeros((2, 2, 32, 2, 2, SX))
    c, s = (a.T.reshape(2, M, SX) / (SX * SY) for a in (np.cos(ax), np.sin(ax)))
    for i in range(2):
        ix[i, :, 0:KR:2, i, 0], ix[i, :, 0:KR:2, i, 1] = c, s
        ix[i, :, 1:KR:2, i, 0], ix[i, :, 1:KR:2, i, 1] = -s, c
    w = np.where(ky == 0, 1.0, 2.0)[:, None]
    iy = np.zeros((4, 32, 4, SY))
    for i in range(4):
        iy[i, 0:KR:2, i] = w * np.cos(ay).T
        iy[i, 1:KR:2, i] = -w * np.sin(ay).T
    f = lambda a, n: a.reshape(128, n).astype(np.float32)
    fy1 = fy[0, :, 0].reshape(SY, KR)
    fx2 = np.zeros((2, SX, 2, 2, 2, 2, M))
    for i in range(2):
        fx2[i, :, :, i] = fx.transpose(1, 0, 2, 3, 4)
    gx, one = np.linspace(0, 1, SX), np.ones(SX)
    modes = np.stack([np.exp(-1j * ay).T @ b[:, None] * (a[None] @ np.exp(-1j * ax)) for a, b in ((gx, one), (one, gx), (one, one))])
    modes = modes.reshape(3, M, 2, M).transpose(0, 2, 1, 3)
    gm = np.stack([modes.real, modes.imag], axis=2).reshape(12, M * M).astype(np.float32)
    def halves(a):
        a = a.reshape(128, -1)
        high = a.astype(np.float16)
        return np.concatenate([high, (a - high).astype(np.float16)], axis=1)
    return halves(fy), halves(fx), f(ix, 256), halves(iy), fy1.astype(np.float32), f(fx2, 192), gm


def attention_tables():
    import numpy as np

    s, t = np.arange(T)[:, None], np.arange(T)[None, :]
    decay = np.where(s < t, DECAY ** np.maximum(t - 1 - s, 0), 0.0).astype(np.float32)
    rank = np.broadcast_to(np.arange(E, 0, -1, dtype=np.float32), (128, E))
    return np.concatenate([np.concatenate([decay[:SX], decay[:SX]]), decay[SX:, SX:], rank], axis=1)


def build(nc, x, grid, xt, pint, pblk, txt, tables, fw, lp, qblk, qb, att, dxy, et, w1, w2, wr, b1, b2, rdram, out):
    ctx = ExitStack()
    with ctx:
        def sb(name, shape, dt=F32):
            return ctx.enter_context(nc.sbuf_tensor(name, shape, dt))

        def sem(name):
            return ctx.enter_context(nc.semaphore(name))

        v = sb("v", [128, G * NPOS])
        phase = sb("phase", [128, 6656])
        R = phase[:, 0:4096]
        F1o = phase[:, 4096:5632].rearrange("p (k x) -> p k x", x=SX)
        T2h, T2l = (phase[:, a:a + 512].bitcast(F16).rearrange("p (s n) -> p s n", s=2) for a in (5632, 6144))
        H = phase[:, 0:6144].rearrange("p (k o b) -> p k o b", k=6, o=C)
        S = sb("S", [128, 2, 512])
        Sh, Sl = (S[:, i].bitcast(F16).rearrange("p (s n) -> p s n", s=2) for i in range(2))
        Xr = sb("Xr", [128, B * 144])
        X = Xr[:, :].rearrange("p (b k m) -> p b k m", b=B, k=M)
        I1o = Xr[:, 0:4096].rearrange("p (s x k) -> p s x k", s=2, x=SX)
        hbuf = Xr[:, 0:3 * NJ * D].rearrange("p (j t d) -> p j t d", j=NJ, t=3)
        Yr = sb("Yr", [128, 2048])
        F2o = Yr[:, 0:1152].rearrange("p (s h k m) -> p s h k m", s=2, h=4, k=M)
        Ys = Yr[:, :].rearrange("p (s o k) -> p s o k", s=2, o=C)
        Hg = Yr[:, 0:1536].rearrange("p (s k n) -> p s k n", s=2, k=6)
        XB = sb("XB", [128, 2, M, 64])
        W = sb("W", [128, 4, M, 64])
        fy, fx, ix, iy = sb("fy", [128, 96], F16), sb("fx", [128, 96], F16), sb("ix", [128, 256]), sb("iy", [128, 512], F16)
        ident, avg = sb("ident", [128, 128]), sb("avg", [128, 128])
        lps = sb("lps", [128, 131])
        st = sb("st", [128, G * 8 * 6])
        sm = sb("sm", [128, 24])
        qs = sb("qs", [128, 8])
        agg, mv, dif, sq, var, sd, r0, r2, t1, rs, mw, ms, scale, shift, qbias = (
            sm[:, 0:2], sm[:, 2:4], sm[:, 4:5], sm[:, 5:6], sm[:, 6:7], sm[:, 7:8], sm[:, 8:9], sm[:, 9:10],
            sm[:, 10:11], sm[:, 11:12], sm[:, 12:13], sm[:, 13:14], sm[:, 14:15], sm[:, 15:16], sm[:, 16:17])
        ones = sm[:, 18:19]
        wblk, wb, gamma, beta = lps[:, 0:128], lps[:, 128:129], lps[:, 129:130], lps[:, 130:131]

        xts = phase[0:SY, 4608:6656]
        hat = phase[0:16, 0:B * M * M]
        Gy = S[:, 0, 0:384].rearrange("p (r m) -> p r m", r=2)
        Gx = st[0:8 * M, 0:192]
        fx2, pT, pb, fy1 = S[:, 1, 0:192].rearrange("p (r n) -> p r n", r=2), S[:, 1, 192:320], S[0:16, 1, 320:448], S[0:SY, 1, 448:472]

        u_row = v[0:1, 0:NW]
        e2T = v[:, 0:NW // 2].bitcast(F16)
        xa = v[:, NW:3 * NW].rearrange("p (h n) -> p h n", h=2)
        rB, cB = v[:, 3 * NW:4 * NW], v[:, 4 * NW:5 * NW]
        spare = v[:, 5 * NW:]
        es = spare[:, 0:384].bitcast(F16).rearrange("p (s t h d) -> p s t h d", s=2, t=3, h=2)
        eTs = spare[:, 384:768].bitcast(F16).rearrange("p (s n) -> p s n", s=2)
        Vs = spare[:, 1152:1536].rearrange("p (s n) -> p s n", s=2)
        Ai = spare[:, 1536:1920].rearrange("p (s n) -> p s n", s=2)
        At = S[:, 0, :].rearrange("p (s n) -> p s n", s=2)
        xs = Xr[:, 3072:4608].rearrange("p (s h n) -> p s h n", s=2, h=2)
        ys = cB[:, 0:1536].rearrange("p (s h n) -> p s h n", s=2, h=2)
        tok = lambda a: a.rearrange("p (k d) -> p k d", d=D)
        h_all = tok(Xr[:, 0:3072])
        eb, vb, tmp, tmp2 = tok(phase[:, 0:3072]), tok(phase[:, 3072:6144]), tok(W[:, :, :, :].rearrange("p a b c -> p (a b c)")), tok(rB[:, 0:3072])
        Dxy = S[:, 1, :]
        XBr = XB[:, :, :, :].rearrange("p a b c -> p (a b c)")
        W2f = XBr[:, 0:1152]
        ET = XBr[:, 1152:1280]
        Dh, Dxl, Dyl = st[:, 0:256].bitcast(F16), spare[:, 1920:2048].bitcast(F16), XBr[:, 1314:1442].bitcast(F16)
        Eh, El = (st[:, a:a + 64].bitcast(F16) for a in (256, 320))
        ident16 = XBr[:, 1442:1506].bitcast(F16)
        Ehv, Elv = (a.rearrange("p (h d) -> p h d", h=2) for a in (Eh, El))
        ysh, ysl = (rB[:, a:a + 768].bitcast(F16).rearrange("p (s h n) -> p s h n", s=2, h=2) for a in (3072, 3840))
        Wr = XBr[:, 1280:1288]
        B1 = XBr[:, 1288:1306]
        B2 = Yr[:, 0:576]
        Di, Dt, rank = Yr[:, 576:768], Yr[:, 768:896], XBr[:, 1306:1314]
        U, k1, k2, z, rsum, csum = (Yr[0:B, 896 + i * T:896 + (i + 1) * T] for i in range(6))
        Wf = W[:, :, :, :].rearrange("p a b c -> p (a b c)")
        W1 = Wf[:, 0:2304]
        W1h, W1l = (v[:, 3072 + 1152 * i:4224 + 1152 * i].bitcast(F16) for i in range(2))
        W2h, W2l = v[:, 5376:5952].bitcast(F16), Wf[:, 2304:2880].bitcast(F16)
        Wrh, Wrl = (Wf[:, a:a + 4].bitcast(F16) for a in (2880, 2884))
        W2hv, W2lv = (a.rearrange("p (f e d) -> p f e d", f=2, e=E + 1) for a in (W2h, W2l))
        lns = Xr[:, 3840:4272]
        lg, lz, ex, rw, eq, cd, oh1, rw2, oh2, mask = (
            cB[:, 2048 + 384 * i:2432 + 384 * i].rearrange("p (k e) -> p k e", e=E) for i in range(10))
        rr = rB[:, 4608:5184].rearrange("p (i k) -> p i k", k=NT)
        ehl = rB[:, 0:3072].bitcast(F16).rearrange("p (k h d) -> p k h d", h=2, d=D)
        hid = v[:, NW:NW + 3072].rearrange("p (s n) -> p s n", s=3)
        hh, hl = (v[:, NW + 3072 + 1536 * i:NW + 4608 + 1536 * i].bitcast(F16).rearrange("p (s n) -> p s n", s=3) for i in range(2))
        tb = rB[:, 3648:5696].rearrange("p (t e d) -> p t e d", t=CH, e=E)
        rt = Xr[:, 3072:3328].rearrange("p (t d) -> p t d", d=D)
        s1 = Xr[:, 3328:3584].rearrange("p (t d) -> p t d", d=D)
        s2 = Xr[:, 3584:3840].rearrange("p (t d) -> p t d", d=D)

        ps = ctx.enter_context(nc.psum_tensor("ps", [128, 8, 512], F32))
        TP, FP, T2P, F2P = (0, 1), (2, 3), (4, 5), (6, 7)
        IP, ZP, OP = (0, 1), (2, 3), (4, 5, 6, 7)

        consts, primed, zeroed, carried = (sem(n) for n in ("consts", "primed", "zeroed", "carried"))
        v_in, xt_in, v_zero, xy_done, xye_done, xx_done, xxe_done = (sem(n) for n in (
            "v_in", "xt_in", "v_zero", "xy_done", "xye_done", "xx_done", "xxe_done"))
        hat_in, x0_done, x0e_done, fold_done, folded = (sem(n) for n in (
            "hat_in", "x0_done", "x0e_done", "fold_done", "folded"))
        relu_done, t1_done, sh_split, sl_split, f1_done, f1e_done = (sem(n) for n in (
            "relu_done", "t1_done", "sh_split", "sl_split", "f1_done", "f1e_done"))
        t2_done, t2h_done, t2l_done, f2_done, f2e_done = (sem(n) for n in (
            "t2_done", "t2h_done", "t2l_done", "f2_done", "f2e_done"))
        v_stored = [sem(f"v_stored{r}") for r in range(4)]
        x_stored = [sem(f"x_stored{s}") for s in range(2)]
        w_loaded = [sem(f"w_loaded{s}") for s in range(4)]
        w_neg, xb_done, mix_done, y_done, yt_done = (sem(n) for n in (
            "w_neg", "xb_done", "mix_done", "y_done", "yt_done"))
        hg_done, i1_done, i1e_done, t4_done, zh_done, zl_done = (sem(n) for n in (
            "hg_done", "i1_done", "i1e_done", "t4_done", "zh_done", "zl_done"))
        fin_done, oe_done, bs_done = sem("fin_done"), sem("oe_done"), sem("bs_done")
        lp_loaded, dch, sm_done, sq_done = sem("lp_loaded"), sem("dch"), sem("sm_done"), sem("sq_done")
        qs_done, qt_done, qb_done, h_mm, h_done = (sem(n) for n in ("qs_done", "qt_done", "qb_done", "h_mm", "h_done"))
        h_stored = [sem(f"h_stored{s}") for s in range(2)]
        txt_in, out_st = sem("txt_in"), sem("out_st")
        h_in, out_st2 = sem("h_in"), sem("out_st2")
        es_done, tr_done, eT_done, u_done, wv_done, us_done, ur_done = (sem(n) for n in (
            "es_done", "tr_done", "eT_done", "u_done", "wv_done", "us_done", "ur_done"))
        xs_done, vs_done, sc_done, am_done, a_done, at_done = (sem(n) for n in (
            "xs_done", "vs_done", "sc_done", "am_done", "a_done", "at_done"))
        as_done, tr2_done, aT_done, yc_done, ym_done, vo_done, ve_done = (sem(n) for n in (
            "as_done", "tr2_done", "aT_done", "yc_done", "ym_done", "vo_done", "ve_done"))
        tr3_done, e2T_done, rt_done, lg_done = (sem(n) for n in ("tr3_done", "e2T_done", "rt_done", "lg_done"))
        split, hh_done, hl_done, hlv_done = (sem(n) for n in ("split", "hh_done", "hl_done", "hlv_done"))
        el_done, al_done, yh_done, yl_done = (sem(n) for n in ("el_done", "al_done", "yh_done", "yl_done"))
        hm_done, gelu_done, w2_done, p_done, m_done, r_done, sh_done, f_done = (sem(n) for n in (
            "hm_done", "gelu_done", "w2_done", "p_done", "m_done", "r_done", "sh_done", "f_done"))
        ones_done, s2_done = sem("ones_done"), sem("s2_done")
        late, w1_in, twoin = sem("late"), sem("w1_in"), sem("twoin")
        tok_ready, steps, sqrt_done, exp_done = sem("tok_ready"), sem("steps"), sem("sqrt_done"), sem("exp_done")
        u_moved, rc_out, r_in, c_in = sem("u_moved"), sem("rc_out"), sem("r_in"), sem("c_in")
        SPLIT_D, SPLIT_W = 10, 21
        STEPS = 13
        STEP_E = 12
        STEP_RC = STEP_E + 10
        STEP_V = STEP_RC + 12
        STEP_X = STEP_V + 4
        STEP_A = STEP_X + 12
        STEP_VS = STEP_A + 12
        STEP_H = STEP_VS + 1 + 12
        STEP_S = STEP_H + 2
        STEP_L = STEP_S + 2
        STEP_M = STEP_L + 19
        NCONST = 12

        block = ctx.enter_context(nc.Block())

        def groups(eng, body):
            settle(eng)
            with eng.Fori(0, G // 2) as i:
                for s in range(2):
                    body(2 * i + s, s, i)

        def skewed(eng, body):
            body(0, 0, True, False, True)
            settle(eng)
            with eng.Fori(0, G // 2 - 1) as i:
                for s in (1, 0):
                    body(2 * i + 2 - s, s, True, True, True)
            body(G - 1, 1, True, True, False)
            body(G, 0, False, True, False)

        def leading(eng, body):
            settle(eng)
            with eng.Fori(0, G // 2 - 1) as i:
                for s in range(2):
                    body(2 * i + s, s, True)
            body(G - 2, 0, True)
            body(G - 1, 1, False)

        def in_turns(eng, count, *stages):
            def turn(i, lags):
                for stage, lag in stages:
                    if lag in lags:
                        for s in range(2):
                            stage(2 * (i - lag) + s, s)
            longest = max(lag for _, lag in stages)
            for i in range(longest):
                turn(i, range(i + 1))
            settle(eng)
            with eng.Fori(longest, count) as i:
                turn(i, range(longest + 1))
            for i in range(count, count + longest):
                turn(i, range(i - count + 1, longest + 1))

        def settle(eng):
            eng.sem_inc(carried, 1)

        def layers(eng, first, step):
            first()
            settle(eng)
            with eng.Fori(0, L - 1) as l:
                step(l, False)
            step(L - 1, True)

        @block.sync
        def _(sp):
            sp.dma_start(xts, xt).then_inc(xt_in, 16)
            for dst, src in ((fy1, tables[4]), (fx2, tables[5].rearrange("p (r n) -> p r n", r=2)), (pT, pint), (pb, pblk),
                             (fy[:, :], tables[0]), (fx[:, :], tables[1]), (ix[:, :], tables[2]), (iy[:, :], tables[3]),
                             (ident[:, :], tables[7]), (avg[:, :], tables[8]), (qs[:, 0:4], qblk), (qbias[0:4, :], qb)):
                sp.dma_start(dst, src).then_inc(consts, 16)
            sp.dma_start(hat[4:16].rearrange("p (b n) -> p b n", b=B),
                         tables[6].unsqueeze(1).broadcast_to([12, B, M * M])).then_inc(hat_in, 16)
            sp.dma_start(lps[:, :], lp[0]).then_inc(lp_loaded, 16)
            sp.wait_ge(primed, 4)

            def weights(l, kys):
                for ky in kys:
                    sp.wait_ge(mix_done, (l * M + ky) * 2 + 2)
                    sp.dma_start(W[:, ky % 4], fw[ky, :, bass.ds(l, 1)].rearrange("p l m n -> p (l m) n")).then_inc(w_loaded[ky % 4], 16)

            def first():
                weights(0, range(4))
                sp.wait_ge(xxe_done, 1)
                for part in range(4):
                    for two in range(2):
                        for image in range(2):
                            b0 = image * NJ + two * 8
                            o = two * 96 + image * 48 + part * M
                            sp.dma_start(hat[part:part + 1, b0 * M * M:(b0 + 8) * M * M].rearrange("p (n m) -> p n m", m=M),
                                         Gx[:, o:o + M]).then_inc(hat_in, 16)
                sp.wait_ge(v_zero, 2)
                sp.dma_start(v[0:Q, :].rearrange("q (g n) -> q g n", g=G), x.rearrange("(g q) n -> q g n", q=Q)).then_inc(v_in, 16)
                sp.dma_start(v[Q:Q + 3, :].rearrange("q (g n) -> q g n", g=G), grid).then_inc(v_in, 16)
                weights(0, range(4, M))

            def phase_a(a):
                weights(a + 1, range(4))

                def group(g, s, i):
                    sp.wait_ge(f2e_done, 2 + (a * G + g + 1) * 2)
                    for q in range(Q):
                        for h in range(4):
                            sp.dma_start(X[32 * h:32 * h + 32, bass.ds(g * Q + q, 1)].rearrange("p b k m -> p (b k m)"),
                                         F2o[32 * q:32 * q + 32, s, h].rearrange("p k m -> p (k m)")).then_inc(x_stored[s], 16)
                groups(sp, group)
                weights(a + 1, range(4, M))

            def params(l):
                sp.dma_start(lps[:, :], lp[bass.ds(l, 1)].rearrange("l p n -> (l p) n")).then_inc(lp_loaded, 16)

            def step(l, last):
                if not last:
                    sp.wait_ge(dch, (l + 1) * STEPS)
                    params(l + 1)
                    phase_a(l)
            layers(sp, first, step)

            def tokens(g, s, i):
                for hf in range(2):
                    sp.wait_ge(h_done, 4 + g * 8 + hf * 4 + 4)
                    for q in range(Q):
                        p0 = (q % 2) * 64 + 32 * hf
                        sp.dma_start(hbuf[p0:p0 + 32, bass.ds(2 * g + q // 2, 1), 0].rearrange("p j d -> p (j d)"),
                                     phase[q:q + 1, hf * 2048:(hf + 1) * 2048].rearrange("p (x y) -> p x y", y=D)
                                     ).then_inc(h_stored[hf], 16)
            sp.wait_ge(fin_done, 4 + L * 64)
            for two in range(2):
                sp.dma_start(hbuf[:, :, 1 + two], txt.rearrange("(j b) t d -> b t j d", b=2)[two]).then_inc(txt_in, 16)
            groups(sp, tokens)
            for dst, src in ((Dxy[0:D], dxy), (Dxy[D:2 * D], dxy), (Di, att[:, 0:T]), (Dt, att[:, T:T + TXT]),
                             (rank, att[:, T + TXT:]), (ET.rearrange("p (h d) -> p h d", h=2), et), (Wr[0:D], wr), (Wr[D:2 * D], wr), (B1, b1), (W2f.rearrange("p (f e d) -> p f e d", f=2, e=E + 1), w2), (B2, b2)):
                sp.dma_start(dst, src).then_inc(late, 16)
            sp.wait_ge(ur_done, 2 + NJ)
            sp.dma_start(U, u_row).then_inc(u_moved, 16)
            sp.wait_ge(steps, STEP_RC)
            sp.dma_start(rdram[0].rearrange("(b t) -> b t", b=B), rsum).then_inc(rc_out, 16)
            sp.dma_start(rdram[1].rearrange("(b t) -> b t", b=B), csum).then_inc(rc_out, 16)
            sp.wait_ge(rc_out, 32)
            sp.dma_start(cB, rdram[1:2, :].partition_broadcast(128)).then_inc(c_in, 16)
            sp.dma_start(rB, rdram[0:1, :].partition_broadcast(128)).then_inc(r_in, 16)
            sp.wait_ge(steps, STEP_V)
            for two in range(2):
                sp.dma_start(W1[D * two:D * two + D], w1).then_inc(w1_in, 16)
            o = out.rearrange("(j b) t d -> b t j d", b=2)
            for j0, j1 in ((0, NJ // 2), (NJ // 2, NJ)):
                sp.wait_ge(f_done, j1 * 3 // CH)
                for two in range(2):
                    sp.dma_start(o[two, 0:SX, j0:j1], hbuf[64 * two:64 * two + 64, j0:j1, 0]).then_inc(out_st, 16)
                    sp.dma_start(o[two, SX:T, j0:j1], hbuf[:, j0:j1, 1 + two]).then_inc(out_st, 16)
            sp.wait_ge(out_st, 128)

        @block.gpsimd
        def _(pool):
            pool.memset(v[:, 0:G * NPOS // 4], 0.0).then_inc(v_zero, 1)
            pool.memset(XB[:, :, :, :], 0.0).then_inc(zeroed, 1)
            pool.memset(Yr[:, :], 0.0).then_inc(zeroed, 1)
            for s in range(2):
                pool.sem_inc(x_stored[s], 256)
                pool.sem_inc(h_stored[s], 16)
            for r in range(4):
                pool.sem_inc(v_stored[r], 16)
            pool.sem_inc(hl_done, 3)
            pool.sem_inc(yl_done, 2)
            pool.sem_inc(primed, 1)
            pool.wait_ge(primed, 4)

            def phase_b(l):
                pool.wait_ge(yt_done, 2 + (l + 1) * 6)

                def group(g, s, i):
                    pool.wait_ge(i1_done, (l * G + g) * 3 + 3)
                    settle(pool)
                    pool.tensor_copy(Hg[:, s].rearrange("p k (q o) -> p k q o", q=Q),
                                     H[:, :, :, bass.ds(g * Q, Q)].rearrange("p k o q -> p k q o")).then_inc(hg_done, 1)
                    pool.wait_ge(hg_done, l * G + g + 1)
                groups(pool, group)

            pool.wait_ge(zeroed, 2)
            settle(pool)
            with pool.Fori(0, L) as l:
                phase_b(l)
            n_split = [0]

            def part(ins):
                n_split[0] += 1
                ins.then_inc(split, 1)
                pool.wait_ge(split, n_split[0])

            def halve(full, high, factor, *lows):
                part(pool.tensor_scalar(full, full, factor, None, ALU.mult))
                part(pool.tensor_copy(high, full))
                for low, cols, rows in lows:
                    part(pool.tensor_tensor(low[0:rows], full[0:rows, cols], high[0:rows, cols], ALU.subtract))
                    if rows < 128:
                        part(pool.memset(low[rows:128], 0.0))

            def pairs(*stages):
                settle(pool)
                with pool.Fori(0, NJ // 2) as i:
                    for stage in stages:
                        for s in range(2):
                            stage(2 * i + s, s)
            pool.wait_ge(late, 176)
            part(pool.tensor_copy(ident16, ident[:, :]))
            halve(Dxy, Dh, DS, (Dxl, slice(0, N), D), (Dyl, slice(N, 2 * N), D))
            halve(ET, Eh, ES, (El, slice(0, 2 * D), 128))
            assert n_split[0] == SPLIT_D

            def token_low(high_done, low_done):
                def stage(j, s):
                    pool.wait_ge(high_done, j + 1)
                    settle(pool)
                    pool.tensor_tensor(es[:, s, :, 1], phase[:, bass.ds(j * 192, 192)].rearrange("p (t d) -> p t d", d=D),
                                       es[:, s, :, 0], ALU.subtract).then_inc(low_done, 1)
                    pool.wait_ge(low_done, j + 1)
                return stage
            pairs(token_low(es_done, el_done))

            def values(j, s):
                pool.wait_ge(a_done, j + 1)
                settle(pool)
                pool.tensor_copy(Vs[:, s], phase[:, bass.ds(3072 + j * 192, 192)]).then_inc(vs_done, 1)
                pool.wait_ge(vs_done, j + 1)
            pool.wait_ge(steps, STEP_V)
            pairs(values)

            def y_low(j, s):
                pool.wait_ge(yh_done, j + 1)
                settle(pool)
                pool.tensor_tensor(ysl[:, s], ys[:, s], ysh[:, s], ALU.subtract).then_inc(yl_done, 1)
                pool.wait_ge(yl_done, 2 + j + 1)
            in_turns(pool, NJ // 2, (token_low(as_done, al_done), 0), (y_low, 2))
            pool.wait_ge(w1_in, 32)
            halve(Wr, Wrh, RS, (Wrl, slice(0, E), D))
            halve(W1, W1h, WS, (W1l, slice(0, 2304), D))
            halve(W2f, W2h, WS, (W2l, slice(0, 1152), 128))
            assert n_split[0] == SPLIT_W

            def chunk(k):
                for e in range(E + 1):
                    pool.wait_ge(w2_done, k * 9 + e + 1)
                    pool.wait_ge(hh_done, 3 + k * 9 + e + 1)
                    settle(pool)
                    pool.tensor_tensor(hl[:, e % 3, 0:LP], hid[:, e % 3, 0:LP], hh[:, e % 3, 0:LP], ALU.subtract).then_inc(hl_done, 1)
                    pool.wait_ge(hl_done, 3 + k * 9 + e + 1)
            settle(pool)
            with pool.Fori(0, NC) as k:
                chunk(k)

        @block.tensor
        def _(pe):
            pe.sem_inc(t1_done, 8)
            pe.sem_inc(f1_done, 2)
            pe.sem_inc(t2_done, 2)
            pe.sem_inc(f2_done, 2)
            pe.sem_inc(mix_done, 8)
            pe.sem_inc(i1_done, 6)
            pe.sem_inc(t4_done, 8)
            pe.sem_inc(fin_done, 4)
            for sm_, n in ((tr_done, 2), (u_done, 4), (sc_done, 2), (a_done, 2), (tr2_done, 2), (yc_done, 4),
                           (vo_done, 2), (tr3_done, 2), (rt_done, 2), (w2_done, 3)):
                pe.sem_inc(sm_, n)
            pe.sem_inc(primed, 1)
            pe.wait_ge(primed, 4)
            pe.wait_ge(consts, 16 * NCONST)
            pe.wait_ge(xt_in, 16)

            def first():
                for p in range(NJ):
                    mm = pe.matmul(ps[:, 0, KR * p:KR * p + KR], xts[:, 128 * p:128 * p + 128], fy1, start=True, stop=True)
                mm.then_inc(xy_done, 1)
                pe.wait_ge(lp_loaded, 16)
                pe.matmul(ps[:, 2, 0:128], pT, wblk, start=True, stop=True).then_inc(fold_done, 1)
                pe.wait_ge(xye_done, 1)
                for two in range(2):
                    for ri in range(2):
                        mm = pe.matmul(ps[0:96, 1, 192 * two:192 * two + 96], Gy[:, ri, 96 * two:96 * two + 96], fx2[:, ri],
                                       start=ri == 0, stop=ri == 1)
                mm.then_inc(xx_done, 1)
                pe.wait_ge(hat_in, 17 * 16)
                for c in range(9):
                    if c >= 5:
                        pe.wait_ge(x0e_done, c - 4)
                    pe.matmul(ps[:, 3 + c % 5, :], pb, hat[:, 512 * c:512 * c + 512], start=True, stop=True).then_inc(x0_done, 1)
                pe.wait_ge(v_in, 32)
                pe.wait_ge(folded, 1)
                pe.wait_ge(x0e_done, 9)

            def phase_a(a):
                def group(g, s, now, before, after):
                    ga = a * G + g

                    def turn(c):
                        if c % 2 == 0:
                            pe.wait_ge(relu_done, ga * 4 + c // 2 + 1)
                        pe.wait_ge(sl_split, ga * 8 + c + 1)
                        for j in range(4):
                            mm = pe.transpose(ps[:, TP[c % 2], 128 * j:128 * j + 128],
                                              R[:, 512 * c + 128 * j:512 * c + 128 * j + 128], ident[:, :])
                        mm.then_inc(t1_done, 1)

                    def ydft(c):
                        pe.wait_ge(sl_split, ga * 8 + c + 3)
                        if c % 2 == 0:
                            pe.wait_ge(f1e_done, ga * 4 + c // 2 + 1)
                        for j in range(4):
                            o, rows = (c % 2) * 192 + 48 * j, slice(128 * j, 128 * j + 128)
                            out1 = ps[:, FP[(c // 2) % 2], o:o + 48]
                            pe.matmul(out1, Sh[:, c % 2, rows], fy[:, 0:48], start=True, stop=False)
                            pe.matmul(out1, Sh[:, c % 2, rows], fy[:, 48:96], start=False, stop=False)
                            mm = pe.matmul(out1, Sl[:, c % 2, rows], fy[:, 0:48], start=False, stop=True)
                        mm.then_inc(f1_done, 1)

                    gb, sb_ = ga - 1, 1 - s

                    def turn2(k):
                        if k == 0:
                            pe.wait_ge(f1e_done, 2 + gb * 4 + 4)
                        pe.wait_ge(t2l_done, gb * 3 + k + 1)
                        for j in range(4):
                            ky = 4 * k + j
                            mm = pe.transpose(ps[:, T2P[(sb_ * 3 + k) % 2], 128 * j:128 * j + 128],
                                              F1o[:, 2 * ky:2 * ky + 2].rearrange("p k x -> p (k x)"), ident[:, :])
                        mm.then_inc(t2_done, 1)

                    def xdft(k):
                        pe.wait_ge(t2l_done, 2 + gb * 3 + k + 1)
                        slot = (sb_ * 3 + k) % 2
                        for j in range(4):
                            ky, rows = 4 * k + j, slice(128 * j, 128 * j + 128)
                            if ky % 6 == 0:
                                pe.wait_ge(f2e_done, gb * 2 + ky // 6 + 1)
                            out2 = ps[:, F2P[ky // 6], 48 * (ky % 6):48 * (ky % 6) + 48]
                            pe.matmul(out2, T2h[:, slot, rows], fx[:, 0:48], start=True, stop=False)
                            pe.matmul(out2, T2h[:, slot, rows], fx[:, 48:96], start=False, stop=False)
                            mm = pe.matmul(out2, T2l[:, slot, rows], fx[:, 0:48], start=False, stop=True)
                        mm.then_inc(f2_done, 1)

                    for c in range(9):
                        if now and c < 8:
                            turn(c)
                        if now and c > 0:
                            ydft(c - 1)
                        if before and 2 <= c < 5:
                            xdft(c - 2)
                        if before and c < 3:
                            turn2(c)
                skewed(pe, group)

            def mix(l):
                for p in range(6):
                    for par in range(2):
                        ky = 2 * p + par
                        pe.wait_ge(w_neg, (l * M + ky + 1) * 2)
                        pe.wait_ge(xb_done, (l * M + ky + 1) * 2)
                        for h in range(2):
                            pe.wait_ge(y_done, (l * 6 + p) * 2 + h + 1)
                            for m in range(6):
                                mm = pe.matmul(ps[64 * par:64 * par + 64, (p % 2) * 2 + h, 64 * m:64 * m + 64],
                                               XB[:, par, 6 * h + m], W[:, ky % 4, 6 * h + m], start=True, stop=True)
                            mm.then_inc(mix_done, 1)

            def phase_b(l):
                for r in range(4):
                    pe.wait_ge(v_stored[r], 16 * G * l + 16)
                pe.wait_ge(lp_loaded, 16 * (l + 1))

                def xinv(g, s, u):
                    gb = l * G + g
                    if u == 0:
                        pe.wait_ge(hg_done, gb + 1)
                    pe.wait_ge(i1e_done, gb * 3 + u + 1)
                    for j in range(2):
                        mm = pe.matmul(ps[:, IP[(s * 3 + u) % 2], 256 * j:256 * j + 256], Hg[:, s, 2 * u + j], ix[:, :],
                                       start=True, stop=True)
                    mm.then_inc(i1_done, 1)

                def turn(g, s, z):
                    gb = l * G + g
                    if z == 0:
                        pe.wait_ge(i1e_done, 2 + gb * 3 + 3)
                    pe.wait_ge(zl_done, gb * 4 + z + 1)
                    for j in range(4):
                        x0 = 16 * z + 4 * j
                        mm = pe.transpose(ps[:, ZP[z % 2], 128 * j:128 * j + 128],
                                          I1o[:, s, x0:x0 + 4].rearrange("p x k -> p (x k)"), ident[:, :])
                    mm.then_inc(t4_done, 1)

                def group(g, s, after):
                    gb = l * G + g

                    def add(c):
                        cf = gb * 8 + c
                        pe.wait_ge(oe_done, cf + 1)
                        pe.wait_ge(zl_done, 2 + gb * 4 + c // 2 + 1)
                        pe.matmul(ps[:, OP[c % 4], :], wblk, v[:, bass.ds(g * NPOS + c * 512, 512)],
                                  start=True, stop=False, skip_group_check=True)
                        for j in range(2):
                            z0 = (c % 2) * 256 + 128 * j
                            zh, zl = (a[:, (c // 2) % 2, z0:z0 + 128] for a in (Sh, Sl))
                            for z, table in ((zh, iy[:, 0:256]), (zh, iy[:, 256:512]), (zl, iy[:, 0:256])):
                                mm = pe.matmul(ps[:, OP[c % 4], 256 * j:256 * j + 256], z, table,
                                               start=False, stop=z is zl, skip_group_check=True)
                        mm.then_inc(fin_done, 1)
                    add(0)
                    add(1)
                    turn(g, s, 2)
                    add(2)
                    add(3)
                    turn(g, s, 3)
                    for c in range(4, 8):
                        add(c)
                        if after and c < 6:
                            xinv(g + 1, 1 - s, c - 4)
                        if after and c == 5:
                            xinv(g + 1, 1 - s, 2)
                        if after and c >= 6:
                            turn(g + 1, 1 - s, c - 6)
                for u in range(3):
                    xinv(0, 0, u)
                turn(0, 0, 0)
                turn(0, 0, 1)
                leading(pe, group)
                pe.wait_ge(dch, l * STEPS + 1)
                pe.matmul(ps[:, 0, 0:2], avg[:, :], agg, start=True, stop=True).then_inc(sm_done, 1)
                pe.wait_ge(dch, l * STEPS + 4)
                pe.matmul(ps[:, 1, 0:1], avg[:, :], sq, start=True, stop=True).then_inc(sm_done, 1)

            def step(l, last):
                mix(l)
                phase_b(l)
                if not last:
                    phase_a(l)
            layers(pe, first, step)
            pe.wait_ge(dch, L * STEPS)
            pe.matmul(ps[0:4, 0, 0:1], qs[:, 0:4], shift, start=True, stop=True).then_inc(qt_done, 1)
            pe.wait_ge(qs_done, 1)

            def tokens(g, s, i):
                for c in range(8):
                    pe.wait_ge(h_done, g * 8 + c + 1)
                    pe.matmul(ps[0:4, OP[c % 4], :], qs[:, 4:8], v[:, bass.ds(g * NPOS + c * 512, 512)],
                              start=True, stop=True).then_inc(h_mm, 1)
            groups(pe, tokens)

            def pairs(*stages):
                with pe.Fori(0, NJ // 2) as i:
                    for stage in stages:
                        for s in range(2):
                            stage(2 * i + s, s)

            def turn3(bank, s):
                settle(pe)
                for t in range(3):
                    mm = pe.transpose(ps[:, bank, 64 * t:64 * t + 64].bitcast(F16),
                                      es[:, s, t].rearrange("p h d -> p (h d)"), ident16)
                return mm

            def d_product(s, nh, first, low):
                o = ps[:, 2 + 2 * s + nh, 0:384]
                pe.matmul(o, Dh[:, first + 128 * nh:first + 128 * nh + 128], eTs[:, s], start=True, stop=False)
                return pe.matmul(o, low[:, 128 * nh:128 * nh + 128], eTs[:, s], start=False, stop=True)

            pe.wait_ge(ones_done, 1)
            pe.wait_ge(split, SPLIT_D)

            def turn_e(j, s):
                pe.wait_ge(el_done, j + 1)
                pe.wait_ge(eT_done, 2 * j + 2)
                turn3(s, s).then_inc(tr_done, 1)

            def u_mm(j, s):
                pe.wait_ge(eT_done, 4 + 2 * j + 2)
                pe.wait_ge(wv_done, 2 * j + 2)
                for nh in range(2):
                    d_product(s, nh, 0, Dxl).then_inc(u_done, 1)

            def u_sum(j, s):
                pe.wait_ge(wv_done, 4 + 2 * j + 2)
                pe.wait_ge(ur_done, j + 1)
                for nh in range(2):
                    mm = pe.matmul(ps[0:1, 6 + s, 0:384], ones, xa[:, nh, bass.ds(j * 384, 384)],
                                   start=nh == 0, stop=nh == 1)
                mm.then_inc(us_done, 1)
            pairs(turn_e, u_mm, u_sum)

            def scores(j, s):
                pe.wait_ge(xs_done, j + 1)
                pe.wait_ge(am_done, 2 * j + 2)
                for two in range(2):
                    o = two * T
                    for nh in range(2):
                        pe.matmul(ps[64 * two:64 * two + 64, s, 0:T], xs[:, s, nh, o:o + SX], xs[:, s, nh, o:o + T],
                                  start=nh == 0, stop=nh == 1)
                    for nh in range(2):
                        mm = pe.matmul(ps[:, 2 + s, 128 * two:128 * two + 128], xs[:, s, nh, o + SX:o + T],
                                       xs[:, s, nh, o + SX:o + T], start=nh == 0, stop=nh == 1)
                mm.then_inc(sc_done, 1)

            def values(j, s):
                pe.wait_ge(am_done, 4 + 2 * j + 2)
                pe.wait_ge(vs_done, j + 1)
                pe.wait_ge(at_done, 3 * j + 3)
                settle(pe)
                for two in range(2):
                    bank, h = 4 + 2 * s + two, slice(64 * two, 64 * two + 64)
                    pe.matmul(ps[h, bank, 0:64], Ai[h, s, 0:SX], Vs[h, s, 0:D], start=True, stop=True)
                    pe.matmul(ps[:, bank, 64:128], Ai[h, s, SX:T], Vs[h, s, 0:D], start=True, stop=False)
                    mm = pe.matmul(ps[:, bank, 64:128], At[:, s, 128 * two:128 * two + 128],
                                   Vs[:, s, D * (1 + two):D * (2 + two)], start=False, stop=True)
                mm.then_inc(a_done, 1)
            pairs(scores, values)

            def turn_a(j, s):
                pe.wait_ge(al_done, j + 1)
                pe.wait_ge(aT_done, 2 * j + 2)
                turn3(s, s).then_inc(tr2_done, 1)

            def y_mm(j, s):
                pe.wait_ge(aT_done, 4 + 2 * j + 2)
                pe.wait_ge(ym_done, 2 * j + 2)
                for nh in range(2):
                    d_product(s, nh, N, Dyl).then_inc(yc_done, 1)

            def e_mm(j, s):
                pe.wait_ge(yl_done, 2 + j + 1)
                pe.wait_ge(ve_done, j + 1)

                def product(o, cols):
                    for nh in range(2):
                        pe.matmul(o, ysh[:, s, nh, cols], Ehv[:, nh], start=nh == 0, stop=False)
                        pe.matmul(o, ysh[:, s, nh, cols], Elv[:, nh], start=False, stop=False)
                        mm = pe.matmul(o, ysl[:, s, nh, cols], Ehv[:, nh], start=False, stop=nh == 1)
                    return mm
                for two in range(2):
                    product(ps[64 * two:64 * two + 64, 6 + s, 0:D], slice(two * T, two * T + SX))
                for two in range(2):
                    mm = product(ps[:, 6 + s, D * (1 + two):D * (2 + two)], slice(two * T + SX, two * T + T))
                mm.then_inc(vo_done, 1)
            in_turns(pe, NJ // 2, (turn_a, 1), (y_mm, 2), (e_mm, 3))

            def chunks(*stages):
                with pe.Fori(0, NT // CH // 2) as i:
                    for stage in stages:
                        for s in range(2):
                            stage(2 * i + s, s)

            def turn_h(k, s):
                pe.wait_ge(e2T_done, k + 1)
                settle(pe)
                o = ps[:, s, 0:256].bitcast(F16)
                for t in range(CH):
                    mm = pe.transpose(o[:, 128 * t:128 * t + 128], rB[:, bass.ds((k * CH + t) * 64, 64)].bitcast(F16), ident16)
                mm.then_inc(tr3_done, 1)

            def route(k, s):
                pe.wait_ge(e2T_done, 2 + k + 1)
                pe.wait_ge(lg_done, k + 1)
                settle(pe)
                for t in range(CH):
                    for w in (Wrh, Wrl):
                        mm = pe.matmul(ps[:, 2 + s, E * t:E * t + E], v[:, bass.ds((k * CH + t) * 64, 64)].bitcast(F16), w,
                                       start=w is Wrh, stop=w is Wrl)
                mm.then_inc(rt_done, 1)
            pe.wait_ge(split, SPLIT_W)
            pe.wait_ge(steps, STEP_S)
            in_turns(pe, NC // 2, (turn_h, 0), (route, 1))

            pe.wait_ge(lg_done, 2 + NC)

            def up(k, e):
                for fh in range(2):
                    n = 2 * e + fh
                    pe.wait_ge(gelu_done, k * 18 + n + 1)
                    settle(pe)
                    for w in (W1h, W1l):
                        mm = pe.matmul(ps[:, n % 3, :], w[:, 256 * e + 128 * fh:256 * e + 128 * fh + 128],
                                       v[:, bass.ds(k * 256, 256)].bitcast(F16), start=w is W1h, stop=w is W1l)
                    mm.then_inc(hm_done, 1)

            def down(k, e):
                pe.wait_ge(hl_done, 3 + k * 9 + e + 1)
                pe.wait_ge(hlv_done, 3 + k * 9 + e + 1)
                if e == E:
                    pe.wait_ge(sh_done, k + 1)
                for t in range(CH):
                    if e == 0:
                        pe.wait_ge(p_done, 4 * k + t + 1)
                    o = ps[:, 4 + t, D * e:D * e + D] if e < E else ps[:, 3, D * t:D * t + D]
                    for fh in range(2):
                        a = slice(512 * fh + 128 * t, 512 * fh + 128 * t + 128)
                        pe.matmul(o, hh[:, e % 3, a], W2hv[:, fh, e], start=fh == 0, stop=False)
                        pe.matmul(o, hh[:, e % 3, a], W2lv[:, fh, e], start=False, stop=False)
                        mm = pe.matmul(o, hl[:, e % 3, a], W2hv[:, fh, e], start=False, stop=fh == 1)
                mm.then_inc(w2_done, 1)

            def experts(k, last=False):
                for e in range(E + 1):
                    if e + 2 <= E:
                        up(k, e + 2)
                    elif not last:
                        up(k + 1, e + 2 - (E + 1))
                    down(k, e)
            up(0, 0)
            up(0, 1)
            with pe.Fori(0, NC - 1) as k:
                experts(k)
            experts(NC - 1, True)

        @block.scalar
        def _(act):
            act.sem_inc(f2e_done, 2)
            act.sem_inc(y_done, 4)
            act.sem_inc(oe_done, 4)
            act.sem_inc(h_done, 4)
            for sm_, n in ((wv_done, 4), (at_done, 6), (ve_done, 2), (gelu_done, 3)):
                act.sem_inc(sm_, n)
            act.sem_inc(primed, 1)
            act.wait_ge(primed, 4)

            def first():
                act.wait_ge(xy_done, 1)
                act.activation(Gy, ps[:, 0, 0:384].rearrange("p (m r) -> p r m", r=2), ACT.Copy).then_inc(xye_done, 1)
                act.wait_ge(fold_done, 1)
                act.activation(wblk, ps[:, 2, 0:128], ACT.Copy).then_inc(folded, 1)
                act.wait_ge(xx_done, 1)
                act.activation(Gx.rearrange("p (a n) -> p a n", a=2),
                               ps[0:96, 1, 0:384].rearrange("p (a n) -> p a n", a=2)[:, :, 0:96], ACT.Copy).then_inc(xxe_done, 1)
                for c in range(9):
                    act.wait_ge(x0_done, c + 1)
                    act.activation(Xr[:, 512 * c:512 * c + 512], ps[:, 3 + c % 5, :], ACT.Copy).then_inc(x0e_done, 1)

            def phase_a(a):
                def relu(g, r):
                    ga = a * G + g
                    act.wait_ge(t1_done, ga * 8 + 2 * r + 2)
                    act.wait_ge(v_stored[r], 16 * ga + 16)
                    act.activation(R[:, r * 1024:(r + 1) * 1024], v[:, bass.ds(g * NPOS + r * 1024, 1024)], ACT.Relu,
                                   bias=shift, scale=scale).then_inc(relu_done, 1)

                def store(g, r):
                    act.wait_ge(relu_done, (a * G + g) * 4 + r + 1)
                    act.dma_start(v[:, bass.ds(g * NPOS + r * 1024, 1024)],
                                  R[:, r * 1024:(r + 1) * 1024]).then_inc(v_stored[r], 16)

                def group(g, s, now, before, after):
                    ga = a * G + g
                    gb, sb_ = ga - 1, 1 - s

                    def high(c):
                        act.wait_ge(t1_done, 8 + ga * 8 + c + 1)
                        act.wait_ge(f1_done, ga * 8 + c + 1)
                        act.activation(Sh[:, c % 2], ps[:, TP[c % 2], :], ACT.Copy).then_inc(sh_split, 1)

                    def high2(k):
                        act.wait_ge(t2_done, 2 + gb * 3 + k + 1)
                        act.wait_ge(f2_done, gb * 3 + k + 1)
                        act.activation(T2h[:, (sb_ * 3 + k) % 2], ps[:, T2P[(sb_ * 3 + k) % 2], :], ACT.Copy).then_inc(t2h_done, 1)

                    def modes(m):
                        act.wait_ge(f2_done, 2 + gb * 3 + 2 + m)
                        act.wait_ge(x_stored[sb_], 128 * (a * 8 + g - 1 - sb_) + 256)
                        act.activation(F2o[:, sb_, :, 6 * m:6 * m + 6].rearrange("p h k m -> p k h m"),
                                       ps[:, F2P[m], 0:288].rearrange("p (k h m) -> p k h m", k=6, h=4),
                                       ACT.Copy).then_inc(f2e_done, 1)

                    for c in range(8):
                        if now:
                            if c in (0, 2):
                                relu(g, 2 + c // 2)
                            if c in (4, 6) and after:
                                relu(g + 1, c // 2 - 2)
                            high(c)
                            if c in (0, 2):
                                store(g, 2 + c // 2)
                            if c in (4, 6) and after:
                                store(g + 1, c // 2 - 2)
                        if before:
                            if c < 3:
                                high2(c)
                            if c in (3, 4):
                                modes(c - 3)
                relu(0, 0)
                relu(0, 1)
                store(0, 0)
                store(0, 1)
                skewed(act, group)

            def mix(l):
                def negate(ky):
                    act.wait_ge(w_loaded[ky % 4], (l * 3 + ky // 4 + 1) * 16)
                    for h in range(2):
                        wi = W[64 * h + 32:64 * h + 64, ky % 4, :, 0:32]
                        act.activation(wi, wi, ACT.Copy, scale=-1.0).then_inc(w_neg, 1)
                negate(0)
                negate(1)
                for p in range(6):
                    if p < 5:
                        negate(2 * p + 2)
                        negate(2 * p + 3)
                    for h in range(2):
                        act.wait_ge(mix_done, 8 + (l * M + 2 * p + 1) * 2 + h + 1)
                        act.wait_ge(yt_done, l * 6 + p + 1)
                        act.activation(Ys[:, p % 2, :, 12 * h:12 * h + 12].rearrange("p o k -> p k o"),
                                       ps[:, (p % 2) * 2 + h, 0:384].rearrange("p (k o) -> p k o", o=C),
                                       ACT.Copy).then_inc(y_done, 1)

            def phase_b(l):
                act.wait_ge(lp_loaded, 16 * (l + 1))

                def zcopy(g, z):
                    gb = l * G + g
                    act.wait_ge(t4_done, 8 + gb * 4 + z + 1)
                    act.wait_ge(fin_done, (gb * 4 + z) * 2 + 2)
                    act.activation(Sh[:, z % 2], ps[:, ZP[z % 2], :], ACT.Copy).then_inc(zh_done, 1)

                def group(g, s, after):
                    for c in range(8):
                        act.wait_ge(fin_done, 4 + (l * G + g) * 8 + c + 1)
                        act.activation(v[:, bass.ds(g * NPOS + c * 512, 512)], ps[:, OP[c % 4], :], ACT.Identity,
                                       bias=wb).then_inc(oe_done, 1)
                        if c in (1, 3):
                            zcopy(g, 2 + c // 2)
                        if c >= 6 and after:
                            zcopy(g + 1, c - 6)
                zcopy(0, 0)
                zcopy(0, 1)
                leading(act, group)
                act.wait_ge(dch, l * STEPS + 5)
                act.activation(sd, var, ACT.Sqrt).then_inc(sq_done, 1)
                act.wait_ge(dch, (l + 1) * STEPS)
                act.wait_ge(oe_done, 4 + (l + 1) * 64)

            def step(l, last):
                mix(l)
                phase_b(l)
                if not last:
                    phase_a(l)
            layers(act, first, step)
            act.wait_ge(qb_done, 1)

            def tokens(g, s, i):
                for c in range(8):
                    act.wait_ge(h_mm, g * 8 + c + 1)
                    if c % 4 == 0:
                        act.wait_ge(h_stored[c // 4], 64 * g + 16)
                    act.activation(phase[0:4, 512 * c:512 * c + 512], ps[0:4, OP[c % 4], :], ACT.Identity,
                                   bias=sm[0:4, 17:18]).then_inc(h_done, 1)
            groups(act, tokens)

            def pairs(*stages):
                settle(act)
                with act.Fori(0, NJ // 2) as i:
                    for stage in stages:
                        for s in range(2):
                            stage(2 * i + s, s)

            def root(n, after):
                act.wait_ge(steps, after)
                act.activation(lns[:, 192:240], lns[:, 144:192], ACT.Sqrt).then_inc(sqrt_done, 1)

            root(1, STEP_E - 6)
            act.wait_ge(steps, STEP_E)

            def e_copy(j, s):
                act.wait_ge(tr_done, j + 1)
                settle(act)
                act.activation(es[:, s, :, 0], phase[:, bass.ds(j * 192, 192)].rearrange("p (t d) -> p t d", d=D),
                               ACT.Copy).then_inc(es_done, 1)

            def u_relu(j, s):
                for nh in range(2):
                    act.wait_ge(u_done, 4 + 2 * j + nh + 1)
                    settle(act)
                    act.activation(xa[:, nh, bass.ds(j * 384, 384)], ps[:, 2 + 2 * s + nh, 0:384],
                                   ACT.Relu, scale=1.0 / DS).then_inc(wv_done, 1)
            in_turns(act, NJ // 2, (e_copy, 0), (u_relu, 1))
            root(2, STEP_V - 6)
            act.wait_ge(steps, STEP_X)

            def x_copy(j, s):
                act.wait_ge(sc_done, j + 1)
                settle(act)
                act.activation(xs[:, s], xa[:, :, bass.ds(j * 384, 384)], ACT.Copy).then_inc(xs_done, 1)

            def a_copy(j, s):
                act.wait_ge(a_done, 2 + j + 1)
                o = bass.ds(j * 192, 64)
                settle(act)
                act.activation(phase[0:64, o], ps[0:64, 4 + 2 * s, 0:64], ACT.Copy).then_inc(at_done, 1)
                act.activation(phase[64:128, o], ps[64:128, 5 + 2 * s, 0:64], ACT.Copy).then_inc(at_done, 1)
                act.activation(phase[:, bass.ds(j * 192 + 64, 128)].rearrange("p (b d) -> p b d", b=2),
                               ps[:, 4 + 2 * s:6 + 2 * s, 64:128], ACT.Copy).then_inc(at_done, 1)
            in_turns(act, NJ // 2, (x_copy, 0), (a_copy, 1))
            root(3, STEP_A - 6)
            act.wait_ge(steps, STEP_A)

            def an_copy(j, s):
                act.wait_ge(tr2_done, j + 1)
                settle(act)
                act.activation(es[:, s, :, 0], phase[:, bass.ds(j * 192, 192)].rearrange("p (t d) -> p t d", d=D),
                               ACT.Copy).then_inc(as_done, 1)

            def v_copy(j, s):
                act.wait_ge(vo_done, 2 + j + 1)
                settle(act)
                act.activation(phase[:, bass.ds(3072 + j * 192, 192)], ps[:, 6 + s, 0:192], ACT.Copy,
                               scale=1.0 / (DS * ES)).then_inc(ve_done, 1)

            def y_high(j, s):
                act.wait_ge(ym_done, 4 + 2 * j + 2)
                act.wait_ge(vo_done, j + 1)
                settle(act)
                act.activation(ysh[:, s], ys[:, s], ACT.Copy).then_inc(yh_done, 1)
            in_turns(act, NJ // 2, (an_copy, 0), (v_copy, 3), (y_high, 2))
            root(4, STEP_VS - 6)
            root(5, STEP_H - 6)
            act.wait_ge(steps, STEP_H)

            def chunks(*stages):
                settle(act)
                with act.Fori(0, NT // CH // 2) as i:
                    for stage in stages:
                        for s in range(2):
                            stage(2 * i + s, s)

            def gelu(k, e):
                act.wait_ge(hl_done, k * 9 + e + 1)
                act.wait_ge(hlv_done, k * 9 + e + 1)
                for fh in range(2):
                    n = 2 * e + fh
                    act.wait_ge(hm_done, k * 18 + n + 1)
                    act.activation(hid[:, e % 3, 512 * fh:512 * fh + 512], ps[:, n % 3, :], ACT.Gelu,
                                   bias=B1[:, n:n + 1], scale=1.0 / WS).then_inc(gelu_done, 1)
            for e in range(E + 1):
                gelu(0, e)
                if e == 1:
                    act.wait_ge(steps, STEP_L)
                    act.activation(ex, lz, ACT.Exp).then_inc(exp_done, 1)
            settle(act)
            with act.Fori(1, NC) as k:
                for e in range(E + 1):
                    gelu(k, e)

        @block.vector
        def _(dve):
            dve.sem_inc(sl_split, 2)
            dve.sem_inc(t2l_done, 2)
            dve.sem_inc(zl_done, 2)
            dve.sem_inc(f1e_done, 2)
            dve.sem_inc(yt_done, 2)
            dve.sem_inc(i1e_done, 2)
            dve.sem_inc(bs_done, 4)
            for sm_, n in ((eT_done, 4), (ur_done, 2), (am_done, 4), (aT_done, 4), (ym_done, 4), (e2T_done, 2),
                           (lg_done, 2), (p_done, 4), (m_done, 4), (sh_done, 1), (hh_done, 3), (hlv_done, 3)):
                dve.sem_inc(sm_, n)
            dve.memset(ones, 1.0).then_inc(ones_done, 1)
            dve.sem_inc(primed, 1)
            dve.wait_ge(primed, 4)
            dve.memset(v[:, G * NPOS // 4:], 0.0).then_inc(v_zero, 1)
            dve.wait_ge(consts, 16 * NCONST)
            dve.wait_ge(zeroed, 2)

            def phase_a(a):
                def group(g, s, now, before, after):
                    ga = a * G + g
                    gb, sb_ = ga - 1, 1 - s

                    def low(c):
                        dve.wait_ge(sh_split, ga * 8 + c + 1)
                        dve.tensor_tensor(Sl[:, c % 2], ps[:, TP[c % 2], :], Sh[:, c % 2], ALU.subtract).then_inc(sl_split, 1)

                    def low2(k):
                        dve.wait_ge(t2h_done, gb * 3 + k + 1)
                        slot = (sb_ * 3 + k) % 2
                        dve.tensor_tensor(T2l[:, slot], ps[:, T2P[slot], :], T2h[:, slot], ALU.subtract).then_inc(t2l_done, 1)

                    def modes(m):
                        dve.wait_ge(f1_done, 2 + ga * 8 + 2 * m + 2)
                        dve.wait_ge(t2_done, 2 + ga * 3)
                        dve.tensor_copy(F1o[:, :, 16 * m:16 * m + 16],
                                        ps[:, FP[m % 2], 0:384].rearrange("p (x k) -> p k x", k=KR)).then_inc(f1e_done, 1)

                    for c in range(9):
                        if now and c in (3, 5, 7):
                            modes((c - 3) // 2)
                        if now and c < 8:
                            low(c)
                        if before and c < 3:
                            low2(c)
                    if now:
                        modes(3)
                skewed(dve, group)

            def mix(l):
                for s in range(2):
                    dve.wait_ge(x_stored[s], 256 * l * 4 + 256)
                for r in range(4):
                    dve.wait_ge(v_stored[r], 16 * G * l + 16)
                for p in range(6):
                    for par in range(2):
                        ky = 2 * p + par
                        dve.wait_ge(mix_done, (l * M + ky) * 2 + 6)
                        for h in range(2):
                            rows = slice(64 * h, 64 * h + 64)
                            dve.tensor_copy(XB[rows, par, :, 32 * h:32 * h + 32],
                                            X[rows, :, ky].rearrange("p b m -> p m b")).then_inc(xb_done, 1)
                    if p >= 1:
                        turn(l, p - 1)
                turn(l, 5)

            def turn(l, p):
                dve.wait_ge(y_done, 4 + (l * 6 + p) * 2 + 2)
                dve.transpose(H[:, p].rearrange("p o b -> p (o b)"), Ys[:, p % 2].rearrange("p o k -> p (o k)")).then_inc(yt_done, 1)

            def phase_b(l):
                def z_low(g, z):
                    dve.wait_ge(zh_done, (l * G + g) * 4 + z + 1)
                    dve.tensor_tensor(Sl[:, z % 2], ps[:, ZP[z % 2], :], Sh[:, z % 2], ALU.subtract).then_inc(zl_done, 1)

                def x_inverse(g, s, u):
                    gb = l * G + g
                    if u == 0:
                        dve.wait_ge(t4_done, gb * 4 + 4)
                    dve.wait_ge(i1_done, 6 + gb * 3 + u + 1)
                    dve.tensor_copy(I1o[:, s, :, 8 * u:8 * u + 8].rearrange("p x k -> p k x"),
                                    ps[:, IP[(s * 3 + u) % 2], :].rearrange("p (k x) -> p k x", x=SX)).then_inc(i1e_done, 1)

                def group(g, s, after):
                    for c in range(8):
                        dve.wait_ge(oe_done, 4 + (l * G + g) * 8 + c + 1)
                        settle(dve)
                        dve.bn_stats(st[:, bass.ds((g * 8 + c) * 6, 6)],
                                     v[:, bass.ds(g * NPOS + c * 512, 512)]).then_inc(bs_done, 1)
                        if c in (1, 3):
                            z_low(g, 2 + c // 2)
                        if after and 3 <= c < 6:
                            x_inverse(g + 1, 1 - s, c - 3)
                        if after and c >= 6:
                            z_low(g + 1, c - 6)
                for u in range(3):
                    x_inverse(0, 0, u)
                z_low(0, 0)
                z_low(0, 1)
                leading(dve, group)

                def link(n, ins):
                    ins.then_inc(dch, 1)
                    dve.wait_ge(dch, l * STEPS + n)
                dve.wait_ge(bs_done, 4 + (l + 1) * 64)
                settle(dve)
                link(1, dve.bn_aggr(agg, st[:, :]))
                dve.wait_ge(sm_done, 2 * l + 1)
                link(2, dve.tensor_copy(mv, ps[:, 0, 0:2]))
                link(3, dve.tensor_tensor(dif, agg[:, 0:1], mv[:, 0:1], ALU.subtract))
                link(4, dve.tensor_tensor(sq, dif, dif, ALU.mult))
                dve.wait_ge(sm_done, 2 * l + 2)
                link(5, dve.tensor_scalar(var, ps[:, 1, 0:1], mv[:, 1:2], EPS, ALU.add, ALU.add))
                dve.wait_ge(sq_done, l + 1)
                link(6, dve.reciprocal(r0, sd))
                link(7, dve.tensor_tensor(r2, r0, r0, ALU.mult))
                link(8, dve.tensor_scalar(t1, r2, var, -0.5, ALU.mult, ALU.mult))
                link(9, dve.tensor_scalar(rs, t1, 1.5, r0, ALU.add, ALU.mult))
                link(10, dve.tensor_tensor(scale, rs, gamma, ALU.mult))
                link(11, dve.tensor_copy(mw, mv[:, 0:1]))
                link(12, dve.tensor_tensor(ms, mw, scale, ALU.mult))
                link(13, dve.tensor_tensor(shift, beta, ms, ALU.subtract))

            def step(l, last):
                mix(l)
                phase_b(l)
                if not last:
                    phase_a(l)
            layers(dve, lambda: dve.wait_ge(x0e_done, 9), step)
            dve.tensor_scalar(qs[:, 4:8], qs[:, 0:4], scale, None, ALU.mult).then_inc(qs_done, 1)
            dve.wait_ge(qt_done, 1)
            dve.tensor_tensor(sm[0:4, 17:18], ps[0:4, 0, 0:1], qbias[0:4, :], ALU.add).then_inc(qb_done, 1)


            def pairs(*stages):
                settle(dve)
                with dve.Fori(0, NJ // 2) as i:
                    for stage in stages:
                        for s in range(2):
                            stage(2 * i + s, s)

            done = [0]

            def do(ins):
                done[0] += 1
                ins.then_inc(steps, 1)
                dve.wait_ge(steps, done[0])

            def norm(dst, src, scratch, eps, nth):
                wide = lambda a: a.unsqueeze(2).broadcast_to([128, NT, D])
                tot, mean, vs, ve, sdv, rv, rv2, nt, rst = (lns[:, 48 * i:48 * i + 48] for i in range(9))
                do(dve.tensor_reduce(tot, src, AX.X, ALU.add))
                do(dve.tensor_scalar(mean, tot, 1.0 / D, None, ALU.mult))
                do(dve.tensor_tensor(dst, src, wide(mean), ALU.subtract))
                do(dve.tensor_tensor(scratch, dst, dst, ALU.mult))
                do(dve.tensor_reduce(vs, scratch, AX.X, ALU.add))
                do(dve.tensor_scalar(ve, vs, 1.0 / D, eps, ALU.mult, ALU.add))
                dve.wait_ge(sqrt_done, nth)
                do(dve.reciprocal(rv, sdv))
                do(dve.tensor_tensor(rv2, rv, rv, ALU.mult))
                do(dve.tensor_tensor(nt, rv2, ve, ALU.mult))
                do(dve.tensor_scalar(rst, nt, -0.5, 1.5, ALU.mult, ALU.add))
                do(dve.tensor_tensor(rst, rst, rv, ALU.mult))
                do(dve.tensor_tensor(dst, dst, wide(rst), ALU.mult))

            dve.wait_ge(txt_in, 32)
            for s in range(2):
                dve.wait_ge(h_stored[s], 16 * (1 + 4 * G))
            norm(eb, h_all, tmp, EPS, 1)
            assert done[0] == STEP_E

            def by_batch(k, s, done_sem):
                src, dst = ps[:, s, 0:192].bitcast(F16), eTs[:, s].rearrange("p (b t) -> p b t", b=2)
                dve.tensor_copy(dst[:, :, 0:SX], src[:, 0:128].rearrange("p (b t) -> p b t", b=2)).then_inc(done_sem, 1)
                dve.tensor_copy(dst[:, :, SX:T], src[:, 128:384].rearrange("p (b t) -> p b t", b=2)).then_inc(done_sem, 1)

            def e_turned(j, s):
                dve.wait_ge(tr_done, 2 + j + 1)
                dve.wait_ge(u_done, 2 * j + 2)
                by_batch(j, s, eT_done)

            def u_total(j, s):
                dve.wait_ge(us_done, j + 1)
                dve.tensor_copy(u_row[:, bass.ds(j * 384, 384)], ps[0:1, 6 + s, 0:384]).then_inc(ur_done, 1)
            pairs(e_turned, u_total)

            dve.wait_ge(u_moved, 16)
            big = DECAY / TINY
            do(dve.tensor_scalar(k1, U, TINY, -big, ALU.is_ge, ALU.mult))
            do(dve.tensor_scalar(k2, k1, big, 1.0, ALU.add, ALU.max))
            do(dve.tensor_tensor_scan(z, k2, U, 0.0, ALU.mult, ALU.add))
            do(dve.tensor_scalar(k1[:, 1:T], z[:, 0:T - 1], big, DECAY, ALU.mult, ALU.min))
            do(dve.memset(k1[:, 0:1], 0.0))
            do(dve.tensor_tensor(k2, k1, U, ALU.add))
            do(dve.tensor_scalar(k1, k2, TINY, None, ALU.max))
            do(dve.reciprocal(rsum, k1))
            do(dve.memset(csum[:, 0:1], 0.0))
            do(dve.tensor_scalar(csum[:, 1:T], rsum[:, 0:T - 1], DECAY, None, ALU.mult))
            assert done[0] == STEP_RC
            norm(vb, eb, tmp, EPS, 2)
            assert done[0] == STEP_V
            dve.wait_ge(c_in, 16)
            for nh in range(2):
                do(dve.tensor_tensor_scan(xa[:, nh], cB, xa[:, nh], 0.0, ALU.mult, ALU.add))
            dve.wait_ge(r_in, 16)
            for nh in range(2):
                do(dve.tensor_tensor(xa[:, nh], xa[:, nh], rB, ALU.mult))
            assert done[0] == STEP_X

            def decay(j, s):
                dve.wait_ge(sc_done, 2 + j + 1)
                dve.wait_ge(a_done, j + 1)
                dve.tensor_tensor(Ai[:, s], ps[:, s, 0:T], Di, ALU.mult).then_inc(am_done, 1)
                dve.tensor_tensor(At[:, s].rearrange("p (b t) -> p b t", b=2),
                                  ps[:, 2 + s, 0:256].rearrange("p (b t) -> p b t", b=2),
                                  Dt.unsqueeze(1).broadcast_to([128, 2, TXT]), ALU.mult).then_inc(am_done, 1)
            pairs(decay)
            dve.wait_ge(at_done, 6 + 3 * NJ)
            norm(eb, eb, tmp2, EPS, 3)
            assert done[0] == STEP_A

            def a_turned(j, s):
                dve.wait_ge(tr2_done, 2 + j + 1)
                dve.wait_ge(yc_done, 2 * j + 2)
                by_batch(j, s, aT_done)

            def gate(j, s):
                dve.wait_ge(yl_done, j + 1)
                for nh in range(2):
                    dve.wait_ge(yc_done, 4 + 2 * j + nh + 1)
                    dve.scalar_tensor_tensor(ys[:, s, nh], ps[:, 2 + 2 * s + nh, 0:384], 0.0,
                                             xa[:, nh, bass.ds(j * 384, 384)], ALU.max, ALU.mult).then_inc(ym_done, 1)
            in_turns(dve, NJ // 2, (gate, 2), (a_turned, 1))
            dve.wait_ge(ve_done, 2 + NJ)
            norm(vb, vb, tmp2, EPS, 4)
            do(dve.tensor_tensor(h_all, h_all, vb, ALU.add))
            norm(eb, h_all, tmp2, EPS, 5)
            assert done[0] == STEP_H

            def chunks(*stages):
                settle(dve)
                with dve.Fori(0, NT // CH // 2) as i:
                    for stage in stages:
                        for s in range(2):
                            stage(2 * i + s, s)

            do(dve.tensor_copy(ehl[:, :, 0], eb))
            do(dve.tensor_tensor(ehl[:, :, 1], eb, ehl[:, :, 0], ALU.subtract))
            assert done[0] == STEP_S

            def h_turned(k, s):
                dve.wait_ge(tr3_done, 2 + k + 1)
                settle(dve)
                dve.tensor_copy(v[:, bass.ds(k * 256, 256)].bitcast(F16), ps[:, s, 0:256].bitcast(F16)).then_inc(e2T_done, 1)

            def logits(k, s):
                dve.wait_ge(rt_done, 2 + k + 1)
                settle(dve)
                dve.tensor_scalar(cB[:, bass.ds(2048 + k * CH * E, CH * E)], ps[:, 2 + s, 0:CH * E], 1.0 / RS, None,
                                  ALU.mult).then_inc(lg_done, 1)
            in_turns(dve, NC // 2, (h_turned, 0), (logits, 1))
            dve.wait_ge(lg_done, 2 + NC)
            settle(dve)

            wide = lambda a: a.unsqueeze(2).broadcast_to([128, NT, E])
            ranks = rank.unsqueeze(1).broadcast_to([128, NT, E])
            top, tot, inv, m1, c1, m2, c2, den, dinv = (rr[:, i] for i in range(9))
            def high(k, e):
                dve.wait_ge(gelu_done, 3 + k * 18 + 2 * e + 2)
                dve.wait_ge(w2_done, k * 9 + e + 1)
                settle(dve)
                dve.tensor_copy(hh[:, e % 3], hid[:, e % 3]).then_inc(hh_done, 1)
                dve.wait_ge(hh_done, 3 + k * 9 + e + 1)
                dve.tensor_tensor(hl[:, e % 3, LP:], hid[:, e % 3, LP:], hh[:, e % 3, LP:], ALU.subtract).then_inc(hlv_done, 1)

            def biased(k, t):
                dve.wait_ge(w2_done, 3 + 9 * k + E)
                dve.wait_ge(m_done, 4 * k + t + 1)
                dve.scalar_tensor_tensor(tb[:, t].rearrange("p e d -> p (e d)"), ps[:, 4 + t, :], 1.0 / WS, B2[:, 0:E * D],
                                         ALU.mult, ALU.add).then_inc(p_done, 1)

            def weighted(k, t):
                dve.wait_ge(p_done, 4 + 4 * k + t + 1)
                mk = cB[:, bass.ds(2048 + 9 * 384 + (k * CH + t) * E, E)].unsqueeze(2).broadcast_to([128, E, D])
                dve.tensor_tensor(tb[:, t], tb[:, t], mk, ALU.mult).then_inc(m_done, 1)
                dve.wait_ge(m_done, 4 + 4 * k + t + 1)
                dve.tensor_reduce(rt[:, t], tb[:, t].rearrange("p e d -> p d e"), AX.X, ALU.add).then_inc(r_done, 1)

            def shared(k):
                dve.wait_ge(w2_done, 3 + 9 * k + 9)
                dve.scalar_tensor_tensor(s1, ps[:, 3, 0:256].rearrange("p (t d) -> p t d", d=D), 1.0 / WS,
                                         B2[:, E * D:].unsqueeze(1).broadcast_to([128, CH, D]),
                                         ALU.mult, ALU.add).then_inc(sh_done, 1)

            def total(k):
                dve.wait_ge(r_done, 4 * k + 4)
                dve.wait_ge(sh_done, 1 + k + 1)
                dve.tensor_tensor(s2, s1, rt, ALU.add).then_inc(s2_done, 1)
                dve.wait_ge(s2_done, k + 1)
                hk = Xr[:, bass.ds(k * 256, 256)].rearrange("p (t d) -> p t d", d=D)
                dve.tensor_tensor(hk, hk, s2, ALU.add).then_inc(f_done, 1)

            def combine(k, piece):
                if piece == 0:
                    for t in range(CH):
                        biased(k, t)
                elif piece <= CH:
                    weighted(k, piece - 1)
                elif piece == CH + 1:
                    shared(k)
                elif piece == CH + 2:
                    total(k)

            def mask_part(part):
                if part == 0:
                    do(dve.tensor_reduce(top, lg, AX.X, ALU.max))
                    do(dve.tensor_tensor(lz, lg, wide(top), ALU.subtract))
                    assert done[0] == STEP_L
                elif part == 1:
                    dve.wait_ge(exp_done, 1)
                    do(dve.tensor_reduce(tot, ex, AX.X, ALU.add))
                    do(dve.reciprocal(inv, tot))
                    do(dve.tensor_tensor(rw, ex, wide(inv), ALU.mult))
                elif part == 2:
                    do(dve.tensor_reduce(m1, rw, AX.X, ALU.max))
                    do(dve.tensor_tensor(eq, rw, wide(m1), ALU.is_equal))
                    do(dve.tensor_tensor(cd, eq, ranks, ALU.mult))
                elif part == 3:
                    do(dve.tensor_reduce(c1, cd, AX.X, ALU.max))
                    do(dve.tensor_tensor(oh1, wide(c1), ranks, ALU.is_equal))
                    do(dve.scalar_tensor_tensor(rw2, oh1, -4.0, rw, ALU.mult, ALU.add))
                elif part == 4:
                    do(dve.tensor_reduce(m2, rw2, AX.X, ALU.max))
                    do(dve.tensor_tensor(eq, rw2, wide(m2), ALU.is_equal))
                    do(dve.tensor_tensor(cd, eq, ranks, ALU.mult))
                elif part == 5:
                    do(dve.tensor_reduce(c2, cd, AX.X, ALU.max))
                    do(dve.tensor_tensor(oh2, wide(c2), ranks, ALU.is_equal))
                    do(dve.tensor_tensor(den, m1, m2, ALU.add))
                elif part == 6:
                    do(dve.reciprocal(dinv, den))
                    do(dve.tensor_tensor(oh1, oh1, oh2, ALU.add))
                elif part == 7:
                    do(dve.tensor_tensor(oh1, oh1, rw, ALU.mult))
                    do(dve.tensor_tensor(mask, oh1, wide(dinv), ALU.mult))
                    assert done[0] == STEP_M

            for e in range(E + 1):
                high(0, e)
                mask_part(e)
            settle(dve)
            with dve.Fori(1, NC) as k:
                for e in range(E + 1):
                    high(k, e)
                    combine(k - 1, e)
            for piece in range(E + 1):
                combine(NC - 1, piece)


def kernel(**inputs):
    import numpy as np
    import concourse.bacc as bacc
    from concourse.bass_utils import run_bass_kernel_spmd

    f = {k: np.ascontiguousarray(a) for k, a in inputs.items()}
    arrays = {}
    arrays["x"] = f["x"].reshape(B, NPOS)
    gx = np.linspace(0.0, 1.0, SX, dtype=np.float32)
    grid = np.stack([np.repeat(gx, SY), np.tile(gx, SX), np.ones(NPOS, np.float32)])
    arrays["grid"] = np.ascontiguousarray(np.broadcast_to(grid[:, None], (3, G, NPOS)))
    pin = np.zeros((Q + 3, Q, C), np.float32)
    for q in range(Q):
        pin[q, q] = f["L0_tok_p_w"][0]
        pin[Q, q] = f["L0_tok_p_w"][1]
        pin[Q + 1, q] = f["L0_tok_p_w"][2]
        pin[Q + 2, q] = f["L0_tok_p_b"]
    pint = np.zeros((128, 128), np.float32)
    pint[:, 0:Q + 3] = pin.reshape(Q + 3, 128).T
    arrays["pint"] = pint
    pblk = np.zeros((4, 4, 4, C), np.float32)
    for part in range(4):
        pblk[:, part, part] = np.concatenate([f["L0_tok_p_w"], f["L0_tok_p_b"][None]])
    arrays["pblk"] = pblk.reshape(16, 128)
    arrays["xt"] = f["x"].reshape(2, NJ, SX, SY).transpose(3, 1, 0, 2).reshape(SY, NJ * 128)
    arrays["txt"] = f["txt"]
    avg = np.kron(np.full((Q, Q), 1.0 / Q), np.eye(C)).astype(np.float32)
    names = []
    for n, a in enumerate([*spectral_tables(), np.eye(128, dtype=np.float32), avg]):
        arrays[f"table{n}"] = a
        names.append(f"table{n}")
    fw = np.stack([f["L0_tok_fw1"], f["L0_tok_fw2"]])
    a = fw.transpose(5, 0, 2, 1, 4, 6, 3)
    a = np.stack([a, a[..., ::-1, :]], axis=2)
    arrays["fw"] = np.ascontiguousarray(a.reshape(M, 128, L, M, 64))
    lp = np.zeros((L, 128, 131), np.float32)
    for q in range(Q):
        s = slice(q * C, (q + 1) * C)
        lp[:, s, s] = f["L0_tok_w_w"]
        lp[:, s, 128], lp[:, s, 129], lp[:, s, 130] = f["L0_tok_w_b"], f["L0_tok_bn_g"], f["L0_tok_bn_b"]
    arrays["lp"] = lp
    qblk = np.zeros((128, 4), np.float32)
    for q in range(Q):
        qblk[q * C:(q + 1) * C, q] = f["L0_tok_q_w"][:, 0]
    arrays["qblk"] = qblk
    arrays["qb"] = np.ascontiguousarray(np.broadcast_to(f["L0_tok_q_b"].reshape(1, 1), (4, 1)))

    arrays["att"] = attention_tables()
    arrays["dxy"] = np.concatenate([f["L0_attn_Dx"].T, f["L0_attn_Dy"].T], axis=1)
    arrays["et"] = f["L0_attn_E"].T.reshape(2, 128, D).transpose(1, 0, 2)
    w1 = np.concatenate([f["L0_ffn_W1p"], f["L0_ffn_W1s"][None]])
    w2 = np.concatenate([f["L0_ffn_W2p"], f["L0_ffn_W2s"][None]])
    b1 = np.concatenate([f["L0_ffn_b1p"], f["L0_ffn_b1s"][None]])
    b2 = np.concatenate([f["L0_ffn_b2p"], f["L0_ffn_b2s"][None]])
    arrays["w1"] = w1.transpose(1, 0, 2)
    arrays["w2"] = w2.reshape(E + 1, 2, 128, D).transpose(2, 1, 0, 3)
    arrays["wr"] = f["L0_ffn_Wr"]
    arrays["b1"] = b1.reshape(2 * (E + 1), 128).T
    arrays["b2"] = np.broadcast_to(b2.reshape(1, -1), (128, (E + 1) * D))

    nc = bacc.Bacc("TRN2", target_bir_lowering=False, num_devices=1)
    arrays = {f"in_{k}": np.ascontiguousarray(a) for k, a in arrays.items()}
    ap = {k: nc.dram_tensor(k, a.shape, mybir.dt.from_np(a.dtype), kind="ExternalInput").ap() for k, a in arrays.items()}
    out = nc.dram_tensor("out_0", (B, T, D), F32, kind="ExternalOutput").ap()
    build(nc, ap["in_x"], ap["in_grid"], ap["in_xt"], ap["in_pint"], ap["in_pblk"], ap["in_txt"], [ap[f"in_{n}"] for n in names], ap["in_fw"],
          ap["in_lp"], ap["in_qblk"], ap["in_qb"], ap["in_att"], ap["in_dxy"], ap["in_et"], ap["in_w1"], ap["in_w2"],
          ap["in_wr"], ap["in_b1"], ap["in_b2"], nc.dram_tensor("norms", (2, NW), F32, kind="Internal").ap(), out)
    r = run_bass_kernel_spmd(nc, [arrays], core_ids=[0])
    return r.results[0]["out_0"]
```
